# Optimizing a Trainium2 kernel written in Bass

```python
import numpy as np
import jax
import jax.numpy as jnp

def _softmax(x, axis=-1):
    return jax.nn.softmax(x, axis=axis)

def _gelu(x):
    return jax.nn.gelu(x, approximate=True)

def _silu(x):
    return jax.nn.silu(x)

def _sigmoid(x):
    return jax.nn.sigmoid(x)

def _layernorm(x, axis=-1, eps=1e-05):
    m = jnp.mean(x, axis=axis, keepdims=True)
    v = jnp.var(x, axis=axis, keepdims=True)
    return (x - m) / jnp.sqrt(v + eps)

def _scatter_add(tgt, idx, src, axis=0):
    return tgt.at[idx].add(src)

def _segment_sum(src, seg, n):
    return jax.ops.segment_sum(src, seg, n)
kernel_name = 'mk_seq_postln_d2_jaxref_r4_56f7de'

def setup_inputs(seed: int=0):
    np.random.seed(seed)
    _w = jnp.asarray

    def _L0_attn_setup():
        import jax, jax.numpy as jnp
        import numpy as np
        N_HEAD = 16
        PAGE_SIZE = 64
        ROPE_THETA = 10000.0

        def _rope_tables(T, D, dtype):
            inv = 1.0 / ROPE_THETA ** (np.arange(0, D, 2, dtype=np.float32) / D)
            ang = np.outer(np.arange(T, dtype=np.float32), inv)
            return (jnp.asarray(np.cos(ang), dtype), jnp.asarray(np.sin(ang), dtype))

        def _apply_rope(x, cos, sin):
            x1 = x[..., 0::2]
            x2 = x[..., 1::2]
            c = cos[None, :, None, :]
            s = sin[None, :, None, :]
            out = jnp.stack([x1 * c - x2 * s, x1 * s + x2 * c], axis=-1)
            return out.reshape(x.shape)
        key = jax.random.key(seed)
        ks = jax.random.split(key, 6)
        B, T, E = (2, 512, 256)
        L = E // 2
        sc = lambda fan: 1.0 / np.sqrt(fan)
        return {'x': jax.random.normal(ks[0], (B, T, E), jnp.float32), 'wq': jax.random.normal(ks[1], (E, E), jnp.float32) * sc(E), 'w_down': jax.random.normal(ks[2], (E, L), jnp.float32) * sc(E), 'wk_up': jax.random.normal(ks[3], (L, E), jnp.float32) * sc(L), 'wv_up': jax.random.normal(ks[4], (L, E), jnp.float32) * sc(L), 'wo': jax.random.normal(ks[5], (E, E), jnp.float32) * sc(E)}
    _L0_attn_in = _L0_attn_setup()

    def _L0_ffn_setup():
        import jax, jax.numpy as jnp
        import numpy as np
        CAPACITY_FACTOR = 0.5
        key = jax.random.key(seed)
        ks = jax.random.split(key, 5)
        B, S, D, F = (4, 1024, 256, 1024)
        scale_in = 1.0 / np.sqrt(D)
        scale_ff = 1.0 / np.sqrt(F)
        return {'hidden_states': jax.random.normal(ks[0], (B, S, D), dtype=jnp.float32), 'w_router': jax.random.normal(ks[1], (D,), dtype=jnp.float32) * scale_in, 'W1': jax.random.normal(ks[2], (D, F), dtype=jnp.float32) * scale_in, 'b1': jnp.zeros((F,), dtype=jnp.float32), 'W2': jax.random.normal(ks[3], (F, D), dtype=jnp.float32) * scale_ff, 'b2': jnp.zeros((D,), dtype=jnp.float32)}
    _L0_ffn_in = _L0_ffn_setup()

    def _L1_attn_setup():
        import jax, jax.numpy as jnp
        import numpy as np
        _J6 = jnp.array([[0, 0, 0, 0, 0, 1], [0, 0, 0, 0, -1, 0], [0, 0, 0, 1, 0, 0], [0, 0, 1, 0, 0, 0], [0, -1, 0, 0, 0, 0], [1, 0, 0, 0, 0, 0]], dtype=jnp.float32)
        _PI = np.array([0, 0, 0, 1, 1, 2])
        _PJ = np.array([1, 2, 3, 2, 3, 3])

        def plucker_lines(p1, p2):
            lines = p1[..., _PI] * p2[..., _PJ] - p1[..., _PJ] * p2[..., _PI]
            n = jnp.linalg.norm(lines, axis=-1, keepdims=True)
            return lines / jnp.maximum(n, 1e-12)
        key = jax.random.key(seed)
        ks = jax.random.split(key, 6)
        B, T, D, H = (1, 512, 256, 16)
        s = D ** (-0.5)
        x = jax.random.normal(ks[0], (B, T, D), jnp.float32)
        Wqkv = jax.random.normal(ks[1], (D, 3 * D), jnp.float32) * s
        bqkv = jnp.zeros((3 * D,), jnp.float32)
        W1p = jax.random.normal(ks[2], (D, 4 * H), jnp.float32) * s
        W2p = jax.random.normal(ks[3], (D, 4 * H), jnp.float32) * s
        plucker_scale = jnp.full((H,), 0.1, jnp.float32)
        Wout = jax.random.normal(ks[4], (D, D), jnp.float32) * s
        bout = jnp.zeros((D,), jnp.float32)
        return {'x': x, 'Wqkv': Wqkv, 'bqkv': bqkv, 'W1p': W1p, 'W2p': W2p, 'plucker_scale': plucker_scale, 'Wout': Wout, 'bout': bout}
    _L1_attn_in = _L1_attn_setup()

    def _L1_ffn_setup():
        import jax, jax.numpy as jnp
        import numpy as np
        E, D, F = (8, 256, 1024)
        B, S = (4, 512)

        def _layernorm(x, g, b, eps=1e-05):
            mu = jnp.mean(x, axis=-1, keepdims=True)
            var = jnp.var(x, axis=-1, keepdims=True)
            return (x - mu) * jax.lax.rsqrt(var + eps) * g + b
        key = jax.random.key(seed)
        ks = jax.random.split(key, 5)
        return {'input_features': jax.random.normal(ks[0], (B, S, D), jnp.float32), 'centroids': jax.random.normal(ks[1], (E, D), jnp.float32) * 0.1, 'ln_g': jnp.ones((E, D), jnp.float32), 'ln_b': jnp.zeros((E, D), jnp.float32), 'w1': jax.random.normal(ks[2], (E, F, D), jnp.float32) * (1.0 / np.sqrt(D).astype(np.float32)), 'b1': jnp.zeros((E, F), jnp.float32), 'w2': jax.random.normal(ks[3], (E, D, F), jnp.float32) * (1.0 / np.sqrt(F).astype(np.float32)), 'b2': jnp.zeros((E, D), jnp.float32)}
    _L1_ffn_in = _L1_ffn_setup()
    _d = {'L0_attn_x': _L0_attn_in['x'], 'L0_attn_wq': _L0_attn_in['wq'], 'L0_attn_w_down': _L0_attn_in['w_down'], 'L0_attn_wk_up': _L0_attn_in['wk_up'], 'L0_attn_wv_up': _L0_attn_in['wv_up'], 'L0_attn_wo': _L0_attn_in['wo'], 'L0_ffn_w_router': _L0_ffn_in['w_router'], 'L0_ffn_W1': _L0_ffn_in['W1'], 'L0_ffn_b1': _L0_ffn_in['b1'], 'L0_ffn_W2': _L0_ffn_in['W2'], 'L0_ffn_b2': _L0_ffn_in['b2'], 'L1_attn_Wqkv': _L1_attn_in['Wqkv'], 'L1_attn_bqkv': _L1_attn_in['bqkv'], 'L1_attn_W1p': _L1_attn_in['W1p'], 'L1_attn_W2p': _L1_attn_in['W2p'], 'L1_attn_plucker_scale': _L1_attn_in['plucker_scale'], 'L1_attn_Wout': _L1_attn_in['Wout'], 'L1_attn_bout': _L1_attn_in['bout'], 'L1_ffn_centroids': _L1_ffn_in['centroids'], 'L1_ffn_ln_g': _L1_ffn_in['ln_g'], 'L1_ffn_ln_b': _L1_ffn_in['ln_b'], 'L1_ffn_w1': _L1_ffn_in['w1'], 'L1_ffn_b1': _L1_ffn_in['b1'], 'L1_ffn_w2': _L1_ffn_in['w2'], 'L1_ffn_b2': _L1_ffn_in['b2']}
    _x0 = _d['L0_attn_x']
    _d['L0_attn_x'] = jax.random.normal(jax.random.fold_in(jax.random.key(seed), 1), (4, 1024, 256), dtype=_x0.dtype)
    del _x0
    return _d

def reference(L0_attn_x, L0_attn_wq, L0_attn_w_down, L0_attn_wk_up, L0_attn_wv_up, L0_attn_wo, L0_ffn_w_router, L0_ffn_W1, L0_ffn_b1, L0_ffn_W2, L0_ffn_b2, L1_attn_Wqkv, L1_attn_bqkv, L1_attn_W1p, L1_attn_W2p, L1_attn_plucker_scale, L1_attn_Wout, L1_attn_bout, L1_ffn_centroids, L1_ffn_ln_g, L1_ffn_ln_b, L1_ffn_w1, L1_ffn_b1, L1_ffn_w2, L1_ffn_b2):

    def _L0_attn_ref(x, wq, w_down, wk_up, wv_up, wo):
        import jax, jax.numpy as jnp
        import numpy as np
        N_HEAD = 16
        PAGE_SIZE = 64
        ROPE_THETA = 10000.0

        def _rope_tables(T, D, dtype):
            inv = 1.0 / ROPE_THETA ** (np.arange(0, D, 2, dtype=np.float32) / D)
            ang = np.outer(np.arange(T, dtype=np.float32), inv)
            return (jnp.asarray(np.cos(ang), dtype), jnp.asarray(np.sin(ang), dtype))

        def _apply_rope(x, cos, sin):
            x1 = x[..., 0::2]
            x2 = x[..., 1::2]
            c = cos[None, :, None, :]
            s = sin[None, :, None, :]
            out = jnp.stack([x1 * c - x2 * s, x1 * s + x2 * c], axis=-1)
            return out.reshape(x.shape)
        B, T, E = x.shape
        H = N_HEAD
        D = E // H
        q = (x @ wq).reshape(B, T, H, D)
        lat = x @ w_down
        k = (lat @ wk_up).reshape(B, T, H, D)
        v = (lat @ wv_up).reshape(B, T, H, D)
        cos, sin = _rope_tables(T, D, x.dtype)
        q = _apply_rope(q, cos, sin)
        k = _apply_rope(k, cos, sin)
        scale = 1.0 / jnp.sqrt(jnp.asarray(D, x.dtype))
        scores = jnp.einsum('bqhd,bkhd->bhqk', q, k) * scale
        pages = jnp.arange(T) // PAGE_SIZE
        allowed = pages[None, :] <= pages[:, None]
        scores = jnp.where(allowed[None, None], scores, jnp.finfo(scores.dtype).min)
        attn = jax.nn.softmax(scores, axis=-1)
        out = jnp.einsum('bhqk,bkhd->bqhd', attn, v).reshape(B, T, E)
        return out @ wo

    def _L0_ffn_ref(hidden_states, w_router, W1, b1, W2, b2):
        import jax, jax.numpy as jnp
        import numpy as np
        CAPACITY_FACTOR = 0.5
        'Mixture-of-Depths block: route top-k tokens through an FFN inner block,\n            scatter back with sigmoid router weights; bypassed tokens pass through.'
        B, S, D = hidden_states.shape
        k = int(S * CAPACITY_FACTOR)
        scores = jnp.einsum('bsd,d->bs', hidden_states, w_router)
        top_scores, top_idx = jax.lax.top_k(scores, k)
        weights = jax.nn.sigmoid(top_scores)
        selected = jnp.take_along_axis(hidden_states, top_idx[:, :, None], axis=1)
        h = jax.nn.gelu(jnp.einsum('bkd,df->bkf', selected, W1) + b1)
        processed = jnp.einsum('bkf,fd->bkd', h, W2) + b2
        update = weights[:, :, None] * processed

        def scatter_one(xb, ib, ub):
            return xb.at[ib].add(ub)
        output = jax.vmap(scatter_one)(hidden_states, top_idx, update)
        return output

    def _L1_attn_ref(x, Wqkv, bqkv, W1p, W2p, plucker_scale, Wout, bout):
        import jax, jax.numpy as jnp
        import numpy as np
        _J6 = jnp.array([[0, 0, 0, 0, 0, 1], [0, 0, 0, 0, -1, 0], [0, 0, 0, 1, 0, 0], [0, 0, 1, 0, 0, 0], [0, -1, 0, 0, 0, 0], [1, 0, 0, 0, 0, 0]], dtype=jnp.float32)
        _PI = np.array([0, 0, 0, 1, 1, 2])
        _PJ = np.array([1, 2, 3, 2, 3, 3])

        def plucker_lines(p1, p2):
            lines = p1[..., _PI] * p2[..., _PJ] - p1[..., _PJ] * p2[..., _PI]
            n = jnp.linalg.norm(lines, axis=-1, keepdims=True)
            return lines / jnp.maximum(n, 1e-12)
        B, T, D = x.shape
        H = plucker_scale.shape[0]
        dh = D // H
        qkv = (x @ Wqkv + bqkv).reshape(B, T, 3, H, dh)
        q = jnp.transpose(qkv[:, :, 0], (0, 2, 1, 3))
        k = jnp.transpose(qkv[:, :, 1], (0, 2, 1, 3))
        v = jnp.transpose(qkv[:, :, 2], (0, 2, 1, 3))
        std_logits = jnp.einsum('bhid,bhjd->bhij', q, k) * dh ** (-0.5)
        p1 = (x @ W1p).reshape(B, T, H, 4)
        p2 = (x @ W2p).reshape(B, T, H, 4)
        lines_h = jnp.transpose(plucker_lines(p1, p2), (0, 2, 1, 3))
        Jlines = lines_h @ _J6.T
        plucker_bias = jnp.einsum('bhic,bhjc->bhij', lines_h, Jlines)
        logits = std_logits + plucker_bias * plucker_scale[None, :, None, None]
        causal = jnp.triu(jnp.ones((T, T), bool), 1)
        logits = jnp.where(causal[None, None], -jnp.inf, logits)
        attn = jax.nn.softmax(logits, axis=-1)
        out = jnp.einsum('bhij,bhjd->bhid', attn, v)
        out = jnp.transpose(out, (0, 2, 1, 3)).reshape(B, T, D)
        return out @ Wout + bout

    def _L1_ffn_ref(input_features, centroids, ln_g, ln_b, w1, b1, w2, b2):
        import jax, jax.numpy as jnp
        import numpy as np
        E, D, F = (8, 256, 1024)
        B, S = (4, 512)

        def _layernorm(x, g, b, eps=1e-05):
            mu = jnp.mean(x, axis=-1, keepdims=True)
            var = jnp.var(x, axis=-1, keepdims=True)
            return (x - mu) * jax.lax.rsqrt(var + eps) * g + b
        Bf, Sf, Df = input_features.shape
        x = input_features.reshape(-1, Df)
        aff = x @ centroids.T
        assign = jnp.argmax(aff, axis=1)
        order = jnp.argsort(assign)
        xs = x[order]
        es = assign[order]
        alpha = jax.nn.sigmoid(jnp.take_along_axis(aff[order], es[:, None], axis=1))
        nE = centroids.shape[0]
        y = jnp.zeros_like(xs)
        for e in range(nE):
            h = _layernorm(xs, ln_g[e], ln_b[e])
            h = jax.nn.relu(h @ w1[e].T + b1[e])
            ye = xs + h @ w2[e].T + b2[e]
            y = y + jnp.where((es == e)[:, None], ye, 0.0)
        out_sorted = alpha * y + (1.0 - alpha) * xs
        inv = jnp.argsort(order)
        return out_sorted[inv].reshape(Bf, Sf, Df)
    x = L0_attn_x
    x = _layernorm(x + _L0_attn_ref(x, L0_attn_wq, L0_attn_w_down, L0_attn_wk_up, L0_attn_wv_up, L0_attn_wo), axis=-1)
    x = _layernorm(x + _L0_ffn_ref(x, L0_ffn_w_router, L0_ffn_W1, L0_ffn_b1, L0_ffn_W2, L0_ffn_b2), axis=-1)
    x = _layernorm(x + _L1_attn_ref(x, L1_attn_Wqkv, L1_attn_bqkv, L1_attn_W1p, L1_attn_W2p, L1_attn_plucker_scale, L1_attn_Wout, L1_attn_bout), axis=-1)
    x = _layernorm(x + _L1_ffn_ref(x, L1_ffn_centroids, L1_ffn_ln_g, L1_ffn_ln_b, L1_ffn_w1, L1_ffn_b1, L1_ffn_w2, L1_ffn_b2), axis=-1)
    return x

_drawn_inputs = setup_inputs


def setup_inputs(seed=0):
    import zlib

    import numpy as np

    out = dict(_drawn_inputs(seed))
    spreads = {'L0_ffn_b1': (0.0, 0.1),
     'L0_ffn_b2': (0.0, 0.1),
     'L1_attn_bqkv': (0.0, 0.1),
     'L1_attn_plucker_scale': (0.10000000149011612, 0.6),
     'L1_attn_bout': (0.0, 0.1),
     'L1_ffn_ln_g': (1.0, 0.2),
     'L1_ffn_ln_b': (0.0, 0.269),
     'L1_ffn_b1': (0.0, 0.1),
     'L1_ffn_b2': (0.0, 0.1)}
    factors = {'L1_attn_W1p': 2.75, 'L1_attn_W2p': 3.066}
    for name, (base, spread) in spreads.items():
        noise = np.random.default_rng([zlib.crc32(name.encode()), seed]).standard_normal(out[name].shape)
        drawn = base * np.exp(spread * noise) if base else spread * noise
        out[name] = jnp.asarray(drawn.astype(out[name].dtype))
    for name, factor in factors.items():
        out[name] = (out[name] * factor).astype(out[name].dtype)
    return out
```

```python
import concourse.bass as bass
from concourse import mybir
from contextlib import ExitStack
import numpy as np

F32 = mybir.dt.float32
F32R = mybir.dt.float32r
BF16 = mybir.dt.bfloat16
I32 = mybir.dt.int32
ALU = mybir.AluOpType
ACT = mybir.ActivationFunctionType
AX = mybir.AxisListType

P = 128
NBATCH, T, D = 4, 1024, 256
NH = 16
DH = D // NH
DC = D // P
TT = T // P
BLK = 512
NBLK = T // BLK
HG = 4
NG = NH // HG
FF = 1024
FC = FF // P
NE = 8
NTOK = NBATCH * T
NTILE = NTOK // P
NSLOT = NTILE + NE
TOPK = T // 2
EPS = 1e-5

LROW = 64
NL = 6
SHROW = 94
KFULL = 96


class Stage:

    def __init__(self, nc, tag):
        self.nc, self.tag, self.ctx = nc, tag, ExitStack()

    def __enter__(self):
        self.ctx.__enter__()
        return self

    def __exit__(self, *a):
        return self.ctx.__exit__(*a)

    def sb(self, name, shape, dt=F32):
        return self.ctx.enter_context(self.nc.sbuf_tensor(f"{self.tag}_{name}", shape, dt))

    def ps(self, name, shape, dt=F32):
        return self.ctx.enter_context(self.nc.psum_tensor(f"{self.tag}_{name}", shape, dt))

    def sem(self, name):
        return self.ctx.enter_context(self.nc.semaphore(f"{self.tag}_{name}"))

    def block(self):
        return self.ctx.enter_context(self.nc.Block())


def hold(eng, sem, value, passed):
    eng.wait_ge(sem, value)
    eng.sem_inc(passed, 1)


class Steps:

    def __init__(self, eng, sem, per, b):
        self.eng, self.sem, self.per, self.b, self.n = eng, sem, per, b, 0

    def did(self, ins):
        self.n += 1
        ins.then_inc(self.sem, 1)

    def settled(self, passed=None):
        if passed is not None:
            hold(self.eng, self.sem, self.b * self.per + self.n, passed)
        else:
            self.eng.wait_ge(self.sem, self.b * self.per + self.n)

    def end(self):
        assert self.n == self.per, f"{self.n} steps, not {self.per}"


def proj_jobs(layer):
    jobs = []
    if layer == 0:
        for n in range(NBLK):
            jobs.append(("lat", n, 0, "act"))
            for c in range(DC):
                jobs += [("q", n, c, "dve"), ("q_swapped", n, c, "dve")]
            for c in range(DC):
                jobs += [("k", n, c, "dve"), ("k_swapped", n, c, "dve")]
            for t in range(4 * n, 4 * n + 4):
                jobs.append(("v", t, 0, "act"))
    else:
        for h in range(2):
            jobs.append(("points", h, 0, "act"))
        for n in range(NBLK):
            for c in range(DC):
                jobs.append(("q", n, c, "dve"))
            for c in range(DC):
                jobs.append(("k", n, c, "dve"))
        for t in range(TT):
            jobs.append(("v", t, 0, "dve"))
        for w in range(2):
            for h in range(2):
                jobs.append(("lines", w, h, "dve"))
    return jobs


def ring_jobs():
    def chunks(g):
        return [("max", g, j, qt, c) for j in range(HG) for qt in range(TT) for c in range(1 + (qt >= 4))]
    first = chunks(0) + [("shift", 0)]
    at = {}
    for g in range(NG):
        for i in range(12):
            at[g, i] = []
        if g + 1 < NG:
            todo = chunks(g + 1)
            for i in range(4, 10):
                at[g, i] += todo[(i - 4) * 8:(i - 3) * 8]
            at[g, 10].append(("shift", g + 1))
        at[g, 7].insert(0, ("sums", 2 * g))
        if g > 0:
            at[g, 3].append(("sums", 2 * g - 1))
    last = [("sums", 2 * NG - 1)]
    order = first + [x for g in range(NG) for i in range(12) for x in at[g, i]] + last
    return first, at, last, order


def attention(nc, layer, W, x_in, xT_in, x_out, xT_out, qk_d, ln_d):
    with Stage(nc, f"at{layer}") as S:
        jobs = proj_jobs(layer)
        NPJ = len(jobs)
        NPJ_ACT = sum(j[3] == "act" for j in jobs)
        NPJ_DVE = NPJ - NPJ_ACT
        first, at, last, order = ring_jobs()
        NR = len(order)
        NSTEP = 12 * NG
        NPAIR = 2 * NSTEP
        NU = 2 * NG
        NNAT = 2 * NBLK * DC

        if layer == 0:
            wq = S.sb("wq", [P, DC, D]); wqs = S.sb("wqs", [P, DC, D])
            wd = S.sb("wd", [P, DC, P]); wk = S.sb("wk", [P, D]); wks = S.sb("wks", [P, D]); wv = S.sb("wv", [P, D])
            rope = S.sb("rope", [P, 2, T])
        else:
            wqkv = S.sb("wqkv", [P, DC, 3 * D]); w12 = S.sb("w12", [P, DC, P])
            bqk = S.sb("bqk", [P, 4]); bv = S.sb("bv", [P, D]); bo = S.sb("bo", [P, D])
            jscale = S.sb("jscale", [P, NH, NL]); scale16 = S.sb("scale16", [P, NH]); jsign = S.sb("jsign", [P, NL])
            nat_l = S.sb("nat_l", [96, 4, T], F32R)
        wo = S.sb("wo", [P, NG, D])
        sel = S.sb("sel", [P, P]); ident = S.sb("ident", [P, P])
        identb = S.sb("identb", [P, P], BF16); maskT = S.sb("maskT", [P, P], BF16); maskf = S.sb("maskf", [P, P])
        xT = S.sb("xT", [P, DC, T])
        xr = S.sb("xr", [P, TT, D])
        nat = S.sb("nat", [P, 4, DC, T], F32R)
        qst = [S.sb(f"qst{i}", [KFULL, HG, T], F32R) for i in range(2)]
        kst = [S.sb(f"kst{i}", [KFULL, HG, T], F32R) for i in range(2)]
        vaug = S.sb("vaug", [P, TT, NH, 32])
        work = S.sb("work", [P, 4 * 1024])
        probs = work[:, :].rearrange("p (s j t) -> p s j t", s=4, j=2)
        o_sb = S.sb("o_sb", [P, 2, BLK]); rec = S.sb("rec", [P, 2, BLK])
        oT = S.sb("oT", [P, NG, T])
        mx = S.sb("mx", [P, HG, TT]); mx2 = S.sb("mx2", [P, HG, 4])
        sh = S.sb("sh", [32, 2, P], F32R)
        stats = S.sb("stats", [P, TT, 6]); mv = S.sb("mv", [P, TT, 2]); sd = S.sb("sd", [P, TT]); rstd = S.sb("rstd", [P, TT])
        if layer == 0:
            rt = work[:, 0:3072].rearrange("p (k s t) -> p k s t", k=3, s=2)
            lat = work[:, 3072:4096]
        else:
            rt = work[:, 0:1024].rearrange("p (k s t) -> p k s t", k=1, s=2)
            p1 = work[:, 1024:1536]; p2 = work[:, 1536:2048]
            la = work[:, 2048:2816]; lb = work[:, 2816:3584]
            ln2 = S.sb("ln2", [P, P]); lrn = S.sb("lrn", [P, P])
        bank = S.ps("bank", [P, 8, BLK])
        scores = [bank[:, 0:2, :], bank[:, 2:4, :]]
        PV0, RING0 = 4, 6

        s_w = S.sem("weights_loaded"); s_init = S.sem("constants_set"); s_js = S.sem("line_scales_set")
        s_xt = S.sem("features_loaded"); s_xr = S.sem("tokens_loaded"); s_bo = S.sem("bias_added")
        s_pj = S.sem("projection_ready"); s_pa = S.sem("bank_emptied_by_act"); s_pd = S.sem("bank_emptied_by_dve")
        s_cast = S.sem("masks_cast"); s_lh = S.sem("line_high_ready"); s_rs = S.sem("rstd_ready"); s_nat = S.sem("nat_piece_ready"); s_pl = S.sem("pool_steps"); s_passed_pool = S.sem("pool_waits_passed")
        s_lv = S.sem("line_steps"); s_lq = S.sem("lines_ready"); s_sq = S.sem("norms_rooted")
        s_qkd = S.sem("qk_stored"); s_stk = [S.sem(f"stack_loaded{i}") for i in range(2)]
        s_sh = S.sem("shift_ready"); s_shl = S.sem("shift_loaded")
        s_ring = S.sem("ring_filled"); s_rd = S.sem("ring_emptied"); s_cb = S.sem("maxima_ready")
        s_st = S.sem("scores_ready"); s_ex = S.sem("probs_ready"); s_pv = S.sem("values_added")
        s_ov = S.sem("output_copied"); s_ot = S.sem("output_scaled")
        s_wo = S.sem("out_projected"); s_z = S.sem("ln_steps"); s_sd = S.sem("deviation_ready")
        s_y = S.sem("result_ready"); s_passed = S.sem("waits_passed"); s_tr = S.sem("result_transposed"); s_te = S.sem("features_ready")
        s_out = S.sem("result_stored")
        block = S.block()

        NW = 8
        NWALL = NW + 3
        SCALE = float(DH) ** -0.5
        NQKD = 4 if layer == 0 else 8
        NSTK = 8 if layer == 0 else 16
        NLINE = 17

        @block.sync
        def _(sp):
            def load_weights():
                if layer == 0:
                    pairs = [(wq, W["L0_wq"].rearrange("(c p) n -> p c n", p=P)), (wqs, W["L0_wqs"].rearrange("(c p) n -> p c n", p=P)),
                             (wd, W["L0_wd"].rearrange("(c p) n -> p c n", p=P)), (wk, W["L0_wk"]), (wks, W["L0_wks"]),
                             (wv, W["L0_wv"]), (rope, W["rope"].rearrange("k p t -> p k t")),
                             (wo, W["L0_wo"].rearrange("(c p) n -> p c n", p=P))]
                else:
                    pairs = [(wqkv, W["L1_wqkv"].rearrange("(c p) n -> p c n", p=P)), (w12, W["L1_w12"].rearrange("(c p) n -> p c n", p=P)),
                             (bqk, W["L1_bqk"]),
                             (bv, W["L1_bv"].partition_broadcast(P)), (bo, W["L1_bout"].partition_broadcast(P)),
                             (scale16, W["L1_pscale"].partition_broadcast(P)), (jsign, W["jsign"]),
                             (wo, W["L1_wo"].rearrange("(c p) n -> p c n", p=P))]
                assert len(pairs) == NW
                for dst, src in pairs:
                    dst = dst[:, :, :] if len(dst.shape) == 3 else dst[:, :]
                    sp.dma_start(dst, src).then_inc(s_w, 16)
                sp.dma_start(ident[:, :], W["ident"]).then_inc(s_w, 16)
                sp.dma_start(sel[:, :], W["sel"]).then_inc(s_w, 16)
                sp.dma_start(maskf[:, :], W[f"maskT{layer}"]).then_inc(s_w, 16)

            load_weights()
            sp.wait_ge(s_init, 6)
            with sp.Fori(0, NBATCH) as b:
                sp.dma_start(xT[:, :, :], xT_in[b].rearrange("(c p) t -> p c t", p=P)).then_inc(s_xt, 16)
                sp.dma_start(xr[:, :, :], x_in[b].rearrange("(n p) d -> p n d", p=P)).then_inc(s_xr, 16)
                sp.wait_ge(s_nat, b * NNAT + NNAT)
                for m in range(4):
                    sp.dma_start(qk_d[b, m].rearrange("(c p) t -> p c t", p=P), nat[:, m, :, :].bitcast(F32)).then_inc(s_qkd, 16)
                if layer == 1:
                    sp.wait_ge(s_pd, b * NPJ_DVE + NPJ_DVE)
                    for m in range(4):
                        sp.dma_start(ln_d[b, m], nat_l[:, m, :].bitcast(F32)).then_inc(s_qkd, 16)
                sp.wait_ge(s_qkd, b * (16 * NQKD) + 16 * NQKD)

                def load_stacks(g):
                    q, k, sem = qst[g % 2], kst[g % 2], s_stk[g % 2]
                    if g >= 2:
                        sp.wait_ge(s_st, b * NPAIR + (g - 1) * 24)
                    for r, (mq, mk) in enumerate(((0, 2), (0, 3), (1, 2), (1, 3))):
                        for dst, m in ((q, mq), (k, mk)):
                            src = qk_d[b, m, 64 * g:64 * g + 64, :].rearrange("(j p) t -> p j t", j=HG)
                            sp.dma_start(dst[16 * r:16 * r + 16, :, :].bitcast(F32), src).then_inc(sem, 16)
                            if layer == 1:
                                src = ln_d[b, m, 24 * g:24 * g + 24, :].rearrange("(j p) t -> p j t", j=HG)
                                r0 = LROW + NL * r
                                sp.dma_start(dst[r0:r0 + NL, :, :].bitcast(F32), src).then_inc(sem, 16)

                def load_shift(g):
                    sp.wait_ge(s_rd, b * NR + order.index(("shift", g)) + 1)
                    for m in range(2):
                        dst = qst[g % 2][SHROW + m:SHROW + m + 1, :, :].bitcast(F32).rearrange("o j (n t) -> o (j n) t", t=P)
                        sp.dma_start(dst, sh[:, m, :].bitcast(F32)).then_inc(s_shl, 16)

                load_stacks(0)
                load_stacks(1)
                load_shift(0)
                for g in range(NG):
                    if g + 1 < NG:
                        load_shift(g + 1)
                    if g + 2 < NG:
                        load_stacks(g + 2)
                sp.wait_ge(s_y, b * TT + TT)
                sp.dma_start(x_out[b].rearrange("(n p) d -> p n d", p=P), xr[:, :, :]).then_inc(s_out, 16)
                sp.wait_ge(s_te, b * 4 + 4)
                sp.dma_start(xT_out[b].rearrange("(c p) t -> p c t", p=P), xT[:, :, :]).then_inc(s_out, 16)
                hold(sp, s_out, b * 32 + 32, s_passed)

        @block.gpsimd
        def _(pool):
            for i in range(2):
                nc.gpsimd.memset(qst[i][LROW:KFULL, :, :].bitcast(F32), 0.0).then_inc(s_init, 1)
                nc.gpsimd.memset(kst[i][LROW:KFULL, :, :].bitcast(F32), -1.0).then_inc(s_init, 1)
            pool.wait_ge(s_init, 4)
            nc.gpsimd.memset(vaug[:, :, :, 16:32], 0.0).then_inc(s_init, 1)
            pool.wait_ge(s_init, 5)
            nc.gpsimd.memset(vaug[:, :, :, 16:17], 1.0).then_inc(s_init, 1)
            NPL = NNAT * (2 if layer == 0 else 1)
            with pool.Fori(0, NBATCH) as b:
                steps = Steps(pool, s_pl, NPL, b)
                if layer == 1:
                    pool.wait_ge(s_xr, b * 16 + 16)
                    pool.wait_ge(s_w, 16 * NWALL)
                    for t in range(TT):
                        nc.gpsimd.tensor_tensor(out=xr[:, t, :], in0=xr[:, t, :], in1=bo[:, :], op=ALU.add).then_inc(s_bo, 1)
                i = 0
                for n in range(NBLK):
                    for m in (0, 2):
                        for c in range(DC):
                            pool.wait_ge(s_pd, b * NPJ_DVE + (i + 1) * (2 if layer == 0 else 1))
                            high = nat[:, m, c, n * BLK:(n + 1) * BLK]
                            if layer == 0:
                                full = rt[:, 2, i % 2, :]
                                for dst in (full, high):
                                    steps.did(nc.gpsimd.tensor_tensor(out=dst, in0=rt[:, 0, i % 2, :], in1=rt[:, 1, i % 2, :], op=ALU.add))
                            else:
                                full = rt[:, 0, i % 2, :]
                                pool.sem_inc(s_passed_pool, 1)
                                steps.did(nc.gpsimd.tensor_copy(high, full))
                            steps.settled()
                            nc.gpsimd.tensor_tensor(out=nat[:, m + 1, c, n * BLK:(n + 1) * BLK], in0=full, in1=high.bitcast(F32),
                                                    op=ALU.subtract).then_inc(s_nat, 1)
                            i += 1
                steps.end()
                for u in range(NU):
                    pool.wait_ge(s_rd, b * NR + order.index(("sums", u)) + 1)
                    nc.gpsimd.tensor_tensor(out=oT[:, u // 2, (u % 2) * BLK:(u % 2 + 1) * BLK], in0=o_sb[:, u % 2, :],
                                            in1=rec[:, u % 2, :], op=ALU.mult).then_inc(s_ot, 1)
                pool.wait_ge(s_qkd, b * (16 * NQKD) + 16 * NQKD)
                pool.wait_ge(s_wo, b * TT + TT)

        @block.scalar
        def _(act):
            with act.Fori(0, NBATCH) as b:
                na = 0
                for r, (kind, i0, i1, eng) in enumerate(jobs):
                    if eng != "act":
                        continue
                    act.wait_ge(s_pj, b * NPJ + r + 1)
                    src = bank[:, r % 4, :]
                    if kind == "lat":
                        nc.scalar.copy(lat[:, i0 * BLK:(i0 + 1) * BLK], src).then_inc(s_pa, 1)
                    elif kind == "v":
                        if i0 == 0:
                            act.wait_ge(s_init, 6)
                        nc.scalar.copy(vaug[:, i0, :, 0:DH], src[:, 0:D].rearrange("p (h d) -> p h d", d=DH)).then_inc(s_pa, 1)
                    elif kind == "points":
                        s4 = src.rearrange("p (n w h) -> p n w h", n=4, w=2)
                        for w, dst in enumerate((p1, p2)):
                            ins = nc.scalar.copy(dst[:, i0 * 256:(i0 + 1) * 256].rearrange("p (n h) -> p n h", n=4), s4[:, :, w, :])
                        ins.then_inc(s_pa, 1)
                    na += 1
                assert na == NPJ_ACT
                if layer == 1:
                    act.wait_ge(s_lv, b * NLINE + 9)
                    nc.scalar.activation(lrn[:, :], ln2[:, :], ACT.Sqrt).then_inc(s_sq, 1)

                def copy_output(u):
                    act.wait_ge(s_pv, b * NSTEP + (u // 2) * 12 + (12 if u % 2 else 4))
                    if u >= 2:
                        act.wait_ge(s_ot, b * NU + u - 1)
                    nc.scalar.copy(o_sb[:, u % 2, :], bank[:, PV0 + u % 2, :]).then_inc(s_ov, 1)

                for s in range(NSTEP):
                    i = s % 12
                    off = P * (i if i < 4 else max(0, i - 8))
                    for p in range(2):
                        e = 2 * s + p
                        act.wait_ge(s_st, b * NPAIR + e + 1)
                        if s >= 2:
                            act.wait_ge(s_pv, b * NSTEP + s - 1)
                        nc.scalar.activation(probs[:, e % 4, :, off:], scores[e % 2][:, :, off:], ACT.Exp, scale=SCALE).then_inc(s_ex, 1)
                    if i == 5:
                        copy_output(2 * (s // 12))
                    if i == 1 and s > 12:
                        copy_output(2 * (s // 12) - 1)
                copy_output(NU - 1)
                act.wait_ge(s_z, b * (3 * TT + 1) + 3 * TT + 1)
                nc.scalar.activation(sd[:, :], sd[:, :], ACT.Sqrt).then_inc(s_sd, 1)
                for k in range(4):
                    act.wait_ge(s_tr, b * 4 + k + 1)
                    nc.scalar.copy(xT[:, k // 2, (k % 2) * BLK:(k % 2 + 1) * BLK], bank[:, k, :]).then_inc(s_te, 1)

        @block.vector
        def _(dve):
            dve.wait_ge(s_w, 16 * NWALL)
            nc.vector.tensor_copy(identb[:, :], ident[:, :]).then_inc(s_cast, 1)
            nc.vector.tensor_copy(maskT[:, :], maskf[:, :]).then_inc(s_cast, 1)
            if layer == 1:
                for c in range(NL):
                    ins = nc.vector.tensor_scalar(jscale[:, :, c], scale16[:, :], jsign[:, c:c + 1], 1.0 / SCALE, ALU.mult, ALU.mult)
                ins.then_inc(s_js, 1)
                dve.wait_ge(s_js, 1)
            with dve.Fori(0, NBATCH) as b:
                piece = 0
                nd = 0

                def lines():
                    steps = Steps(dve, s_lv, NLINE, b)
                    dve.wait_ge(s_pa, b * NPJ_ACT + NPJ_ACT)
                    q1 = p1.rearrange("p (n c) -> p n c", c=4)
                    q2 = p2.rearrange("p (n c) -> p n c", c=4)
                    a = la.rearrange("p (n c) -> p n c", c=NL)
                    bb = lb.rearrange("p (n c) -> p n c", c=NL)
                    at_ = 0
                    for i, k in ((0, 3), (1, 2), (2, 1)):
                        for dst, x, y in ((a, q1, q2), (bb, q2, q1)):
                            one = x[:, :, i:i + 1] if k == 1 else x[:, :, i:i + 1].broadcast_to([P, P, k])
                            steps.did(nc.vector.tensor_tensor(out=dst[:, :, at_:at_ + k], in0=one, in1=y[:, :, i + 1:4], op=ALU.mult))
                        at_ += k
                    steps.settled()
                    steps.did(nc.vector.tensor_tensor(out=la, in0=la, in1=lb, op=ALU.subtract))
                    steps.settled()
                    steps.did(nc.vector.tensor_tensor(out=lb, in0=la, in1=la, op=ALU.mult))
                    steps.settled()
                    steps.did(nc.vector.tensor_reduce(out=ln2[:, :], in_=bb, axis=AX.X, op=ALU.add))
                    dve.wait_ge(s_sq, b + 1)
                    steps.did(nc.vector.tensor_scalar(lrn[:, :], lrn[:, :], 1e-12, None, ALU.max))
                    steps.settled()
                    steps.did(nc.vector.reciprocal(ln2[:, :], lrn[:, :]))
                    steps.settled()
                    steps.did(nc.vector.tensor_tensor(out=a, in0=a, in1=ln2[:, :].unsqueeze(2).broadcast_to([P, P, NL]), op=ALU.mult))
                    steps.settled()
                    a4 = la.rearrange("p (n h c) -> p n h c", h=NH, c=NL)
                    b4 = lb.rearrange("p (n h c) -> p n h c", h=NH, c=NL)
                    js = jscale[:, :, :]
                    for c in range(NL - 1):
                        steps.did(nc.vector.tensor_tensor(out=b4[:, :, :, c], in0=a4[:, :, :, NL - 1 - c],
                                                          in1=js[:, :, c].unsqueeze(1).broadcast_to([P, TT, NH]), op=ALU.mult))
                    c = NL - 1
                    nc.vector.tensor_tensor(out=b4[:, :, :, c], in0=a4[:, :, :, NL - 1 - c],
                                            in1=js[:, :, c].unsqueeze(1).broadcast_to([P, TT, NH]), op=ALU.mult).then_inc(s_lq, 1)
                    steps.end()

                for r, (kind, i0, i1, eng) in enumerate(jobs):
                    if eng != "dve":
                        continue
                    if kind == "lines" and i0 == 0 and i1 == 0:
                        lines()
                    dve.wait_ge(s_pj, b * NPJ + r + 1)
                    src = bank[:, r % 4, :]
                    if kind in ("q", "k", "q_swapped", "k_swapped"):
                        if piece >= 2 and kind in ("q", "k"):
                            dve.wait_ge(s_nat, b * NNAT + piece - 1)
                        if layer == 0:
                            w = int(kind.endswith("swapped"))
                            nc.vector.tensor_tensor(out=rt[:, w, piece % 2, :], in0=src, in1=rope[:, w, i0 * BLK:(i0 + 1) * BLK],
                                                    op=ALU.mult).then_inc(s_pd, 1)
                            piece += w
                        else:
                            col = i1 + (2 if kind == "k" else 0)
                            nc.vector.tensor_scalar(rt[:, 0, piece % 2, :], src, bqk[:, col:col + 1], None, ALU.add).then_inc(s_pd, 1)
                            piece += 1
                    elif kind == "v":
                        if i0 == 0:
                            dve.wait_ge(s_init, 6)
                        nc.vector.tensor_tensor(out=vaug[:, i0, :, 0:DH], in0=src[:, 0:D].rearrange("p (h d) -> p h d", d=DH),
                                                in1=bv[:, :].rearrange("p (h d) -> p h d", d=DH), op=ALU.add).then_inc(s_pd, 1)
                    else:
                        high = nat_l[:, 2 * i0, i1 * BLK:(i1 + 1) * BLK]
                        nc.vector.tensor_copy(high, src[0:96, :]).then_inc(s_lh, 1)
                        dve.wait_ge(s_lh, b * 4 + 2 * i0 + i1 + 1)
                        nc.vector.tensor_tensor(out=nat_l[:, 2 * i0 + 1, i1 * BLK:(i1 + 1) * BLK], in0=src[0:96, :], in1=high.bitcast(F32),
                                                op=ALU.subtract).then_inc(s_pd, 1)
                    nd += 1
                assert nd == NPJ_DVE

                for r, job in enumerate(order):
                    src = bank[:, RING0 + r % 2, :]
                    if job[0] == "max":
                        _, g, j, qt, c = job
                        dve.wait_ge(s_ring, b * NR + r + 1)
                        w = BLK if (qt >= 4 and c == 0) else P * (qt % 4 + 1)
                        dst = mx2[:, j, qt - 4:qt - 3] if c else mx[:, j, qt:qt + 1]
                        nc.vector.tensor_reduce(out=dst, in_=src[:, 0:w], axis=AX.X, op=ALU.max).then_inc(s_rd, 1)
                    elif job[0] == "shift":
                        g = job[1]
                        dve.wait_ge(s_rd, b * NR + r)
                        nc.vector.tensor_tensor(out=mx[:, :, 4:8], in0=mx[:, :, 4:8], in1=mx2[:, :, :], op=ALU.max).then_inc(s_cb, 1)
                        dve.wait_ge(s_ring, b * NR + r + 1)
                        if g:
                            dve.wait_ge(s_shl, (b * NG + g) * 32)
                        nc.vector.tensor_copy(sh[:, 0, :], src[0:32, 0:P]).then_inc(s_sh, 1)
                        dve.wait_ge(s_sh, b * NG + g + 1)
                        nc.vector.tensor_tensor(out=sh[:, 1, :], in0=src[0:32, 0:P], in1=sh[:, 0, :].bitcast(F32), op=ALU.subtract).then_inc(s_rd, 1)
                    else:
                        u = job[1]
                        dve.wait_ge(s_ring, b * NR + r + 1)
                        if u >= 2:
                            dve.wait_ge(s_ot, b * NU + u - 1)
                        nc.vector.reciprocal(rec[:, u % 2, :], src).then_inc(s_rd, 1)

                steps = Steps(dve, s_z, 3 * TT + 1, b)
                if layer == 0:
                    dve.wait_ge(s_xr, b * 16 + 16)
                else:
                    dve.wait_ge(s_bo, b * TT + TT)
                for t in range(TT):
                    dve.wait_ge(s_wo, b * TT + t + 1)
                    steps.did(nc.vector.tensor_tensor(out=xr[:, t, :], in0=bank[:, t % 4, 0:D], in1=xr[:, t, :], op=ALU.add))
                steps.settled()
                for t in range(TT):
                    steps.did(nc.vector.bn_stats(out=stats[:, t, :], in_=xr[:, t, :]))
                steps.settled(s_passed)
                for t in range(TT):
                    steps.did(nc.vector.bn_aggr(out=mv[:, t, :], in_=stats[:, t, :]))
                steps.settled()
                steps.did(nc.vector.tensor_scalar(sd[:, :], mv[:, :, 1], EPS, None, ALU.add))
                steps.end()
                dve.wait_ge(s_sd, b + 1)
                nc.vector.reciprocal(rstd[:, :], sd[:, :]).then_inc(s_rs, 1)
                dve.wait_ge(s_rs, b + 1)
                for t in range(TT):
                    nc.vector.tensor_scalar(xr[:, t, :], xr[:, t, :], mv[:, t, 0:1], rstd[:, t:t + 1], ALU.subtract, ALU.mult).then_inc(s_y, 1)
                dve.wait_ge(s_shl, b * (32 * NG) + 32 * NG)
                dve.wait_ge(s_qkd, b * (16 * NQKD) + 16 * NQKD)

        @block.tensor
        def _(pe):
            pe.wait_ge(s_w, 16 * NWALL)
            pe.wait_ge(s_cast, 2)
            pe.wait_ge(s_init, 6)
            with pe.Fori(0, NBATCH) as b:
                emptied = {"act": 0, "dve": 0}
                users = []

                def all_k(out, pairs):
                    for n, (lhsT, rhs) in enumerate(pairs):
                        ins = nc.tensor.matmul(out, lhsT, rhs, start=(n == 0), stop=(n == len(pairs) - 1))
                    return ins

                pe.wait_ge(s_xt, b * 16 + 16)
                lat_done = {}
                for r, (kind, i0, i1, eng) in enumerate(jobs):
                    emptied[eng] += 1
                    users.append((eng, emptied[eng]))
                    if r >= 4:
                        e4, n4 = users[r - 4]
                        if e4 == "act":
                            pe.wait_ge(s_pa, b * NPJ_ACT + n4)
                        else:
                            pe.wait_ge(s_pd, b * NPJ_DVE + n4)
                    dst = bank[:, r % 4, :]
                    blk = slice(i0 * BLK, (i0 + 1) * BLK)
                    if kind == "lat":
                        lat_done[i0] = emptied["act"]
                        ins = all_k(dst, [(wd[:, kc, :], xT[:, kc, blk]) for kc in range(DC)])
                    elif kind == "points":
                        for n in range(4):
                            tok = slice((4 * i0 + n) * P, (4 * i0 + n + 1) * P)
                            ins = all_k(dst[:, n * P:(n + 1) * P], [(xT[:, kc, tok], w12[:, kc, :]) for kc in range(DC)])
                    elif kind in ("q", "q_swapped", "k", "k_swapped") and (layer == 1 or kind[0] == "q"):
                        if layer == 0:
                            w, o0 = (wq if kind == "q" else wqs), i1 * P
                        else:
                            w, o0 = wqkv, i1 * P + (D if kind == "k" else 0)
                        ins = all_k(dst, [(w[:, kc, o0:o0 + P], xT[:, kc, blk]) for kc in range(DC)])
                    elif kind in ("k", "k_swapped"):
                        pe.wait_ge(s_pa, b * NPJ_ACT + lat_done[i0])
                        w = wk if kind == "k" else wks
                        ins = all_k(dst, [(w[:, i1 * P:(i1 + 1) * P], lat[:, blk])])
                    elif kind == "v":
                        tok = slice(i0 * P, (i0 + 1) * P)
                        if layer == 0:
                            ins = all_k(dst[:, 0:D], [(lat[:, tok], wv[:, :])])
                        else:
                            ins = all_k(dst[:, 0:D], [(xT[:, kc, tok], wqkv[:, kc, 2 * D:3 * D]) for kc in range(DC)])
                    else:
                        pe.wait_ge(s_lq, b + 1)
                        src = la if i0 == 0 else lb
                        for n in range(4):
                            t = 4 * i1 + n
                            ins = nc.tensor.transpose(dst[0:96, n * P:(n + 1) * P], src[:, t * 96:(t + 1) * 96], ident[:, :])
                    ins.then_inc(s_pj, 1)

                ring = [0]

                def ring_job(job):
                    r = ring[0]
                    ring[0] += 1
                    if r >= 2:
                        pe.wait_ge(s_rd, b * NR + r - 1)
                    dst = bank[:, RING0 + r % 2, :]
                    if job[0] == "max":
                        _, g, j, qt, c = job
                        if j == 0 and qt == 0:
                            pe.wait_ge(s_stk[g % 2], b * (2 * NSTK * 16) + (g // 2 + 1) * NSTK * 16)
                        w = BLK if (qt >= 4 and c == 0) else P * (qt % 4 + 1)
                        diag = qt < 4 or c == 1
                        ins = nc.tensor.matmul(dst[:, 0:w], qst[g % 2][0:SHROW, j, qt * P:(qt + 1) * P],
                                               kst[g % 2][0:SHROW, j, c * BLK:c * BLK + w], start=True, stop=not diag)
                        if diag:
                            ins = nc.tensor.matmul(dst[:, w - P:w], maskT[:, :], identb[:, :], start=False, stop=True)
                    elif job[0] == "shift":
                        pe.wait_ge(s_cb, b * NG + job[1] + 1)
                        ins = nc.tensor.transpose(dst[0:32, 0:P], mx[:, :, :].rearrange("p j n -> p (j n)"), ident[:, :])
                    else:
                        pe.wait_ge(s_ov, b * NU + job[1] + 1)
                        ins = nc.tensor.matmul(dst, sel[:, :], o_sb[:, job[1] % 2, :], start=True, stop=True)
                    ins.then_inc(s_ring, 1)

                def step_of(s):
                    i = s % 12
                    qb, kt = (0, i) if i < 4 else (1, i - 4)
                    return s // 12, qb, kt, P * max(0, kt - 4 * qb)

                def score_pair(s, p):
                    g, qb, kt, off = step_of(s)
                    e = 2 * s + p
                    if e >= 2:
                        pe.wait_ge(s_ex, b * NPAIR + e - 1)
                    for h in range(2):
                        j = 2 * p + h
                        dst = scores[e % 2][:, h, :]
                        diag = kt >= 4 * qb
                        ins = nc.tensor.matmul(dst[:, off:], kst[g % 2][0:KFULL, j, kt * P:(kt + 1) * P],
                                               qst[g % 2][0:KFULL, j, qb * BLK + off:(qb + 1) * BLK], start=True, stop=not diag)
                        if diag:
                            ins = nc.tensor.matmul(dst[:, off:off + P], identb[:, :], maskT[:, :], start=False, stop=True)
                    ins.then_inc(s_st, 1)

                def values(s):
                    g, qb, kt, off = step_of(s)
                    u = 2 * g + qb
                    if kt == 0 and u >= 2:
                        pe.wait_ge(s_ov, b * NU + u - 1)
                    pe.wait_ge(s_ex, b * NPAIR + 2 * s + 2)
                    for j in range(HG):
                        e = 2 * s + j // 2
                        ins = nc.tensor.matmul(bank[32 * j:32 * j + 32, PV0 + u % 2, off:], vaug[:, kt, HG * g + j, :],
                                               probs[:, e % 4, j % 2, off:], start=(kt == 0), stop=(kt == 4 * qb + 3))
                    ins.then_inc(s_pv, 1)

                for job in first:
                    ring_job(job)
                pe.wait_ge(s_pa, b * NPJ_ACT + NPJ_ACT)
                pe.wait_ge(s_pd, b * NPJ_DVE + NPJ_DVE)
                for s in range(NSTEP):
                    if s % 12 == 0:
                        pe.wait_ge(s_shl, (b * NG + s // 12) * 32 + 32)
                    for p in range(2):
                        score_pair(s, p)
                    for job in at[s // 12, s % 12]:
                        ring_job(job)
                    if s:
                        values(s - 1)
                values(NSTEP - 1)
                for job in last:
                    ring_job(job)
                assert ring[0] == NR

                pe.wait_ge(s_ot, b * NU + NU)
                pe.wait_ge(s_ex, b * NPAIR + NPAIR)
                for t in range(TT):
                    if t >= 4:
                        pe.wait_ge(s_z, b * (3 * TT + 1) + t - 3)
                    all_k(bank[:, t % 4, 0:D], [(oT[:, g, t * P:(t + 1) * P], wo[:, g, :]) for g in range(NG)]).then_inc(s_wo, 1)
                pe.wait_ge(s_y, b * TT + TT)
                for k in range(4):
                    for n in range(4):
                        t = 4 * (k % 2) + n
                        ins = nc.tensor.transpose(bank[:, k, n * P:(n + 1) * P], xr[:, t, (k // 2) * P:(k // 2 + 1) * P], ident[:, :])
                    ins.then_inc(s_tr, 1)
                pe.wait_ge(s_te, b * 4 + 4)


def mixture_of_depths(nc, W, x_in, xT_in, x_out, xT_out, score_d):
    with Stage(nc, "mod") as S:
        w1 = S.sb("w1", [P, DC, FF]); w2 = S.sb("w2", [P, FC, D])
        b1 = S.sb("b1", [P, FC]); b2 = S.sb("b2", [P, D]); wr = S.sb("wr", [P, D])
        ident = S.sb("ident", [P, P]); before = S.sb("before", [P, T])
        xT = S.sb("xT", [P, DC, T]); xr = S.sb("xr", [P, TT, D]); x2 = S.sb("x2", [P, TT, D])
        prod = S.sb("prod", [P, TT, D]); hid = S.sb("hid", [P, NBLK, FC, BLK])
        z = S.sb("z", [P, TT, D]); yT = S.sb("yT", [P, DC, T])
        sc = S.sb("sc", [P, TT]); scT = S.sb("scT", [TT, P]); row = S.sb("row", [P, T]); hit = S.sb("hit", [P, T])
        above = S.sb("above", [P, TT]); ties = S.sb("ties", [P, TT]); sig = S.sb("sig", [P, TT]); gate = S.sb("gate", [P, TT])
        stats = S.sb("stats", [P, TT, 6]); mv = S.sb("mv", [P, TT, 2]); sd = S.sb("sd", [P, TT]); rstd = S.sb("rstd", [P, TT])
        bank = S.ps("bank", [P, 8, BLK])
        NW = 7
        NH1 = NBLK * FC
        NSC = TT
        NRK = 2 * TT + 3
        NZ = 4 * TT + 1
        s_w = S.sem("weights_loaded"); s_xt = S.sem("features_loaded"); s_xr = S.sem("tokens_loaded")
        s_x2 = S.sem("doubled"); s_sc = S.sem("scores_ready"); s_sct = S.sem("scores_transposed"); s_scc = S.sem("score_row_copied")
        s_scd = S.sem("score_row_stored"); s_row = S.sem("score_row_loaded"); s_rk = S.sem("rank_steps"); s_sig = S.sem("sigmoid_ready")
        s_h = S.sem("hidden_ready"); s_ge = S.sem("gelu_ready"); s_o = S.sem("update_ready"); s_z = S.sem("ln_steps")
        s_sd = S.sem("deviation_ready"); s_rs = S.sem("rstd_ready"); s_y = S.sem("result_ready"); s_passed = S.sem("waits_passed")
        s_tr = S.sem("result_transposed"); s_te = S.sem("features_ready"); s_out = S.sem("result_stored")
        block = S.block()

        @block.sync
        def _(sp):
            sp.dma_start(w1[:, :, :], W["m_w1"].rearrange("(c p) n -> p c n", p=P)).then_inc(s_w, 16)
            sp.dma_start(w2[:, :, :], W["m_w2"].rearrange("(c p) n -> p c n", p=P)).then_inc(s_w, 16)
            sp.dma_start(b1[:, :], W["m_b1T"]).then_inc(s_w, 16)
            sp.dma_start(b2[:, :], W["m_b2"].partition_broadcast(P)).then_inc(s_w, 16)
            sp.dma_start(wr[:, :], W["m_wr"].partition_broadcast(P)).then_inc(s_w, 16)
            sp.dma_start(ident[:, :], W["ident"]).then_inc(s_w, 16)
            sp.dma_start(before[:, :], W["before"]).then_inc(s_w, 16)
            with sp.Fori(0, NBATCH) as b:
                sp.dma_start(xT[:, :, :], xT_in[b].rearrange("(c p) t -> p c t", p=P)).then_inc(s_xt, 16)
                sp.dma_start(xr[:, :, :], x_in[b].rearrange("(n p) d -> p n d", p=P)).then_inc(s_xr, 16)
                sp.wait_ge(s_scc, b + 1)
                sp.dma_start(score_d[b].rearrange("(n p) -> n p", p=P), scT[:, :]).then_inc(s_scd, 16)
                sp.wait_ge(s_scd, b * 16 + 16)
                sp.dma_start(row[:, :], score_d[b].partition_broadcast(P)).then_inc(s_row, 16)
                sp.wait_ge(s_y, b * TT + TT)
                sp.dma_start(x_out[b].rearrange("(n p) d -> p n d", p=P), z[:, :, :]).then_inc(s_out, 16)
                sp.wait_ge(s_te, b * 4 + 4)
                sp.dma_start(xT_out[b].rearrange("(c p) t -> p c t", p=P), yT[:, :, :]).then_inc(s_out, 16)
            sp.wait_ge(s_out, NBATCH * 32)

        @block.gpsimd
        def _(pool):
            with pool.Fori(0, NBATCH) as b:
                pool.wait_ge(s_xr, b * 16 + 16)
                nc.gpsimd.tensor_tensor(out=x2[:, :, :], in0=xr[:, :, :], in1=xr[:, :, :], op=ALU.add).then_inc(s_x2, 1)
                pool.wait_ge(s_z, b * NZ + NZ)

        @block.scalar
        def _(act):
            act.wait_ge(s_w, 16 * NW)
            with act.Fori(0, NBATCH) as b:
                act.wait_ge(s_sc, b * NSC + NSC)
                nc.scalar.activation(sig[:, :], sc[:, :], ACT.Sigmoid).then_inc(s_sig, 1)
                for q in range(NH1):
                    act.wait_ge(s_h, b * NH1 + q + 1)
                    nc.scalar.activation(hid[:, q // FC, q % FC, :], bank[:, q % 4, :], ACT.Gelu_apprx_tanh,
                                         bias=b1[:, q % FC:q % FC + 1]).then_inc(s_ge, 1)
                act.wait_ge(s_z, b * NZ + NZ)
                nc.scalar.activation(sd[:, :], sd[:, :], ACT.Sqrt).then_inc(s_sd, 1)
                for k in range(4):
                    act.wait_ge(s_tr, b * 4 + k + 1)
                    nc.scalar.copy(yT[:, k // 2, (k % 2) * BLK:(k % 2 + 1) * BLK], bank[:, k, :]).then_inc(s_te, 1)
                act.wait_ge(s_out, b * 32 + 32)

        @block.vector
        def _(dve):
            dve.wait_ge(s_w, 16 * NW)
            with dve.Fori(0, NBATCH) as b:
                dve.wait_ge(s_xr, b * 16 + 16)
                for t in range(TT):
                    nc.vector.tensor_tensor_reduce(out=prod[:, t, :], in0=xr[:, t, :], in1=wr[:, :], scale=1.0, scalar=0.0,
                                                   op0=ALU.mult, op1=ALU.add, accum_out=sc[:, t:t + 1]).then_inc(s_sc, 1)
                dve.wait_ge(s_sct, b + 1)
                nc.vector.tensor_copy(scT[:, :], bank[0:TT, 6, 0:P]).then_inc(s_scc, 1)
                dve.wait_ge(s_row, b * 16 + 16)
                steps = Steps(dve, s_rk, NRK, b)
                for t in range(TT):
                    steps.settled()
                    steps.did(nc.vector.tensor_scalar(hit[:, :], row[:, :], sc[:, t:t + 1], 0.0, ALU.is_gt, ALU.add,
                                                      accum_out=above[:, t:t + 1]))
                    steps.settled()
                    n = P * (t + 1)
                    steps.did(nc.vector.scalar_tensor_tensor(out=hit[:, 0:n], in0=row[:, 0:n], scalar=sc[:, t:t + 1],
                                                             in1=before[:, T - n:T], op0=ALU.is_equal, op1=ALU.mult,
                                                             accum_out=ties[:, t:t + 1]))
                steps.settled()
                steps.did(nc.vector.tensor_tensor(out=above[:, :], in0=above[:, :], in1=ties[:, :], op=ALU.add))
                steps.settled()
                steps.did(nc.vector.tensor_scalar(above[:, :], above[:, :], float(TOPK), None, ALU.is_lt))
                steps.settled()
                dve.wait_ge(s_sig, b + 1)
                steps.did(nc.vector.tensor_tensor(out=gate[:, :], in0=above[:, :], in1=sig[:, :], op=ALU.mult))
                steps.settled()
                steps.end()
                dve.wait_ge(s_x2, b + 1)
                steps = Steps(dve, s_z, NZ, b)
                for t in range(TT):
                    dve.wait_ge(s_o, b * TT + t + 1)
                    steps.did(nc.vector.tensor_tensor(out=z[:, t, :], in0=bank[:, 4 + t % 2, 0:D], in1=b2[:, :], op=ALU.add))
                    steps.settled()
                    steps.did(nc.vector.scalar_tensor_tensor(out=z[:, t, :], in0=z[:, t, :], scalar=gate[:, t:t + 1], in1=x2[:, t, :],
                                                             op0=ALU.mult, op1=ALU.add))
                steps.settled()
                for t in range(TT):
                    steps.did(nc.vector.bn_stats(out=stats[:, t, :], in_=z[:, t, :]))
                steps.settled(s_passed)
                for t in range(TT):
                    steps.did(nc.vector.bn_aggr(out=mv[:, t, :], in_=stats[:, t, :]))
                steps.settled()
                steps.did(nc.vector.tensor_scalar(sd[:, :], mv[:, :, 1], EPS, None, ALU.add))
                steps.end()
                dve.wait_ge(s_sd, b + 1)
                nc.vector.reciprocal(rstd[:, :], sd[:, :]).then_inc(s_rs, 1)
                dve.wait_ge(s_rs, b + 1)
                for t in range(TT):
                    nc.vector.tensor_scalar(z[:, t, :], z[:, t, :], mv[:, t, 0:1], rstd[:, t:t + 1], ALU.subtract, ALU.mult).then_inc(s_y, 1)
                dve.wait_ge(s_tr, b * 4 + 4)
                dve.wait_ge(s_out, b * 32 + 32)

        @block.tensor
        def _(pe):
            pe.wait_ge(s_w, 16 * NW)
            with pe.Fori(0, NBATCH) as b:
                pe.wait_ge(s_xt, b * 16 + 16)
                for n in range(NBLK):
                    for f in range(FC):
                        q = n * FC + f
                        if q >= 4:
                            pe.wait_ge(s_ge, b * NH1 + q - 3)
                        for kc in range(DC):
                            ins = nc.tensor.matmul(bank[:, q % 4, :], w1[:, kc, f * P:(f + 1) * P], xT[:, kc, n * BLK:(n + 1) * BLK],
                                                   start=(kc == 0), stop=(kc == DC - 1))
                        ins.then_inc(s_h, 1)
                    if n == 0:
                        pe.wait_ge(s_sc, b * NSC + NSC)
                        nc.tensor.transpose(bank[0:TT, 6, 0:P], sc[:, :], ident[:, :]).then_inc(s_sct, 1)
                for t in range(TT):
                    pe.wait_ge(s_ge, b * NH1 + FC * (t // 4 + 1))
                    if t >= 2:
                        pe.wait_ge(s_z, b * NZ + 2 * (t - 2) + 1)
                    for f in range(FC):
                        ins = nc.tensor.matmul(bank[:, 4 + t % 2, 0:D], hid[:, t // 4, f, (t % 4) * P:(t % 4 + 1) * P], w2[:, f, :],
                                               start=(f == 0), stop=(f == FC - 1))
                    ins.then_inc(s_o, 1)
                pe.wait_ge(s_y, b * TT + TT)
                for k in range(4):
                    for n in range(4):
                        t = 4 * (k % 2) + n
                        ins = nc.tensor.transpose(bank[:, k, n * P:(n + 1) * P], z[:, t, (k // 2) * P:(k // 2 + 1) * P], ident[:, :])
                    ins.then_inc(s_tr, 1)
                pe.wait_ge(s_te, b * 4 + 4)


def experts(nc, W, x_in, xT_in, out, sorted_d, result_d):
    with Stage(nc, "moe") as S:
        NTE = NTILE * NE
        cT = S.sb("cT", [P, DC, NE])
        ident = S.sb("ident", [P, P])
        upper_f = S.sb("upper_f", [P, P]); upper = S.sb("upper", [P, P], BF16); ones = S.sb("ones", [P, P], BF16)
        rev = S.sb("rev", [P, NE])
        not_first = S.sb("not_first", [P, NTE])
        firsts = S.sb("firsts", [P, NTILE])
        numbers = S.sb("numbers", [P, NSLOT])
        x = S.sb("x", [P, NTILE, D])
        xn = S.sb("xn", [P, NTILE, D])
        xT = S.sb("xT", [P, DC, T])
        zero = S.sb("zero", [P, D])
        aff = S.sb("aff", [P, NTE]); eq = S.sb("eq", [P, NTE]); own = S.sb("own", [P, NTE]); ownb = S.sb("ownb", [P, NTE], BF16)
        best = S.sb("best", [P, NTILE]); pick = S.sb("pick", [P, NTILE]); alpha = S.sb("alpha", [P, NTILE])
        count = S.sb("count", [P, NTE]); cum = S.sb("cum", [P, NTE]); over = S.sb("over", [P, NTE]); pos = S.sb("pos", [P, NTE])
        tiles = S.sb("tiles", [P, NE]); ends = S.sb("ends", [P, NE]); base = S.sb("base", [P, NE])
        slot_f = S.sb("slot_f", [P, NTILE]); slot = S.sb("slot", [P, NTILE], I32)
        past = S.sb("past", [1, NSLOT * NE]); eid_f = S.sb("eid_f", [1, NSLOT]); eid = S.sb("eid", [1, NSLOT], I32)
        stats = S.sb("stats", [P, NTILE, 6]); mv = S.sb("mv", [P, NTILE, 2]); sd = S.sb("sd", [P, NTILE]); rstd = S.sb("rstd", [P, NTILE])
        w1 = [S.sb(f"w1_{i}", [P, DC, FF]) for i in range(2)]
        w2 = [S.sb(f"w2_{i}", [P, FC, D]) for i in range(2)]
        small = [S.sb(f"small{i}", [P, FC + 2 * DC]) for i in range(2)]
        b2 = [S.sb(f"b2_{i}", [P, D]) for i in range(2)]
        xs = [S.sb(f"xs{i}", [P, D]) for i in range(2)]
        xsT = [S.sb(f"xsT{i}", [P, DC, P]) for i in range(2)]
        hid = [S.sb(f"hid{i}", [P, FC, P]) for i in range(2)]
        ys = [S.sb(f"ys{i}", [P, D]) for i in range(2)]
        bank = S.ps("bank", [P, 8, BLK])

        NC = 7
        NWL = 4
        NPAIRS = NSLOT // 2
        GRP = 8
        NGR = NTILE // GRP
        s_c = S.sem("constants_loaded"); s_cb = S.sem("constants_cast"); s_x = S.sem("tokens_loaded")
        s_xt = S.sem("features_loaded"); s_zero = S.sem("zeros_set"); s_zd = S.sem("slots_zeroed")
        s_aff = S.sem("affinities_ready"); s_r = S.sem("route_steps"); s_best = S.sem("best_ready"); s_alpha = S.sem("alpha_ready")
        s_own = S.sem("own_ready"); s_cnt = S.sem("counts_ready"); s_slot = S.sem("slots_ready"); s_eid = S.sem("tile_experts_ready")
        s_n = S.sem("norm_steps"); s_sd = S.sem("deviation_ready"); s_xn = S.sem("normalised"); s_sc = S.sem("scattered"); s_x2 = S.sem("doubled")
        s_wl = [S.sem(f"weights_loaded{i}") for i in range(2)]; s_xs = [S.sem(f"slots_loaded{i}") for i in range(2)]
        s_t = S.sem("slots_transposed"); s_xg = S.sem("slot_features_ready")
        s_h = S.sem("hidden_ready"); s_ra = S.sem("relu_by_act"); s_rv = S.sem("relu_by_dve")
        s_o = S.sem("slot_result_ready"); s_ys = S.sem("slot_result_biased"); s_yd = [S.sem(f"slot_result_stored{i}") for i in range(2)]
        s_g = [S.sem(f"gathered{i}") for i in range(NGR)]; s_f = S.sem("final_steps"); s_fsd = S.sem("final_deviation_ready")
        s_fy = S.sem("final_ready"); s_passed = S.sem("waits_passed"); s_frs = S.sem("final_rstd_ready"); s_out = S.sem("result_stored")
        block = S.block()

        def te(t):
            return t[:, :].rearrange("p (t e) -> p t e", e=NE)

        def et(t):
            return t[:, :].rearrange("p (e t) -> p e t", e=NE)

        def swapped(t):
            return t[:, :].rearrange("p (e t) -> p t e", e=NE)

        def slot_tiles(eng, body):
            with eng.Fori(0, NPAIRS - 1) as turn:
                for i in range(2):
                    body(2 * turn + i, turn, i, False)
            for i in range(2):
                body(NSLOT - 2 + i, NPAIRS - 1, i, i == 1)

        @block.sync
        def _(sp):
            for dst, src in ((cT[:, :, :], W["e_cT"].rearrange("(c p) e -> p c e", p=P)), (ident[:, :], W["ident"]),
                             (upper_f[:, :], W["upper"]), (rev[:, :], W["rev"]), (not_first[:, :], W["not_first"]),
                             (firsts[:, :], W["firsts"]), (numbers[:, :], W["numbers"])):
                sp.dma_start(dst, src).then_inc(s_c, 16)
            for b in range(NBATCH):
                if b:
                    sp.wait_ge(s_aff, b)
                sp.dma_start(xT[:, :, :], xT_in[b].rearrange("(c p) t -> p c t", p=P)).then_inc(s_xt, 16)
                if b == 0:
                    for bb in range(NBATCH):
                        sp.dma_start(x[:, TT * bb:TT * bb + TT, :], x_in[bb].rearrange("(n p) d -> p n d", p=P)).then_inc(s_x, 16)
                    sp.wait_ge(s_zero, 1)
                    sp.dma_start(sorted_d.rearrange("(n p) d -> p n d", p=P), zero[:, :].unsqueeze(1).broadcast_to([P, NSLOT, D])).then_inc(s_zd, 16)

            def load_weights(j, i):
                e = sp.value_load(eid[0:1, bass.ds(j, 1)], min_val=0, max_val=NE - 1)
                sp.dma_start(w1[i][:, :, :], W["e_w1T"][e].rearrange("(c p) n -> p c n", p=P)).then_inc(s_wl[i], 16)
                sp.dma_start(w2[i][:, :, :], W["e_w2T"][e].rearrange("(c p) n -> p c n", p=P)).then_inc(s_wl[i], 16)
                sp.dma_start(small[i][:, :], W["e_small"][e]).then_inc(s_wl[i], 16)
                sp.dma_start(b2[i][:, :], W["e_b2"][e].partition_broadcast(P)).then_inc(s_wl[i], 16)

            for i in range(2):
                sp.sem_inc(s_yd[i], 16)
            sp.wait_ge(s_eid, 1)
            load_weights(0, 0)
            load_weights(1, 1)
            sp.wait_ge(s_sc, 16 * NTILE)
            for i in range(2):
                sp.dma_start(xs[i][:, :], sorted_d[P * i:P * i + P, :]).then_inc(s_xs[i], 16)

            def tile(j, turn, i, last):
                hold(sp, s_ys, j + 1, s_passed)
                sp.dma_start(result_d[bass.ds(j * P, P), :], ys[i][:, :]).then_inc(s_yd[i], 16)
                if not isinstance(j, int):
                    load_weights(j + 2, i)
                    sp.dma_start(xs[i][:, :], sorted_d[bass.ds(j * P + 2 * P, P), :]).then_inc(s_xs[i], 16)

            slot_tiles(sp, tile)
            for gr in range(NGR):
                sp.wait_ge(s_fy, GRP * (gr + 1))
                tok = out.rearrange("b (n p) d -> (b n) p d", p=P)[GRP * gr:GRP * (gr + 1)].rearrange("n p d -> p n d")
                sp.dma_start(tok, xn[:, GRP * gr:GRP * (gr + 1), :]).then_inc(s_out, 16)
            sp.wait_ge(s_out, 16 * NGR)

        @block.gpsimd
        def _(pool):
            nc.gpsimd.memset(zero[:, :], 0.0).then_inc(s_zero, 1)
            pool.wait_ge(s_slot, 1)
            pool.wait_ge(s_zd, 16)
            pool.wait_ge(s_xn, NTILE)
            for t in range(NTILE):
                nc.gpsimd.indirect_dma_start(out=sorted_d[:, :], out_offset=bass.IndirectOffsetOnAxis(ap=slot[:, t:t + 1], axis=0),
                                             in_=xn[:, t, :], in_offset=None).then_inc(s_sc, 16)
            nc.gpsimd.tensor_tensor(out=x[:, :, :], in0=x[:, :, :], in1=x[:, :, :], op=ALU.add).then_inc(s_x2, 1)
            pool.wait_ge(s_sc, 16 * NTILE)
            for i in range(2):
                pool.wait_ge(s_yd[i], 16 * NPAIRS + 16)
            for t in range(NTILE):
                nc.gpsimd.indirect_dma_start(out=xn[:, t, :], out_offset=None, in_=result_d[:, :],
                                             in_offset=bass.IndirectOffsetOnAxis(ap=slot[:, t:t + 1], axis=0)).then_inc(s_g[t // GRP], 16)

        @block.scalar
        def _(act):
            act.wait_ge(s_best, 1)
            nc.scalar.activation(alpha[:, :], best[:, :], ACT.Sigmoid).then_inc(s_alpha, 1)
            act.wait_ge(s_n, 2 * NTILE + 1)
            nc.scalar.activation(sd[:, :], sd[:, :], ACT.Sqrt).then_inc(s_sd, 1)

            def tile(j, turn, i, last):
                act.wait_ge(s_wl[i], (16 * NWL) * turn + 16 * NWL)
                act.wait_ge(s_h, 2 * j + 1)
                for f in range(FC // 2):
                    nc.scalar.activation(hid[i][:, f, :], bank[:, 2 * i + f // 4, (f % 4) * P:(f % 4 + 1) * P], ACT.Relu,
                                         bias=small[i][:, f:f + 1]).then_inc(s_ra, 1)

            slot_tiles(act, tile)
            for gr in range(NGR):
                act.wait_ge(s_f, (gr + 1) * (3 * GRP + 1))
                part = sd[:, GRP * gr:GRP * (gr + 1)]
                nc.scalar.activation(part, part, ACT.Sqrt).then_inc(s_fsd, 1)

        @block.vector
        def _(dve):
            dve.wait_ge(s_c, 16 * NC)
            nc.vector.tensor_copy(upper[:, :], upper_f[:, :]).then_inc(s_cb, 1)
            nc.vector.memset(ones[:, :], 1.0).then_inc(s_cb, 1)
            dve.wait_ge(s_x, 16 * NBATCH)
            steps = Steps(dve, s_n, 2 * NTILE + 1, 0)
            for t in range(NTILE):
                steps.did(nc.vector.bn_stats(out=stats[:, t, :], in_=x[:, t, :]))
            steps.settled()
            for t in range(NTILE):
                steps.did(nc.vector.bn_aggr(out=mv[:, t, :], in_=stats[:, t, :]))
            steps.settled()
            steps.did(nc.vector.tensor_scalar(sd[:, :], mv[:, :, 1], EPS, None, ALU.add))
            steps.end()

            steps = Steps(dve, s_r, 21, 0)
            dve.wait_ge(s_aff, NBATCH)
            steps.did(nc.vector.tensor_copy(aff[:, :], bank[:, 0, 0:NTE]))
            steps.settled()
            nc.vector.tensor_reduce(out=best[:, :], in_=te(aff), axis=AX.X, op=ALU.max).then_inc(s_best, 1)
            dve.wait_ge(s_best, 1)
            per_tile = [P, NTILE, NE]
            revb = rev[:, :].unsqueeze(1).broadcast_to(per_tile)
            steps.did(nc.vector.tensor_tensor(out=te(eq), in0=te(aff), in1=best[:, :].unsqueeze(2).broadcast_to(per_tile), op=ALU.is_equal))
            steps.settled()
            steps.did(nc.vector.tensor_tensor(out=te(eq), in0=te(eq), in1=revb, op=ALU.mult))
            steps.settled()
            steps.did(nc.vector.tensor_reduce(out=pick[:, :], in_=te(eq), axis=AX.X, op=ALU.max))
            steps.settled()
            steps.did(nc.vector.tensor_tensor(out=te(own), in0=revb, in1=pick[:, :].unsqueeze(2).broadcast_to(per_tile), op=ALU.is_equal))
            steps.settled()
            nc.vector.tensor_copy(ownb[:, :], own[:, :]).then_inc(s_own, 1)
            dve.wait_ge(s_cnt, 1)
            steps.did(nc.vector.tensor_copy(et(count), bank[:, 2, 0:NTE].rearrange("p (t e) -> p e t", e=NE)))
            steps.settled()
            steps.did(nc.vector.tensor_tensor_scan(out=cum[:, :], data0=not_first[:, :], data1=count[:, :], initial=0.0,
                                                   op0=ALU.mult, op1=ALU.add))
            steps.settled()
            per_expert = [P, NE, NTILE]
            total = et(cum)[:, :, NTILE - 1:NTILE].broadcast_to(per_expert)
            steps.did(nc.vector.tensor_tensor(out=et(over), in0=total, in1=firsts[:, :].unsqueeze(1).broadcast_to(per_expert), op=ALU.is_gt))
            steps.settled()
            steps.did(nc.vector.tensor_reduce(out=tiles[:, :], in_=et(over), axis=AX.X, op=ALU.add))
            steps.settled()
            steps.did(nc.vector.tensor_tensor_scan(out=ends[:, :], data0=not_first[:, 1:1 + NE], data1=tiles[:, :], initial=0.0,
                                                   op0=ALU.mult, op1=ALU.add))
            steps.settled()
            steps.did(nc.vector.tensor_tensor(out=base[:, :], in0=ends[:, :], in1=tiles[:, :], op=ALU.subtract))
            steps.settled()
            steps.did(nc.vector.tensor_scalar(base[:, :], base[:, :], float(P), None, ALU.mult))
            steps.did(nc.vector.tensor_tensor(out=cum[:, :], in0=cum[:, :], in1=count[:, :], op=ALU.subtract))
            steps.settled()
            steps.did(nc.vector.tensor_tensor(out=te(pos), in0=bank[:, 1, 0:NTE].rearrange("p (t e) -> p t e", e=NE), in1=swapped(cum), op=ALU.add))
            steps.settled()
            steps.did(nc.vector.tensor_tensor(out=te(pos), in0=te(pos), in1=base[:, :].unsqueeze(1).broadcast_to(per_tile), op=ALU.add))
            steps.settled()
            steps.did(nc.vector.tensor_tensor(out=pos[:, :], in0=pos[:, :], in1=own[:, :], op=ALU.mult))
            steps.settled()
            steps.did(nc.vector.tensor_reduce(out=slot_f[:, :], in_=te(pos), axis=AX.X, op=ALU.add))
            steps.settled()
            nc.vector.tensor_copy(slot[:, :], slot_f[:, :]).then_inc(s_slot, 1)
            in_tile = [1, NSLOT, NE]
            pastv = past[:, :].rearrange("p (t e) -> p t e", e=NE)
            steps.did(nc.vector.tensor_tensor(out=pastv, in0=ends[0:1, :].unsqueeze(1).broadcast_to(in_tile),
                                              in1=numbers[0:1, :].unsqueeze(2).broadcast_to(in_tile), op=ALU.is_le))
            steps.settled()
            steps.did(nc.vector.tensor_reduce(out=eid_f[:, :], in_=pastv, axis=AX.X, op=ALU.add))
            steps.settled()
            steps.did(nc.vector.tensor_scalar(eid_f[:, :], eid_f[:, :], float(NE - 1), None, ALU.min))
            steps.settled()
            nc.vector.tensor_copy(eid[:, :], eid_f[:, :]).then_inc(s_eid, 1)
            dve.wait_ge(s_sd, 1)
            steps.did(nc.vector.reciprocal(rstd[:, :], sd[:, :]))
            steps.settled()
            for t in range(NTILE):
                nc.vector.tensor_scalar(xn[:, t, :], x[:, t, :], mv[:, t, 0:1], rstd[:, t:t + 1], ALU.subtract, ALU.mult).then_inc(s_xn, 1)
            steps.end()

            def gain_shift(j, turn, i):
                dve.wait_ge(s_wl[i], (16 * NWL) * turn + 16 * NWL)
                dve.wait_ge(s_t, j + 1)
                for c in range(DC):
                    ins = nc.vector.tensor_scalar(xsT[i][:, c, :], bank[:, 4 + i, c * P:(c + 1) * P], small[i][:, FC + c:FC + c + 1],
                                                  small[i][:, FC + DC + c:FC + DC + c + 1], ALU.mult, ALU.add)
                ins.then_inc(s_xg, 1)

            def tile(j, turn, i, last):
                dve.wait_ge(s_h, 2 * j + 2)
                for f in range(FC // 2, FC):
                    nc.vector.tensor_scalar(hid[i][:, f, :], bank[:, 2 * i + f // 4, (f % 4) * P:(f % 4 + 1) * P], small[i][:, f:f + 1],
                                            0.0, ALU.add, ALU.max).then_inc(s_rv, 1)
                if not last:
                    gain_shift(j + 1, turn + i, 1 - i)
                dve.wait_ge(s_o, j + 1)
                dve.wait_ge(s_yd[i], 16 * turn + 16)
                nc.vector.tensor_tensor(out=ys[i][:, :], in0=bank[:, 6 + i, 0:D], in1=b2[i][:, :], op=ALU.add).then_inc(s_ys, 1)

            gain_shift(0, 0, 0)
            slot_tiles(dve, tile)

            dve.wait_ge(s_alpha, 1)
            dve.wait_ge(s_x2, 1)
            steps = Steps(dve, s_f, NGR * (3 * GRP + 1), 0)
            for gr in range(NGR):
                mine = range(GRP * gr, GRP * (gr + 1))
                dve.wait_ge(s_g[gr], 16 * GRP)
                for t in mine:
                    steps.did(nc.vector.scalar_tensor_tensor(out=xn[:, t, :], in0=xn[:, t, :], scalar=alpha[:, t:t + 1], in1=x[:, t, :],
                                                             op0=ALU.mult, op1=ALU.add))
                steps.settled()
                for t in mine:
                    steps.did(nc.vector.bn_stats(out=stats[:, t, :], in_=xn[:, t, :]))
                steps.settled()
                for t in mine:
                    steps.did(nc.vector.bn_aggr(out=mv[:, t, :], in_=stats[:, t, :]))
                steps.settled()
                part = slice(GRP * gr, GRP * (gr + 1))
                steps.did(nc.vector.tensor_scalar(sd[:, part], mv[:, part, 1], EPS, None, ALU.add))
                dve.wait_ge(s_fsd, gr + 1)
                nc.vector.reciprocal(rstd[:, part], sd[:, part]).then_inc(s_frs, 1)
                dve.wait_ge(s_frs, gr + 1)
                for t in mine:
                    nc.vector.tensor_scalar(xn[:, t, :], xn[:, t, :], mv[:, t, 0:1], rstd[:, t:t + 1], ALU.subtract, ALU.mult).then_inc(s_fy, 1)
            steps.end()

        @block.tensor
        def _(pe):
            pe.wait_ge(s_c, 16 * NC)
            for b in range(NBATCH):
                pe.wait_ge(s_xt, 16 * (b + 1))
                for t in range(TT):
                    col = (TT * b + t) * NE
                    for kc in range(DC):
                        ins = nc.tensor.matmul(bank[:, 0, col:col + NE], xT[:, kc, t * P:(t + 1) * P], cT[:, kc, :],
                                               start=(kc == 0), stop=(kc == DC - 1))
                ins.then_inc(s_aff, 1)
            pe.wait_ge(s_cb, 2)
            pe.wait_ge(s_own, 1)
            nc.tensor.matmul(bank[:, 1, 0:NTE], upper[:, :], ownb[:, :], start=True, stop=True)
            nc.tensor.matmul(bank[:, 2, 0:NTE], ones[:, :], ownb[:, :], start=True, stop=True).then_inc(s_cnt, 1)

            def transpose_slots(j, turn, i):
                pe.wait_ge(s_xs[i], 16 * turn + 16)
                for c in range(DC):
                    ins = nc.tensor.transpose(bank[:, 4 + i, c * P:(c + 1) * P], xs[i][:, c * P:(c + 1) * P], ident[:, :])
                ins.then_inc(s_t, 1)

            def tile(j, turn, i, last):
                pe.wait_ge(s_xg, j + 1)
                pe.wait_ge(s_wl[i], (16 * NWL) * turn + 16 * NWL)
                for f in range(FC):
                    for kc in range(DC):
                        ins = nc.tensor.matmul(bank[:, 2 * i + f // 4, (f % 4) * P:(f % 4 + 1) * P], w1[i][:, kc, f * P:(f + 1) * P],
                                               xsT[i][:, kc, :], start=(kc == 0), stop=(kc == DC - 1))
                    if f % 4 == 3:
                        ins.then_inc(s_h, 1)
                if not last:
                    transpose_slots(j + 1, turn + i, 1 - i)
                for f in range(FC):
                    pe.wait_ge(s_ra if f < 4 else s_rv, (FC // 2) * j + f % 4 + 1)
                    ins = nc.tensor.matmul(bank[:, 6 + i, 0:D], hid[i][:, f, :], w2[i][:, f, :], start=(f == 0), stop=(f == FC - 1))
                ins.then_inc(s_o, 1)

            pe.wait_ge(s_slot, 1)
            transpose_slots(0, 0, 0)
            slot_tiles(pe, tile)


def build_program(nc, I, out):
    def scratch(name, shape):
        return nc.dram_tensor(name, shape, F32).ap()

    qk_d = scratch("qk_parts", [NBATCH, 4, D, T])
    ln_d = scratch("line_parts", [NBATCH, 4, NH * NL, T])
    score_d = scratch("router_scores", [NBATCH, T])
    x1 = scratch("x1", [NBATCH, T, D]); x1T = scratch("x1T", [NBATCH, D, T])
    x2 = scratch("x2", [NBATCH, T, D]); x2T = scratch("x2T", [NBATCH, D, T])
    x3 = scratch("x3", [NBATCH, T, D]); x3T = scratch("x3T", [NBATCH, D, T])
    attention(nc, 0, I, I["x"], I["xT"], x1, x1T, qk_d, ln_d)
    mixture_of_depths(nc, I, x1, x1T, x2, x2T, score_d)
    attention(nc, 1, I, x2, x2T, x3, x3T, qk_d, ln_d)
    sorted_d = scratch("sorted_tokens", [NSLOT * P, D]); result_d = scratch("slot_results", [NSLOT * P, D])
    experts(nc, I, x3, x3T, out, sorted_d, result_d)


def lay_out(inputs):
    a = {k: np.asarray(v) for k, v in inputs.items()}

    def cont(x):
        return np.ascontiguousarray(x)

    def by_strips(w):
        out = np.zeros((NH, 32, D), np.float32)
        out[:, 0:DH, :] = w.reshape(NH, DH, D)
        return out.reshape(NH * 32, D)

    def by_features(v):
        return v.reshape(NE, -1, P).transpose(0, 2, 1)

    small = cont(np.concatenate([by_features(a["L1_ffn_b1"]), by_features(a["L1_ffn_ln_g"]), by_features(a["L1_ffn_ln_b"])], axis=2))
    swap = np.arange(D) ^ 1
    r = np.arange(P)
    inv = 1.0 / 10000.0 ** (np.arange(0, DH, 2, dtype=np.float32) / DH)
    ang = np.outer(np.arange(T, dtype=np.float32), inv)
    cos = np.cos(ang).astype(np.float32).T[(r % DH) // 2]
    sin = np.sin(ang).astype(np.float32).T[(r % DH) // 2]
    sin = np.where((r % 2 == 0)[:, None], -sin, sin)
    k, q = np.meshgrid(np.arange(P), np.arange(P), indexing="ij")
    big = np.float32(-3e38)
    return {
        "x": cont(a["L0_attn_x"]), "xT": cont(a["L0_attn_x"].transpose(0, 2, 1)),
        "L0_wq": cont(a["L0_attn_wq"]), "L0_wqs": cont(a["L0_attn_wq"][:, swap]), "L0_wd": cont(a["L0_attn_w_down"]),
        "L0_wk": cont(a["L0_attn_wk_up"]), "L0_wks": cont(a["L0_attn_wk_up"][:, swap]), "L0_wv": cont(a["L0_attn_wv_up"]),
        "L0_wo": by_strips(a["L0_attn_wo"]),
        "L1_wqkv": cont(a["L1_attn_Wqkv"]), "L1_bqk": cont(a["L1_attn_bqkv"][0:2 * D].reshape(4, P).T), "L1_bv": cont(a["L1_attn_bqkv"][2 * D:]),
        "L1_w12": cont(np.concatenate([a["L1_attn_W1p"], a["L1_attn_W2p"]], axis=1)),
        "L1_pscale": cont(a["L1_attn_plucker_scale"]), "L1_wo": by_strips(a["L1_attn_Wout"]), "L1_bout": cont(a["L1_attn_bout"]),
        "m_wr": cont(a["L0_ffn_w_router"]), "m_w1": cont(a["L0_ffn_W1"]), "m_b1T": cont(a["L0_ffn_b1"].reshape(FC, P).T),
        "m_w2": cont(a["L0_ffn_W2"]), "m_b2": cont(a["L0_ffn_b2"]),
        "e_cT": cont(a["L1_ffn_centroids"].T), "e_small": small,
        "e_w1T": cont(a["L1_ffn_w1"].transpose(0, 2, 1)), 
        "e_w2T": cont(a["L1_ffn_w2"].transpose(0, 2, 1)), "e_b2": cont(a["L1_ffn_b2"]),
        "rope": np.stack([cos, sin]).astype(np.float32),
        "before": np.concatenate([np.ones((P, T - P), np.float32), (q < k).astype(np.float32)], axis=1),
        "upper": (k < q).astype(np.float32),
        "rev": np.tile(NE - np.arange(NE, dtype=np.float32), (P, 1)),
        "not_first": np.tile((np.arange(NTILE * NE) % NTILE != 0).astype(np.float32), (P, 1)),
        "firsts": np.tile(P * np.arange(NTILE, dtype=np.float32), (P, 1)),
        "numbers": np.tile(np.arange(NSLOT, dtype=np.float32), (P, 1)),
        "ident": np.eye(P, dtype=np.float32),
        "sel": (k == 32 * (q // 32) + DH).astype(np.float32),
        "maskT0": np.where((k >= 64) & (q < 64), big, np.float32(0)).astype(np.float32),
        "maskT1": np.where(k > q, big, np.float32(0)).astype(np.float32),
        "jsign": np.tile(np.array([1, -1, 1, 1, -1, 1], np.float32), (P, 1)),
    }


def kernel(**inputs):
    import concourse.bacc as bacc
    from concourse.bass_utils import run_bass_kernel_spmd

    nc = bacc.Bacc("TRN2", target_bir_lowering=False, num_devices=1)
    arrays = lay_out(inputs)
    aps = {name: nc.dram_tensor(name, list(a.shape), mybir.dt.from_np(a.dtype), kind="ExternalInput").ap() for name, a in arrays.items()}
    out = nc.dram_tensor("out", [NBATCH, T, D], F32, kind="ExternalOutput").ap()
    build_program(nc, aps, out)
    r = run_bass_kernel_spmd(nc, [arrays], core_ids=[0])
    return r.results[0]["out"]
```

```python
import concourse.bass as bass
from concourse import mybir
from contextlib import ExitStack
import numpy as np

F32 = mybir.dt.float32
F32R = mybir.dt.float32r
BF16 = mybir.dt.bfloat16
I32 = mybir.dt.int32
ALU = mybir.AluOpType
ACT = mybir.ActivationFunctionType
AX = mybir.AxisListType

P = 128
NBATCH, T, D = 4, 1024, 256
NH = 16
DH = D // NH
DC = D // P
TT = T // P
BLK = 512
NBLK = T // BLK
HG = 4
NG = NH // HG
FF = 1024
FC = FF // P
NE = 8
NTOK = NBATCH * T
NTILE = NTOK // P
SUB = 2
TS = SUB * P
NSLOT = (NTOK + NE * (TS - 1)) // TS
TOPK = T // 2
EPS = 1e-5

LROW = 64
NL = 6
SHROW = 94
KFULL = 96


class Stage:

    def __init__(self, nc, tag):
        self.nc, self.tag, self.ctx, self.sems = nc, tag, ExitStack(), []

    def __enter__(self):
        self.ctx.__enter__()
        return self

    def __exit__(self, *a):
        done = self.ctx.__exit__(*a)
        self.nc.clear_and_free_semaphores(self.sems)
        self.nc.all_engine_barrier()
        return done

    def sb(self, name, shape, dt=F32):
        return self.ctx.enter_context(self.nc.sbuf_tensor(f"{self.tag}_{name}", shape, dt))

    def ps(self, name, shape, dt=F32):
        return self.ctx.enter_context(self.nc.psum_tensor(f"{self.tag}_{name}", shape, dt))

    def sem(self, name):
        self.sems.append(self.nc.alloc_semaphore(f"{self.tag}_{name}"))
        return self.sems[-1]

    def block(self):
        return self.ctx.enter_context(self.nc.Block())


def hold(eng, sem, value, passed):
    eng.wait_ge(sem, value)
    eng.sem_inc(passed, 1)


class Steps:

    def __init__(self, eng, sem, per, b):
        self.eng, self.sem, self.per, self.b, self.n = eng, sem, per, b, 0

    def did(self, ins):
        self.n += 1
        ins.then_inc(self.sem, 1)

    def settled(self, passed=None):
        if passed is not None:
            hold(self.eng, self.sem, self.b * self.per + self.n, passed)
        else:
            self.eng.wait_ge(self.sem, self.b * self.per + self.n)

    def end(self):
        assert self.n == self.per, f"{self.n} steps, not {self.per}"


def proj_jobs(layer):
    jobs = []
    if layer == 0:
        for n in range(NBLK):
            jobs.append(("lat", n, 0, "act"))
        for c in range(DC):
            for kind in ("q", "k"):
                for n in range(NBLK):
                    jobs += [(kind, n, c, "dve"), (kind + "_swapped", n, c, "dve")]
        for t in range(TT):
            jobs.append(("v", t, 0, "act"))
    else:
        for h in range(2):
            jobs.append(("points", h, 0, "act"))
        for c in range(DC):
            for kind in ("q", "k"):
                for n in range(NBLK):
                    jobs.append((kind, n, c, "piece"))
        for t in range(TT):
            jobs.append(("v", t, 0, "dve"))
        for w in range(2):
            for h in range(2):
                jobs.append(("lines", w, h, "dve"))
    return jobs


def ring_jobs():
    def maxima(g):
        return [("max", g, j, qt, c) for j in range(HG) for qt in range(TT) for c in range(1 + (qt >= 4))]
    first = maxima(0) + [("shift", 0)]
    at = [[] for s in range(12 * NG)]
    s = 0
    for g in range(1, NG):
        todo = maxima(g)
        per = 6 if g == 1 else 4
        while todo:
            at[s] += todo[:per]
            todo = todo[per:]
            s += 1
        at[s].append(("shift", g))
    for g in range(NG):
        at[12 * g + 6].insert(1, ("sums", 2 * g))
        at[12 * g + 8].insert(2, ("spread", 2 * g))
        if g:
            at[12 * g + 2].insert(1, ("sums", 2 * g - 1))
            at[12 * g + 4].insert(1, ("spread", 2 * g - 1))
    last = [("sums", 2 * NG - 1), ("spread", 2 * NG - 1)]
    order = first + [x for jobs in at for x in jobs] + last
    banks = [r % 8 if r < len(first) else 6 + r % 2 for r in range(len(order))]
    before = [max([i for i in range(r) if banks[i] == banks[r]], default=None) for r in range(len(order))]
    return first, at, last, order, banks, before


def attention(nc, layer, W, x_in, x_out, qk_d, ln_d):
    with Stage(nc, f"at{layer}") as S:
        jobs = proj_jobs(layer)
        NPJ = len(jobs)
        NPJ_ACT = sum(j[3] == "act" for j in jobs)
        NPJ_DVE = sum(j[3] == "dve" for j in jobs)
        first, at, last, order, ring_bank, bank_before = ring_jobs()
        NR = len(order)
        NSTEP = 12 * NG
        NPAIR = 2 * NSTEP
        NU = 2 * NG
        NNAT = 2 * NBLK * DC

        if layer == 0:
            wq = S.sb("wq", [P, DC, D]); wqs = S.sb("wqs", [P, DC, D])
            wd = S.sb("wd", [P, DC, P]); wk = S.sb("wk", [P, D]); wks = S.sb("wks", [P, D]); wv = S.sb("wv", [P, D])
            rope = S.sb("rope", [P, 2, T])
        else:
            wqkv = S.sb("wqkv", [P, DC, 3 * D]); w12 = S.sb("w12", [P, DC, P])
            bqk = S.sb("bqk", [P, 4]); bv = S.sb("bv", [P, D]); bo = S.sb("bo", [P, D])
            jscale = S.sb("jscale", [P, NH, NL]); scale16 = S.sb("scale16", [P, NH]); jsign = S.sb("jsign", [P, NL])
        wo = S.sb("wo", [P, NG, D])
        sel = S.sb("sel", [P, HG]); ident = S.sb("ident", [P, P])
        identb = S.sb("identb", [P, P], BF16); maskT = S.sb("maskT", [P, P], BF16); maskf = S.sb("maskf", [P, P])
        xin = S.sb("xin", [P, TT, D])
        xT = S.sb("xT", [P, DC, T])
        xr = S.sb("xr", [P, TT, D])
        nat_all = S.sb("nat", [P, 2 * HG * T], F32R)
        nat = nat_all[:, :].rearrange("p (m c t) -> p m c t", m=4, c=DC)
        qst = [S.sb(f"qst{i}", [KFULL, HG, T], F32R) for i in range(2)]
        kst = [S.sb(f"kst{i}", [KFULL, HG, T], F32R) for i in range(2)]
        qst.append(nat_all[0:KFULL, 0:HG * T].rearrange("p (j t) -> p j t", j=HG))
        kst.append(nat_all[0:KFULL, HG * T:2 * HG * T].rearrange("p (j t) -> p j t", j=HG))
        vaug = S.sb("vaug", [P, TT, NH, 32])
        work = S.sb("work", [P, 4 * 1024])
        probs = work[:, :].rearrange("p (s j t) -> p s j t", s=4, j=2)
        o_sb = S.sb("o_sb", [P, 2, BLK])
        rec = S.sb("rec", [P, 4 * HG]); rec_wide = S.sb("rec_wide", [P, BLK])
        oT = S.sb("oT", [P, NG, T])
        mx = S.sb("mx", [P, 2, HG, TT]); mx2 = S.sb("mx2", [P, 2, HG, 4])
        sh = S.sb("sh", [32, 2, P], F32R)
        stats = S.sb("stats", [P, TT, 6]); mv = S.sb("mv", [P, TT, 2]); sd = S.sb("sd", [P, TT]); rstd = S.sb("rstd", [P, TT])
        if layer == 0:
            rt = work[:, 0:3072].rearrange("p (k s t) -> p k s t", k=3, s=2)
            lat = work[:, 3072:4096]
        else:
            rt = work[:, 0:1024].rearrange("p (k s t) -> p k s t", k=1, s=2)
            p1 = work[:, 1024:1536]; p2 = work[:, 1536:2048]
            la = work[:, 2048:2816]; lb = work[:, 2816:3584]
            nat_l = oT[0:96, :, :].bitcast(F32R)
            ln2 = S.sb("ln2", [P, P]); lrn = S.sb("lrn", [P, P])
        bank = S.ps("bank", [P, 8, BLK])
        scores = [bank[:, 0:2, :], bank[:, 2:4, :]]
        PV0, RING0 = 4, 6

        s_w = S.sem("weights_loaded"); s_init = S.sem("constants_set"); s_js = S.sem("line_scales_set"); s_cast = S.sem("masks_cast")
        s_xin = S.sem("next_tokens_loaded"); s_tr = S.sem("tokens_transposed"); s_te = S.sem("features_ready")
        s_xr = S.sem("tokens_loaded"); s_bo = S.sem("bias_added")
        s_pj = S.sem("projection_ready"); s_pa = S.sem("bank_emptied_by_act"); s_pd = S.sem("bank_emptied_by_dve")
        s_full = S.sem("piece_ready"); s_hi = S.sem("piece_high_ready"); s_nat = S.sem("piece_split"); s_lh = S.sem("line_high_ready")
        s_lv = S.sem("line_steps"); s_lq = S.sem("lines_ready"); s_sq = S.sem("norms_rooted")
        s_qkd = S.sem("qk_stored"); s_lnd = S.sem("lines_stored"); s_third = S.sem("third_stacks_set")
        s_stk = [S.sem(f"stack_loaded{i}") for i in range(NG)]
        s_sh = S.sem("shift_ready"); s_shl = S.sem("shift_loaded")
        s_ring = S.sem("ring_filled"); s_rd = S.sem("ring_emptied"); s_cb = S.sem("maxima_ready"); s_rec = S.sem("reciprocal_steps")
        s_st = S.sem("scores_ready"); s_ex = S.sem("probs_ready"); s_pv = S.sem("values_added"); s_ov = S.sem("output_copied")
        s_wo = S.sem("out_projected"); s_z = S.sem("ln_steps"); s_sd = S.sem("deviation_ready"); s_rs = S.sem("rstd_ready")
        s_y = S.sem("result_ready"); s_out = S.sem("result_stored")
        s_passed = S.sem("waits_passed"); s_passed_pool = S.sem("pool_waits_passed"); s_passed_dve = S.sem("dve_waits_passed")
        block = S.block()

        def full_piece(i):
            return rt[:, 2 if layer == 0 else 0, i % 2, :]

        NW = 8
        NWALL = NW + 3
        SCALE = float(DH) ** -0.5
        NLND = 2 if layer == 1 else 0
        NSTK = 8 if layer == 0 else 16
        NLINE = 17

        @block.sync
        def _(sp):
            def load_weights():
                if layer == 0:
                    pairs = [(wq, W["L0_wq"].rearrange("(c p) n -> p c n", p=P)), (wqs, W["L0_wqs"].rearrange("(c p) n -> p c n", p=P)),
                             (wd, W["L0_wd"].rearrange("(c p) n -> p c n", p=P)), (wk, W["L0_wk"]), (wks, W["L0_wks"]),
                             (wv, W["L0_wv"]), (rope, W["rope"].rearrange("k p t -> p k t")),
                             (wo, W["L0_wo"].rearrange("(c p) n -> p c n", p=P))]
                else:
                    pairs = [(wqkv, W["L1_wqkv"].rearrange("(c p) n -> p c n", p=P)), (w12, W["L1_w12"].rearrange("(c p) n -> p c n", p=P)),
                             (bqk, W["L1_bqk"]),
                             (bv, W["L1_bv"].partition_broadcast(P)), (bo, W["L1_bout"].partition_broadcast(P)),
                             (scale16, W["L1_pscale"].partition_broadcast(P)), (jsign, W["jsign"]),
                             (wo, W["L1_wo"].rearrange("(c p) n -> p c n", p=P))]
                assert len(pairs) == NW
                for dst, src in pairs:
                    dst = dst[:, :, :] if len(dst.shape) == 3 else dst[:, :]
                    sp.dma_start(dst, src).then_inc(s_w, 16)
                sp.dma_start(ident[:, :], W["ident"]).then_inc(s_w, 16)
                sp.dma_start(sel[:, :], W["sel"]).then_inc(s_w, 16)
                sp.dma_start(maskf[:, :], W[f"maskT{layer}"]).then_inc(s_w, 16)

            load_weights()
            sp.wait_ge(s_init, 6)
            with sp.Fori(0, NBATCH) as b:
                sp.dma_start(xr[:, :, :], x_in[b].rearrange("(n p) d -> p n d", p=P)).then_inc(s_xr, 16)

                def store_pieces(i):
                    c, m = i // 2, 2 * (i % 2)
                    sp.wait_ge(s_nat, b * NNAT + (i + 1) * NBLK)
                    dst = qk_d[b, m:m + 2, c * P:(c + 1) * P, :].rearrange("m p t -> p m t")
                    sp.dma_start(dst, nat[:, m:m + 2, c, :].bitcast(F32)).then_inc(s_qkd, 16)

                def load_stacks(g):
                    q, k, sem = qst[g % 3], kst[g % 3], s_stk[g]
                    for r, (mq, mk) in enumerate(((0, 2), (0, 3), (1, 2), (1, 3))):
                        for dst, m in ((q, mq), (k, mk)):
                            src = qk_d[b, m, 64 * g:64 * g + 64, :].rearrange("(j p) t -> p j t", j=HG)
                            sp.dma_start(dst[16 * r:16 * r + 16, :, :].bitcast(F32), src).then_inc(sem, 16)
                            if layer == 1:
                                src = ln_d[b, m, 24 * g:24 * g + 24, :].rearrange("(j p) t -> p j t", j=HG)
                                r0 = LROW + NL * r
                                sp.dma_start(dst[r0:r0 + NL, :, :].bitcast(F32), src).then_inc(sem, 16)

                def load_shift(g):
                    sp.wait_ge(s_rd, b * NR + order.index(("shift", g)) + 1)
                    for m in range(2):
                        dst = qst[g % 3][SHROW + m:SHROW + m + 1, :, :].bitcast(F32).rearrange("o j (n t) -> o (j n) t", t=P)
                        sp.dma_start(dst, sh[:, m, :].bitcast(F32)).then_inc(s_shl, 16)

                store_pieces(0)
                store_pieces(1)
                if layer == 0:
                    sp.wait_ge(s_qkd, b * 64 + 32)
                    load_stacks(0)
                store_pieces(2)
                store_pieces(3)
                if layer == 1:
                    for w in range(2):
                        sp.wait_ge(s_pd, b * NPJ_DVE + TT + 2 * w + 2)
                        dst = ln_d[b, 2 * w:2 * w + 2].rearrange("m p t -> p m t")
                        sp.dma_start(dst, nat_l[:, 2 * w:2 * w + 2, :].bitcast(F32)).then_inc(s_lnd, 16)
                    sp.wait_ge(s_qkd, b * 64 + 64)
                    sp.wait_ge(s_lnd, b * 32 + 32)
                    load_stacks(0)
                load_stacks(1)
                if layer == 0:
                    sp.wait_ge(s_qkd, b * 64 + 64)
                sp.wait_ge(s_third, b * 2 + 2)
                load_stacks(2)
                load_shift(0)
                load_shift(1)
                sp.wait_ge(s_st, b * NPAIR + 24)
                load_stacks(3)
                load_shift(2)
                load_shift(3)
                sp.wait_ge(s_y, b * TT + TT)
                sp.dma_start(x_out[b].rearrange("(n p) d -> p n d", p=P), xr[:, :, :]).then_inc(s_out, 16)
                hold(sp, s_out, b * 16 + 16, s_passed)

        @block.gpsimd
        def _(pool):
            for i in range(2):
                nc.gpsimd.memset(qst[i][LROW:KFULL, :, :].bitcast(F32), 0.0).then_inc(s_init, 1)
                nc.gpsimd.memset(kst[i][LROW:KFULL, :, :].bitcast(F32), -1.0).then_inc(s_init, 1)
            pool.wait_ge(s_init, 4)
            nc.gpsimd.memset(vaug[:, :, :, 16:32], 0.0).then_inc(s_init, 1)
            pool.wait_ge(s_init, 5)
            nc.gpsimd.memset(vaug[:, :, :, 16:17], 1.0).then_inc(s_init, 1)

            def load_tokens(b):
                pool.dma_start(xin[:, :, :], x_in[b].rearrange("(n p) d -> p n d", p=P)).then_inc(s_xin, 16)

            def batch(b, following):
                hold(pool, s_tr, b * 4 + 4, s_passed_pool)
                load_tokens(following)
                i = 0
                for c in range(DC):
                    for m in (0, 2):
                        for n in range(NBLK):
                            pool.wait_ge(s_hi, b * NNAT + i + 1)
                            nc.gpsimd.tensor_tensor(out=nat[:, m + 1, c, n * BLK:(n + 1) * BLK], in0=full_piece(i),
                                                    in1=nat[:, m, c, n * BLK:(n + 1) * BLK].bitcast(F32), op=ALU.subtract).then_inc(s_nat, 1)
                            i += 1
                hold(pool, s_qkd, b * 64 + 64, s_passed_pool)
                nc.gpsimd.memset(qst[2][LROW:KFULL, :, :].bitcast(F32), 0.0).then_inc(s_third, 1)
                nc.gpsimd.memset(kst[2][LROW:KFULL, :, :].bitcast(F32), -1.0).then_inc(s_third, 1)
                if layer == 1:
                    hold(pool, s_third, b * 2 + 2, s_passed_pool)
                    pool.wait_ge(s_w, 16 * NWALL)
                    pool.wait_ge(s_xr, b * 16 + 16)
                    for t in range(TT):
                        nc.gpsimd.tensor_tensor(out=xr[:, t, :], in0=xr[:, t, :], in1=bo[:, :], op=ALU.add).then_inc(s_bo, 1)

            load_tokens(0)
            with pool.Fori(0, NBATCH - 1) as b:
                batch(b, b + 1)
            batch(NBATCH - 1, 0)
            pool.wait_ge(s_xin, 16 * (NBATCH + 1))

        @block.scalar
        def _(act):
            def copy_features(b):
                for k in range(4):
                    act.wait_ge(s_tr, b * 4 + k + 1)
                    nc.scalar.copy(xT[:, k // 2, (k % 2) * BLK:(k % 2 + 1) * BLK], bank[:, k, :]).then_inc(s_te, 1)

            copy_features(0)
            act.wait_ge(s_w, 16 * NWALL)
            act.wait_ge(s_init, 6)
            with act.Fori(0, NBATCH) as b:
                na = piece = 0

                def split_high(i):
                    c, m, n = i // 4, 2 * (i // 2 % 2), i % 2
                    act.wait_ge(s_full, b * NNAT + i + 1)
                    nc.scalar.copy(nat[:, m, c, n * BLK:(n + 1) * BLK], full_piece(i)).then_inc(s_hi, 1)

                for r, (kind, i0, i1, eng) in enumerate(jobs):
                    if layer == 0 and kind.endswith("swapped"):
                        split_high(piece)
                        piece += 1
                    if eng == "dve":
                        continue
                    act.wait_ge(s_pj, b * NPJ + r + 1)
                    src = bank[:, r % 4, :]
                    if kind == "lat":
                        nc.scalar.copy(lat[:, i0 * BLK:(i0 + 1) * BLK], src).then_inc(s_pa, 1)
                    elif kind == "v":
                        nc.scalar.copy(vaug[:, i0, :, 0:DH], src[:, 0:D].rearrange("p (h d) -> p h d", d=DH)).then_inc(s_pa, 1)
                    elif kind == "points":
                        s4 = src.rearrange("p (n w h) -> p n w h", n=4, w=2)
                        for w, dst in enumerate((p1, p2)):
                            ins = nc.scalar.copy(dst[:, i0 * 256:(i0 + 1) * 256].rearrange("p (n h) -> p n h", n=4), s4[:, :, w, :])
                        ins.then_inc(s_pa, 1)
                    else:
                        if piece >= 2:
                            act.wait_ge(s_nat, b * NNAT + piece - 1)
                        col = i1 + (2 if kind == "k" else 0)
                        nc.scalar.activation(full_piece(piece), src, ACT.Identity, bias=bqk[:, col:col + 1]).then_inc(s_full, 1)
                        split_high(piece)
                        piece += 1
                    na += eng == "act"
                assert na == NPJ_ACT
                if layer == 1:
                    act.wait_ge(s_lv, b * NLINE + 9)
                    nc.scalar.activation(lrn[:, :], ln2[:, :], ACT.Sqrt).then_inc(s_sq, 1)

                def copy_output(u):
                    act.wait_ge(s_pv, b * NSTEP + (u // 2) * 12 + (12 if u % 2 else 4))
                    if u >= 2:
                        act.wait_ge(s_rd, b * NR + order.index(("spread", u - 2)) + 1)
                    nc.scalar.copy(o_sb[:, u % 2, :], bank[:, PV0 + u % 2, :]).then_inc(s_ov, 1)

                for s in range(NSTEP):
                    i = s % 12
                    off = P * (i if i < 4 else max(0, i - 8))
                    for p in range(2):
                        e = 2 * s + p
                        act.wait_ge(s_st, b * NPAIR + e + 1)
                        if s >= 2:
                            act.wait_ge(s_pv, b * NSTEP + s - 1)
                        nc.scalar.activation(probs[:, e % 4, :, off:], scores[e % 2][:, :, off:], ACT.Exp, scale=SCALE).then_inc(s_ex, 1)
                    if i == 5:
                        copy_output(2 * (s // 12))
                    if i == 1 and s > 12:
                        copy_output(2 * (s // 12) - 1)
                copy_output(NU - 1)
                copy_features(b + 1)
                act.wait_ge(s_z, b * (3 * TT + 1) + 3 * TT + 1)
                nc.scalar.activation(sd[:, :], sd[:, :], ACT.Sqrt).then_inc(s_sd, 1)

        @block.vector
        def _(dve):
            dve.wait_ge(s_w, 16 * NWALL)
            dve.wait_ge(s_init, 6)
            nc.vector.tensor_copy(identb[:, :], ident[:, :]).then_inc(s_cast, 1)
            nc.vector.tensor_copy(maskT[:, :], maskf[:, :]).then_inc(s_cast, 1)
            if layer == 1:
                for c in range(NL):
                    ins = nc.vector.tensor_scalar(jscale[:, :, c], scale16[:, :], jsign[:, c:c + 1], 1.0 / SCALE, ALU.mult, ALU.mult)
                ins.then_inc(s_js, 1)
                dve.wait_ge(s_js, 1)
            with dve.Fori(0, NBATCH) as b:
                piece = 0
                nd = 0

                def lines():
                    steps = Steps(dve, s_lv, NLINE, b)
                    dve.wait_ge(s_pa, b * NPJ_ACT + 2)
                    q1 = p1.rearrange("p (n c) -> p n c", c=4)
                    q2 = p2.rearrange("p (n c) -> p n c", c=4)
                    a = la.rearrange("p (n c) -> p n c", c=NL)
                    bb = lb.rearrange("p (n c) -> p n c", c=NL)
                    at_ = 0
                    for i, k in ((0, 3), (1, 2), (2, 1)):
                        for dst, x, y in ((a, q1, q2), (bb, q2, q1)):
                            one = x[:, :, i:i + 1] if k == 1 else x[:, :, i:i + 1].broadcast_to([P, P, k])
                            steps.did(nc.vector.tensor_tensor(out=dst[:, :, at_:at_ + k], in0=one, in1=y[:, :, i + 1:4], op=ALU.mult))
                        at_ += k
                    steps.settled()
                    steps.did(nc.vector.tensor_tensor(out=la, in0=la, in1=lb, op=ALU.subtract))
                    steps.settled()
                    steps.did(nc.vector.tensor_tensor(out=lb, in0=la, in1=la, op=ALU.mult))
                    steps.settled()
                    steps.did(nc.vector.tensor_reduce(out=ln2[:, :], in_=bb, axis=AX.X, op=ALU.add))
                    dve.wait_ge(s_sq, b + 1)
                    steps.did(nc.vector.tensor_scalar(lrn[:, :], lrn[:, :], 1e-12, None, ALU.max))
                    steps.settled()
                    steps.did(nc.vector.reciprocal(ln2[:, :], lrn[:, :]))
                    steps.settled()
                    steps.did(nc.vector.tensor_tensor(out=a, in0=a, in1=ln2[:, :].unsqueeze(2).broadcast_to([P, P, NL]), op=ALU.mult))
                    steps.settled()
                    a4 = la.rearrange("p (n h c) -> p n h c", h=NH, c=NL)
                    b4 = lb.rearrange("p (n h c) -> p n h c", h=NH, c=NL)
                    js = jscale[:, :, :]
                    for c in range(NL - 1):
                        steps.did(nc.vector.tensor_tensor(out=b4[:, :, :, c], in0=a4[:, :, :, NL - 1 - c],
                                                          in1=js[:, :, c].unsqueeze(1).broadcast_to([P, TT, NH]), op=ALU.mult))
                    c = NL - 1
                    nc.vector.tensor_tensor(out=b4[:, :, :, c], in0=a4[:, :, :, NL - 1 - c],
                                            in1=js[:, :, c].unsqueeze(1).broadcast_to([P, TT, NH]), op=ALU.mult).then_inc(s_lq, 1)
                    steps.end()

                for r, (kind, i0, i1, eng) in enumerate(jobs):
                    if eng != "dve":
                        continue
                    if layer == 1 and nd == 0:
                        lines()
                    dve.wait_ge(s_pj, b * NPJ + r + 1)
                    src = bank[:, r % 4, :]
                    if kind in ("q", "k", "q_swapped", "k_swapped"):
                        w = int(kind.endswith("swapped"))
                        nc.vector.tensor_tensor(out=rt[:, w, piece % 2, :], in0=src, in1=rope[:, w, i0 * BLK:(i0 + 1) * BLK],
                                                op=ALU.mult).then_inc(s_pd, 1)
                        if w:
                            if piece >= 2:
                                dve.wait_ge(s_nat, b * NNAT + piece - 1)
                            dve.wait_ge(s_pd, b * NPJ_DVE + nd + 1)
                            nc.vector.tensor_tensor(out=full_piece(piece), in0=rt[:, 0, piece % 2, :], in1=rt[:, 1, piece % 2, :],
                                                    op=ALU.add).then_inc(s_full, 1)
                            piece += 1
                    elif kind == "v":
                        nc.vector.tensor_tensor(out=vaug[:, i0, :, 0:DH], in0=src[:, 0:D].rearrange("p (h d) -> p h d", d=DH),
                                                in1=bv[:, :].rearrange("p (h d) -> p h d", d=DH), op=ALU.add).then_inc(s_pd, 1)
                    else:
                        high = nat_l[:, 2 * i0, i1 * BLK:(i1 + 1) * BLK]
                        nc.vector.tensor_copy(high, src[0:96, :]).then_inc(s_lh, 1)
                        dve.wait_ge(s_lh, b * 4 + 2 * i0 + i1 + 1)
                        nc.vector.tensor_tensor(out=nat_l[:, 2 * i0 + 1, i1 * BLK:(i1 + 1) * BLK], in0=src[0:96, :], in1=high.bitcast(F32),
                                                op=ALU.subtract).then_inc(s_pd, 1)
                    nd += 1
                assert nd == NPJ_DVE

                for r, job in enumerate(order):
                    src = bank[:, ring_bank[r], :]
                    if job[0] == "max":
                        _, g, j, qt, c = job
                        dve.wait_ge(s_ring, b * NR + r + 1)
                        w = BLK if (qt >= 4 and c == 0) else P * (qt % 4 + 1)
                        dst = mx2[:, g % 2, j, qt - 4:qt - 3] if c else mx[:, g % 2, j, qt:qt + 1]
                        nc.vector.tensor_reduce(out=dst, in_=src[:, 0:w], axis=AX.X, op=ALU.max).then_inc(s_rd, 1)
                    elif job[0] == "shift":
                        g = job[1]
                        dve.wait_ge(s_rd, b * NR + r)
                        nc.vector.tensor_tensor(out=mx[:, g % 2, :, 4:8], in0=mx[:, g % 2, :, 4:8], in1=mx2[:, g % 2, :, :],
                                                op=ALU.max).then_inc(s_cb, 1)
                        dve.wait_ge(s_ring, b * NR + r + 1)
                        if g:
                            dve.wait_ge(s_shl, (b * NG + g) * 32)
                        nc.vector.tensor_copy(sh[:, 0, :], src[0:32, 0:P]).then_inc(s_sh, 1)
                        dve.wait_ge(s_sh, b * NG + g + 1)
                        nc.vector.tensor_tensor(out=sh[:, 1, :], in0=src[0:32, 0:P], in1=sh[:, 0, :].bitcast(F32), op=ALU.subtract).then_inc(s_rd, 1)
                    elif job[0] == "sums":
                        u = job[1]
                        dve.wait_ge(s_ring, b * NR + r + 1)
                        nc.vector.reciprocal(rec[:, :], src[:, 0:4 * HG]).then_inc(s_rec, 1)
                        dve.wait_ge(s_rec, (b * NU + u) * 2 + 1)
                        nc.vector.tensor_copy(rec_wide[:, :].rearrange("p (n k) -> p n k", k=32),
                                              rec[:, :].unsqueeze(2).broadcast_to([P, 4 * HG, 32])).then_inc(s_rec, 1)
                        dve.wait_ge(s_rec, (b * NU + u) * 2 + 2)
                        dve.sem_inc(s_rd, 1)
                    else:
                        u = job[1]
                        if layer == 1 and u == 0:
                            hold(dve, s_lnd, b * 32 + 32, s_passed_dve)
                        dve.wait_ge(s_ring, b * NR + r + 1)
                        nc.vector.tensor_tensor(out=oT[:, u // 2, (u % 2) * BLK:(u % 2 + 1) * BLK], in0=o_sb[:, u % 2, :],
                                                in1=src, op=ALU.mult).then_inc(s_rd, 1)

                steps = Steps(dve, s_z, 3 * TT + 1, b)
                if layer == 0:
                    dve.wait_ge(s_xr, b * 16 + 16)
                else:
                    dve.wait_ge(s_bo, b * TT + TT)
                for t in range(TT):
                    dve.wait_ge(s_wo, b * TT + t + 1)
                    steps.did(nc.vector.tensor_tensor(out=xr[:, t, :], in0=bank[:, 4 + t % 4, 0:D], in1=xr[:, t, :], op=ALU.add))
                steps.settled()
                for t in range(TT):
                    steps.did(nc.vector.bn_stats(out=stats[:, t, :], in_=xr[:, t, :]))
                steps.settled(s_passed)
                for t in range(TT):
                    steps.did(nc.vector.bn_aggr(out=mv[:, t, :], in_=stats[:, t, :]))
                steps.settled()
                steps.did(nc.vector.tensor_scalar(sd[:, :], mv[:, :, 1], EPS, None, ALU.add))
                steps.end()
                dve.wait_ge(s_sd, b + 1)
                nc.vector.reciprocal(rstd[:, :], sd[:, :]).then_inc(s_rs, 1)
                dve.wait_ge(s_rs, b + 1)
                for t in range(TT):
                    nc.vector.tensor_scalar(xr[:, t, :], xr[:, t, :], mv[:, t, 0:1], rstd[:, t:t + 1], ALU.subtract, ALU.mult).then_inc(s_y, 1)
                dve.wait_ge(s_shl, b * (32 * NG) + 32 * NG)

        @block.tensor
        def _(pe):
            pe.wait_ge(s_w, 16 * NWALL)
            pe.wait_ge(s_cast, 2)
            pe.wait_ge(s_init, 6)

            def transpose_tokens(b):
                pe.wait_ge(s_xin, b * 16 + 16)
                for k in range(4):
                    for n in range(4):
                        t = 4 * (k % 2) + n
                        ins = nc.tensor.transpose(bank[:, k, n * P:(n + 1) * P], xin[:, t, (k // 2) * P:(k // 2 + 1) * P], ident[:, :])
                    ins.then_inc(s_tr, 1)

            transpose_tokens(0)
            with pe.Fori(0, NBATCH) as b:
                emptied = {"act": 0, "dve": 0, "piece": 0}
                users = []

                def all_k(out, pairs):
                    for n, (lhsT, rhs) in enumerate(pairs):
                        ins = nc.tensor.matmul(out, lhsT, rhs, start=(n == 0), stop=(n == len(pairs) - 1))
                    return ins

                pe.wait_ge(s_te, b * 4 + 4)
                lat_done = {}
                for r, (kind, i0, i1, eng) in enumerate(jobs):
                    emptied[eng] += 1
                    users.append((eng, emptied[eng]))
                    if r >= 4:
                        e4, n4 = users[r - 4]
                        if e4 == "act":
                            pe.wait_ge(s_pa, b * NPJ_ACT + n4)
                        elif e4 == "piece":
                            pe.wait_ge(s_full, b * NNAT + n4)
                        else:
                            pe.wait_ge(s_pd, b * NPJ_DVE + n4)
                    dst = bank[:, r % 4, :]
                    blk = slice(i0 * BLK, (i0 + 1) * BLK)
                    if kind == "lat":
                        lat_done[i0] = emptied["act"]
                        ins = all_k(dst, [(wd[:, kc, :], xT[:, kc, blk]) for kc in range(DC)])
                    elif kind == "points":
                        for n in range(4):
                            tok = slice((4 * i0 + n) * P, (4 * i0 + n + 1) * P)
                            ins = all_k(dst[:, n * P:(n + 1) * P], [(xT[:, kc, tok], w12[:, kc, :]) for kc in range(DC)])
                    elif kind in ("q", "q_swapped", "k", "k_swapped") and (layer == 1 or kind[0] == "q"):
                        if layer == 0:
                            w, o0 = (wq if kind == "q" else wqs), i1 * P
                        else:
                            w, o0 = wqkv, i1 * P + (D if kind == "k" else 0)
                        ins = all_k(dst, [(w[:, kc, o0:o0 + P], xT[:, kc, blk]) for kc in range(DC)])
                    elif kind in ("k", "k_swapped"):
                        pe.wait_ge(s_pa, b * NPJ_ACT + lat_done[i0])
                        w = wk if kind == "k" else wks
                        ins = all_k(dst, [(w[:, i1 * P:(i1 + 1) * P], lat[:, blk])])
                    elif kind == "v":
                        tok = slice(i0 * P, (i0 + 1) * P)
                        if layer == 0:
                            ins = all_k(dst[:, 0:D], [(lat[:, tok], wv[:, :])])
                        else:
                            ins = all_k(dst[:, 0:D], [(xT[:, kc, tok], wqkv[:, kc, 2 * D:3 * D]) for kc in range(DC)])
                    else:
                        pe.wait_ge(s_lq, b + 1)
                        src = la if i0 == 0 else lb
                        for n in range(4):
                            t = 4 * i1 + n
                            ins = nc.tensor.transpose(dst[0:96, n * P:(n + 1) * P], src[:, t * 96:(t + 1) * 96], ident[:, :])
                    ins.then_inc(s_pj, 1)

                ring = [0]

                def ring_job(job):
                    r = ring[0]
                    ring[0] += 1
                    if bank_before[r] is not None:
                        pe.wait_ge(s_rd, b * NR + bank_before[r] + 1)
                    dst = bank[:, ring_bank[r], :]
                    if job[0] == "max":
                        _, g, j, qt, c = job
                        if j == 0 and qt == 0:
                            pe.wait_ge(s_stk[g], b * (NSTK * 16) + NSTK * 16)
                        w = BLK if (qt >= 4 and c == 0) else P * (qt % 4 + 1)
                        diag = qt < 4 or c == 1
                        ins = nc.tensor.matmul(dst[:, 0:w], qst[g % 3][0:SHROW, j, qt * P:(qt + 1) * P],
                                               kst[g % 3][0:SHROW, j, c * BLK:c * BLK + w], start=True, stop=not diag)
                        if diag:
                            ins = nc.tensor.matmul(dst[:, w - P:w], maskT[:, :], identb[:, :], start=False, stop=True)
                    elif job[0] == "shift":
                        pe.wait_ge(s_cb, b * NG + job[1] + 1)
                        ins = nc.tensor.transpose(dst[0:32, 0:P], mx[:, job[1] % 2, :, :].rearrange("p j n -> p (j n)"), ident[:, :])
                    elif job[0] == "sums":
                        pe.wait_ge(s_ov, b * NU + job[1] + 1)
                        for n in range(4):
                            ins = nc.tensor.matmul(dst[:, n * HG:(n + 1) * HG], o_sb[:, job[1] % 2, n * P:(n + 1) * P], sel[:, :],
                                                   start=True, stop=True)
                    else:
                        pe.wait_ge(s_rec, (b * NU + job[1]) * 2 + 2)
                        for n in range(4):
                            ins = nc.tensor.transpose(dst[:, n * P:(n + 1) * P], rec_wide[:, n * P:(n + 1) * P], ident[:, :])
                    ins.then_inc(s_ring, 1)

                def step_of(s):
                    i = s % 12
                    qb, kt = (0, i) if i < 4 else (1, i - 4)
                    return s // 12, qb, kt, P * max(0, kt - 4 * qb)

                def score_pair(s, p):
                    g, qb, kt, off = step_of(s)
                    e = 2 * s + p
                    if e >= 2:
                        pe.wait_ge(s_ex, b * NPAIR + e - 1)
                    for h in range(2):
                        j = 2 * p + h
                        dst = scores[e % 2][:, h, :]
                        diag = kt >= 4 * qb
                        ins = nc.tensor.matmul(dst[:, off:], kst[g % 3][0:KFULL, j, kt * P:(kt + 1) * P],
                                               qst[g % 3][0:KFULL, j, qb * BLK + off:(qb + 1) * BLK], start=True, stop=not diag)
                        if diag:
                            ins = nc.tensor.matmul(dst[:, off:off + P], identb[:, :], maskT[:, :], start=False, stop=True)
                    ins.then_inc(s_st, 1)

                def values(s):
                    g, qb, kt, off = step_of(s)
                    u = 2 * g + qb
                    if kt == 0 and u >= 2:
                        pe.wait_ge(s_ov, b * NU + u - 1)
                    pe.wait_ge(s_ex, b * NPAIR + 2 * s + 2)
                    for j in range(HG):
                        e = 2 * s + j // 2
                        ins = nc.tensor.matmul(bank[32 * j:32 * j + 32, PV0 + u % 2, off:], vaug[:, kt, HG * g + j, :],
                                               probs[:, e % 4, j % 2, off:], start=(kt == 0), stop=(kt == 4 * qb + 3))
                    ins.then_inc(s_pv, 1)

                pe.wait_ge(s_pa, b * NPJ_ACT + NPJ_ACT)
                pe.wait_ge(s_pd, b * NPJ_DVE + NPJ_DVE)
                pe.wait_ge(s_full, b * NNAT + NNAT)
                for job in first:
                    ring_job(job)
                pe.wait_ge(s_rd, b * NR + len(first))
                for s in range(NSTEP):
                    if s % 12 == 0:
                        pe.wait_ge(s_shl, (b * NG + s // 12) * 32 + 32)
                    score_pair(s, 0)
                    for job in at[s][0:2]:
                        ring_job(job)
                    score_pair(s, 1)
                    for job in at[s][2:4]:
                        ring_job(job)
                    if s:
                        values(s - 1)
                    for job in at[s][4:]:
                        ring_job(job)
                values(NSTEP - 1)
                pe.wait_ge(s_ex, b * NPAIR + NPAIR)
                transpose_tokens(b + 1)
                for job in last:
                    ring_job(job)
                assert ring[0] == NR

                pe.wait_ge(s_rd, b * NR + NR)
                for t in range(TT):
                    if t >= 4:
                        pe.wait_ge(s_z, b * (3 * TT + 1) + t - 3)
                    all_k(bank[:, 4 + t % 4, 0:D], [(oT[:, g, t * P:(t + 1) * P], wo[:, g, :]) for g in range(NG)]).then_inc(s_wo, 1)


def mixture_of_depths(nc, W, x_in, x_out, score_d):
    with Stage(nc, "mod") as S:
        w1 = S.sb("w1", [P, DC, FF]); w2 = S.sb("w2", [P, FC, D])
        b1 = S.sb("b1", [P, FC]); b2 = S.sb("b2", [P, D]); wr = S.sb("wr", [P, D])
        ident = S.sb("ident", [P, P]); before = S.sb("before", [P, T])
        xT = S.sb("xT", [P, DC, T]); xr = S.sb("xr", [P, TT, D]); x2 = S.sb("x2", [P, TT, D])
        prod = S.sb("prod", [P, TT, D]); hid = S.sb("hid", [P, NBLK, FC, BLK])
        z = S.sb("z", [P, TT, D])
        sc = S.sb("sc", [P, TT]); scT = S.sb("scT", [TT, P]); row = S.sb("row", [P, T]); hit = S.sb("hit", [P, T])
        above = S.sb("above", [P, TT]); ties = S.sb("ties", [P, TT]); sig = S.sb("sig", [P, TT]); gate = S.sb("gate", [P, TT])
        stats = S.sb("stats", [P, TT, 6]); mv = S.sb("mv", [P, TT, 2]); sd = S.sb("sd", [P, TT]); rstd = S.sb("rstd", [P, TT])
        bank = S.ps("bank", [P, 8, BLK])
        NW = 7
        NH1 = NBLK * FC
        NSC = TT
        NRK = 2 * TT + 3
        NZ = 4 * TT + 1
        s_w = S.sem("weights_loaded"); s_xr = S.sem("tokens_loaded")
        s_x2 = S.sem("doubled"); s_sc = S.sem("scores_ready"); s_sct = S.sem("scores_transposed"); s_scc = S.sem("score_row_copied")
        s_scd = S.sem("score_row_stored"); s_row = S.sem("score_row_loaded"); s_rk = S.sem("rank_steps"); s_sig = S.sem("sigmoid_ready")
        s_h = S.sem("hidden_ready"); s_ge = S.sem("gelu_ready"); s_o = S.sem("update_ready"); s_z = S.sem("ln_steps")
        s_sd = S.sem("deviation_ready"); s_rs = S.sem("rstd_ready"); s_y = S.sem("result_ready"); s_passed = S.sem("waits_passed")
        s_tr = S.sem("tokens_transposed"); s_te = S.sem("features_ready"); s_out = S.sem("result_stored")
        block = S.block()

        @block.sync
        def _(sp):
            def load_tokens(b):
                sp.dma_start(xr[:, :, :], x_in[b].rearrange("(n p) d -> p n d", p=P)).then_inc(s_xr, 16)

            sp.dma_start(ident[:, :], W["ident"]).then_inc(s_w, 16)
            load_tokens(0)
            sp.dma_start(w1[:, :, :], W["m_w1"].rearrange("(c p) n -> p c n", p=P)).then_inc(s_w, 16)
            sp.dma_start(w2[:, :, :], W["m_w2"].rearrange("(c p) n -> p c n", p=P)).then_inc(s_w, 16)
            sp.dma_start(b1[:, :], W["m_b1T"]).then_inc(s_w, 16)
            sp.dma_start(b2[:, :], W["m_b2"].partition_broadcast(P)).then_inc(s_w, 16)
            sp.dma_start(wr[:, :], W["m_wr"].partition_broadcast(P)).then_inc(s_w, 16)
            sp.dma_start(before[:, :], W["before"]).then_inc(s_w, 16)
            sp.sem_inc(s_out, 16)

            def batch(b, following):
                sp.wait_ge(s_scc, b + 1)
                sp.dma_start(score_d[b].rearrange("(n p) -> n p", p=P), scT[:, :]).then_inc(s_scd, 16)
                sp.wait_ge(s_scd, b * 16 + 16)
                sp.dma_start(row[:, :], score_d[b].partition_broadcast(P)).then_inc(s_row, 16)
                sp.wait_ge(s_x2, b + 1)
                sp.wait_ge(s_tr, b * 4 + 4)
                load_tokens(following)
                sp.wait_ge(s_y, b * TT + TT)
                sp.dma_start(x_out[b].rearrange("(n p) d -> p n d", p=P), z[:, :, :]).then_inc(s_out, 16)

            with sp.Fori(0, NBATCH - 1) as b:
                batch(b, b + 1)
            batch(NBATCH - 1, 0)
            sp.wait_ge(s_xr, (NBATCH + 1) * 16)
            sp.wait_ge(s_out, NBATCH * 16 + 16)

        @block.gpsimd
        def _(pool):
            with pool.Fori(0, NBATCH) as b:
                pool.wait_ge(s_xr, b * 16 + 16)
                nc.gpsimd.tensor_tensor(out=x2[:, :, :], in0=xr[:, :, :], in1=xr[:, :, :], op=ALU.add).then_inc(s_x2, 1)
                pool.wait_ge(s_z, b * NZ + NZ)

        @block.scalar
        def _(act):
            def copy_features(b):
                for k in range(4):
                    act.wait_ge(s_tr, b * 4 + k + 1)
                    nc.scalar.copy(xT[:, k // 2, (k % 2) * BLK:(k % 2 + 1) * BLK], bank[:, k, :]).then_inc(s_te, 1)

            copy_features(0)
            act.wait_ge(s_w, 16 * NW)
            with act.Fori(0, NBATCH) as b:
                act.wait_ge(s_sc, b * NSC + NSC)
                nc.scalar.activation(sig[:, :], sc[:, :], ACT.Sigmoid).then_inc(s_sig, 1)
                for q in range(NH1):
                    act.wait_ge(s_h, b * NH1 + q + 1)
                    nc.scalar.activation(hid[:, q // FC, q % FC, :], bank[:, q % 4, :], ACT.Gelu_apprx_tanh,
                                         bias=b1[:, q % FC:q % FC + 1]).then_inc(s_ge, 1)
                copy_features(b + 1)
                act.wait_ge(s_z, b * NZ + NZ)
                nc.scalar.activation(sd[:, :], sd[:, :], ACT.Sqrt).then_inc(s_sd, 1)

        @block.vector
        def _(dve):
            dve.wait_ge(s_w, 16 * NW)
            with dve.Fori(0, NBATCH) as b:
                dve.wait_ge(s_xr, b * 16 + 16)
                for t in range(TT):
                    nc.vector.tensor_tensor_reduce(out=prod[:, t, :], in0=xr[:, t, :], in1=wr[:, :], scale=1.0, scalar=0.0,
                                                   op0=ALU.mult, op1=ALU.add, accum_out=sc[:, t:t + 1]).then_inc(s_sc, 1)
                dve.wait_ge(s_sct, b + 1)
                nc.vector.tensor_copy(scT[:, :], bank[0:TT, 6, 0:P]).then_inc(s_scc, 1)
                dve.wait_ge(s_row, b * 16 + 16)
                steps = Steps(dve, s_rk, NRK, b)
                for t in range(TT):
                    steps.settled()
                    steps.did(nc.vector.tensor_scalar(hit[:, :], row[:, :], sc[:, t:t + 1], 0.0, ALU.is_gt, ALU.add,
                                                      accum_out=above[:, t:t + 1]))
                    steps.settled()
                    n = P * (t + 1)
                    steps.did(nc.vector.scalar_tensor_tensor(out=hit[:, 0:n], in0=row[:, 0:n], scalar=sc[:, t:t + 1],
                                                             in1=before[:, T - n:T], op0=ALU.is_equal, op1=ALU.mult,
                                                             accum_out=ties[:, t:t + 1]))
                steps.settled()
                steps.did(nc.vector.tensor_tensor(out=above[:, :], in0=above[:, :], in1=ties[:, :], op=ALU.add))
                steps.settled()
                steps.did(nc.vector.tensor_scalar(above[:, :], above[:, :], float(TOPK), None, ALU.is_lt))
                steps.settled()
                dve.wait_ge(s_sig, b + 1)
                steps.did(nc.vector.tensor_tensor(out=gate[:, :], in0=above[:, :], in1=sig[:, :], op=ALU.mult))
                steps.settled()
                steps.end()
                dve.wait_ge(s_x2, b + 1)
                dve.wait_ge(s_out, b * 16 + 16)
                steps = Steps(dve, s_z, NZ, b)
                for t in range(TT):
                    dve.wait_ge(s_o, b * TT + t + 1)
                    steps.did(nc.vector.tensor_tensor(out=z[:, t, :], in0=bank[:, 4 + t % 2, 0:D], in1=b2[:, :], op=ALU.add))
                    steps.settled()
                    steps.did(nc.vector.scalar_tensor_tensor(out=z[:, t, :], in0=z[:, t, :], scalar=gate[:, t:t + 1], in1=x2[:, t, :],
                                                             op0=ALU.mult, op1=ALU.add))
                steps.settled()
                for t in range(TT):
                    steps.did(nc.vector.bn_stats(out=stats[:, t, :], in_=z[:, t, :]))
                steps.settled(s_passed)
                for t in range(TT):
                    steps.did(nc.vector.bn_aggr(out=mv[:, t, :], in_=stats[:, t, :]))
                steps.settled()
                steps.did(nc.vector.tensor_scalar(sd[:, :], mv[:, :, 1], EPS, None, ALU.add))
                steps.end()
                dve.wait_ge(s_sd, b + 1)
                nc.vector.reciprocal(rstd[:, :], sd[:, :]).then_inc(s_rs, 1)
                dve.wait_ge(s_rs, b + 1)
                for t in range(TT):
                    nc.vector.tensor_scalar(z[:, t, :], z[:, t, :], mv[:, t, 0:1], rstd[:, t:t + 1], ALU.subtract, ALU.mult).then_inc(s_y, 1)

        @block.tensor
        def _(pe):
            def transpose_tokens(b):
                pe.wait_ge(s_xr, b * 16 + 16)
                for k in range(4):
                    for n in range(4):
                        t = 4 * (k % 2) + n
                        ins = nc.tensor.transpose(bank[:, k, n * P:(n + 1) * P], xr[:, t, (k // 2) * P:(k // 2 + 1) * P], ident[:, :])
                    ins.then_inc(s_tr, 1)

            pe.wait_ge(s_w, 16 * NW)
            transpose_tokens(0)
            with pe.Fori(0, NBATCH) as b:
                pe.wait_ge(s_te, b * 4 + 4)
                for n in range(NBLK):
                    for f in range(FC):
                        q = n * FC + f
                        if q >= 4:
                            pe.wait_ge(s_ge, b * NH1 + q - 3)
                        for kc in range(DC):
                            ins = nc.tensor.matmul(bank[:, q % 4, :], w1[:, kc, f * P:(f + 1) * P], xT[:, kc, n * BLK:(n + 1) * BLK],
                                                   start=(kc == 0), stop=(kc == DC - 1))
                        ins.then_inc(s_h, 1)
                    if n == 0:
                        pe.wait_ge(s_sc, b * NSC + NSC)
                        nc.tensor.transpose(bank[0:TT, 6, 0:P], sc[:, :], ident[:, :]).then_inc(s_sct, 1)
                for t in range(TT):
                    if t == TT - 2:
                        pe.wait_ge(s_ge, b * NH1 + NH1)
                        transpose_tokens(b + 1)
                    pe.wait_ge(s_ge, b * NH1 + FC * (t // 4 + 1))
                    if t >= 2:
                        pe.wait_ge(s_z, b * NZ + 2 * (t - 2) + 1)
                    for f in range(FC):
                        ins = nc.tensor.matmul(bank[:, 4 + t % 2, 0:D], hid[:, t // 4, f, (t % 4) * P:(t % 4 + 1) * P], w2[:, f, :],
                                               start=(f == 0), stop=(f == FC - 1))
                    ins.then_inc(s_o, 1)


def experts(nc, W, x_in, out, sorted_d, result_d):
    with Stage(nc, "moe") as S:
        NTE = NTILE * NE
        cT = S.sb("cT", [P, DC, NE])
        ident = S.sb("ident", [P, P])
        upper_f = S.sb("upper_f", [P, P]); upper = S.sb("upper", [P, P], BF16); ones = S.sb("ones", [P, P], BF16)
        rev = S.sb("rev", [P, NE])
        not_first = S.sb("not_first", [P, NTE])
        firsts = S.sb("firsts", [P, NTILE])
        numbers = S.sb("numbers", [P, NSLOT])
        x = S.sb("x", [P, NTILE, D])
        xn = S.sb("xn", [P, NTILE, D])
        xT = S.sb("xT", [P, DC, T])
        zero = S.sb("zero", [P, D])
        aff = S.sb("aff", [P, NTE]); eq = S.sb("eq", [P, NTE]); own = S.sb("own", [P, NTE]); ownb = S.sb("ownb", [P, NTE], BF16)
        best = S.sb("best", [P, NTILE]); pick = S.sb("pick", [P, NTILE]); alpha = S.sb("alpha", [P, NTILE])
        count = S.sb("count", [P, NTE]); cum = S.sb("cum", [P, NTE]); over = S.sb("over", [P, NTE]); pos = S.sb("pos", [P, NTE])
        tiles = S.sb("tiles", [P, NE]); ends = S.sb("ends", [P, NE]); base = S.sb("base", [P, NE])
        slot_f = S.sb("slot_f", [P, NTILE]); slot = S.sb("slot", [P, NTILE], I32)
        past = S.sb("past", [1, NSLOT * NE]); eid_f = S.sb("eid_f", [1, NSLOT]); eid = S.sb("eid", [1, NSLOT], I32)
        stats = S.sb("stats", [P, NTILE, 6]); mv = S.sb("mv", [P, NTILE, 2]); sd = S.sb("sd", [P, NTILE]); rstd = S.sb("rstd", [P, NTILE])
        w1 = [S.sb(f"w1_{i}", [P, DC, FF]) for i in range(2)]
        w2 = [S.sb(f"w2_{i}", [P, FC, D]) for i in range(2)]
        small = [S.sb(f"small{i}", [P, FC + 2 * DC]) for i in range(2)]
        b2 = [S.sb(f"b2_{i}", [P, D]) for i in range(2)]
        xs = [S.sb(f"xs{i}", [P, SUB, D]) for i in range(2)]
        xsT = [S.sb(f"xsT{i}", [P, DC, TS]) for i in range(2)]
        hid = [S.sb(f"hid{i}", [P, FC, TS]) for i in range(2)]
        ys = [S.sb(f"ys{i}", [P, SUB, D]) for i in range(2)]
        bank = S.ps("bank", [P, 8, BLK])

        NC = 7
        TURNS = (NSLOT - 2) // 2
        GRP = 8
        NGR = NTILE // GRP
        s_c = S.sem("constants_loaded"); s_cb = S.sem("constants_cast"); s_x = [S.sem(f"tokens_loaded{b}") for b in range(NBATCH)]
        s_xtr = S.sem("tokens_transposed"); s_xt = S.sem("features_ready"); s_zero = S.sem("zeros_set"); s_zd = S.sem("slots_zeroed")
        s_aff = S.sem("affinities_ready"); s_r = S.sem("route_steps"); s_best = S.sem("best_ready"); s_alpha = S.sem("alpha_ready")
        s_own = S.sem("own_ready"); s_cnt = S.sem("counts_ready"); s_slot = S.sem("slots_ready"); s_eid = S.sem("tile_experts_ready")
        s_n = S.sem("norm_steps"); s_sd = S.sem("deviation_ready"); s_xn = S.sem("normalised"); s_sc = S.sem("scattered"); s_x2 = S.sem("doubled")
        s_w1 = [S.sem(f"first_weights_loaded{i}") for i in range(2)]; s_w2 = [S.sem(f"second_weights_loaded{i}") for i in range(2)]
        s_sm = [S.sem(f"small_weights_loaded{i}") for i in range(2)]; s_xs = [S.sem(f"slots_loaded{i}") for i in range(2)]
        s_t = S.sem("slots_transposed"); s_xg = S.sem("slot_features_ready")
        s_h = S.sem("hidden_ready"); s_ra = S.sem("relu_by_act"); s_rv = S.sem("relu_by_dve")
        s_o = S.sem("slot_result_ready"); s_ys = S.sem("slot_result_biased"); s_yd = [S.sem(f"slot_result_stored{i}") for i in range(2)]
        s_g = [S.sem(f"gathered{i}") for i in range(NGR)]; s_f = S.sem("final_steps"); s_fsd = S.sem("final_deviation_ready")
        s_fy = S.sem("final_ready"); s_passed = S.sem("waits_passed"); s_passed_pool = S.sem("pool_waits_passed"); s_frs = S.sem("final_rstd_ready"); s_out = S.sem("result_stored")
        block = S.block()

        def te(t):
            return t[:, :].rearrange("p (t e) -> p t e", e=NE)

        def et(t):
            return t[:, :].rearrange("p (e t) -> p e t", e=NE)

        def swapped(t):
            return t[:, :].rearrange("p (e t) -> p t e", e=NE)

        def slot_tiles(eng, body):
            with eng.Fori(0, TURNS) as turn:
                for i in range(2):
                    body(2 * turn + i, turn, i, True, True)
            for j in range(2 * TURNS, NSLOT):
                body(j, j // 2, j % 2, j + 1 < NSLOT, j + 2 < NSLOT)

        def hidden_bank(f):
            return bank[:, f // 2, (f % 2) * TS:(f % 2 + 1) * TS]

        @block.sync
        def _(sp):
            sp.dma_start(ident[:, :], W["ident"]).then_inc(s_c, 16)
            sp.dma_start(cT[:, :, :], W["e_cT"].rearrange("(c p) e -> p c e", p=P)).then_inc(s_c, 16)
            for b in range(NBATCH):
                sp.dma_start(x[:, TT * b:TT * b + TT, :], x_in[b].rearrange("(n p) d -> p n d", p=P)).then_inc(s_x[b], 16)
            for dst, src in ((upper_f[:, :], W["upper"]), (rev[:, :], W["rev"]), (not_first[:, :], W["not_first"]),
                             (firsts[:, :], W["firsts"]), (numbers[:, :], W["numbers"])):
                sp.dma_start(dst, src).then_inc(s_c, 16)
            sp.wait_ge(s_zero, 1)
            slots = sorted_d.rearrange("(n p) d -> p n d", p=P)
            sp.dma_start(slots, zero[:, :].unsqueeze(1).broadcast_to([P, NSLOT * SUB, D])).then_inc(s_zd, 16)

            def expert_of(j):
                return sp.value_load(eid[0:1, bass.ds(j, 1)], min_val=0, max_val=NE - 1)

            def load_first(e, i):
                sp.dma_start(small[i][:, :], W["e_small"][e]).then_inc(s_sm[i], 16)
                sp.dma_start(w1[i][:, :, :], W["e_w1T"][e].rearrange("(c p) n -> p c n", p=P)).then_inc(s_w1[i], 16)

            def load_second(e, i):
                sp.dma_start(w2[i][:, :, :], W["e_w2T"][e].rearrange("(c p) n -> p c n", p=P)).then_inc(s_w2[i], 16)
                sp.dma_start(b2[i][:, :], W["e_b2"][e].partition_broadcast(P)).then_inc(s_w2[i], 16)

            for i in range(2):
                sp.sem_inc(s_yd[i], 16)
            sp.wait_ge(s_eid, 1)
            for j in range(2):
                e = expert_of(j)
                load_first(e, j)
                load_second(e, j)

            def tile(j, turn, i, following, second):
                if second:
                    e = expert_of(j + 2)
                    sp.wait_ge(s_ra, 4 * j + 4)
                    hold(sp, s_rv, 4 * j + 4, s_passed)
                    load_first(e, i)
                hold(sp, s_ys, j + 1, s_passed)
                sp.dma_start(result_d[bass.ds(j * TS, TS), :].rearrange("(n p) d -> p n d", p=P), ys[i][:, :, :]).then_inc(s_yd[i], 16)
                if second:
                    load_second(e, i)

            slot_tiles(sp, tile)
            for gr in range(NGR):
                sp.wait_ge(s_fy, GRP * (gr + 1))
                tok = out.rearrange("b (n p) d -> (b n) p d", p=P)[GRP * gr:GRP * (gr + 1)].rearrange("n p d -> p n d")
                sp.dma_start(tok, xn[:, GRP * gr:GRP * (gr + 1), :]).then_inc(s_out, 16)
            sp.wait_ge(s_out, 16 * NGR)

        @block.gpsimd
        def _(pool):
            nc.gpsimd.memset(zero[:, :], 0.0).then_inc(s_zero, 1)
            pool.wait_ge(s_slot, 1)
            pool.wait_ge(s_zd, 16)
            pool.wait_ge(s_xn, NTILE)
            for t in range(NTILE):
                nc.gpsimd.indirect_dma_start(out=sorted_d[:, :], out_offset=bass.IndirectOffsetOnAxis(ap=slot[:, t:t + 1], axis=0),
                                             in_=xn[:, t, :], in_offset=None).then_inc(s_sc, 16)
            nc.gpsimd.tensor_tensor(out=x[:, :, :], in0=x[:, :, :], in1=x[:, :, :], op=ALU.add).then_inc(s_x2, 1)
            pool.wait_ge(s_sc, 16 * NTILE)

            def load_slots(j, i):
                pool.dma_start(xs[i][:, :, :], sorted_d[bass.ds(j * TS, TS), :].rearrange("(n p) d -> p n d", p=P)).then_inc(s_xs[i], 16)

            for i in range(2):
                load_slots(i, i)

            def tile(j, turn, i, following, second):
                if second:
                    hold(pool, s_t, j + 1, s_passed_pool)
                    load_slots(j + 2, i)

            slot_tiles(pool, tile)
            for i in range(2):
                pool.wait_ge(s_yd[i], 16 * ((NSLOT + 1 - i) // 2) + 16)
            for t in range(NTILE):
                nc.gpsimd.indirect_dma_start(out=xn[:, t, :], out_offset=None, in_=result_d[:, :],
                                             in_offset=bass.IndirectOffsetOnAxis(ap=slot[:, t:t + 1], axis=0)).then_inc(s_g[t // GRP], 16)

        @block.scalar
        def _(act):
            for b in range(NBATCH):
                for k in range(4):
                    act.wait_ge(s_xtr, 4 * b + k + 1)
                    nc.scalar.copy(xT[:, k // 2, (k % 2) * BLK:(k % 2 + 1) * BLK], bank[:, 4 + k, :]).then_inc(s_xt, 1)
            act.wait_ge(s_best, 1)
            nc.scalar.activation(alpha[:, :], best[:, :], ACT.Sigmoid).then_inc(s_alpha, 1)
            act.wait_ge(s_n, 2 * NTILE + 1)
            nc.scalar.activation(sd[:, :], sd[:, :], ACT.Sqrt).then_inc(s_sd, 1)

            def tile(j, turn, i, following, second):
                act.wait_ge(s_sm[i], 16 * turn + 16)
                for f in range(FC // 2):
                    if f % 2 == 0:
                        act.wait_ge(s_h, 4 * j + f // 2 + 1)
                    nc.scalar.activation(hid[i][:, f, :], hidden_bank(f), ACT.Relu, bias=small[i][:, f:f + 1]).then_inc(s_ra, 1)

            slot_tiles(act, tile)
            for gr in range(NGR):
                act.wait_ge(s_f, (gr + 1) * (3 * GRP + 1))
                part = sd[:, GRP * gr:GRP * (gr + 1)]
                nc.scalar.activation(part, part, ACT.Sqrt).then_inc(s_fsd, 1)

        @block.vector
        def _(dve):
            dve.wait_ge(s_c, 16 * NC)
            nc.vector.tensor_copy(upper[:, :], upper_f[:, :]).then_inc(s_cb, 1)
            nc.vector.memset(ones[:, :], 1.0).then_inc(s_cb, 1)
            steps = Steps(dve, s_n, 2 * NTILE + 1, 0)
            for t in range(NTILE):
                dve.wait_ge(s_x[t // TT], 16)
                steps.did(nc.vector.bn_stats(out=stats[:, t, :], in_=x[:, t, :]))
            steps.settled()
            for t in range(NTILE):
                steps.did(nc.vector.bn_aggr(out=mv[:, t, :], in_=stats[:, t, :]))
            steps.settled()
            steps.did(nc.vector.tensor_scalar(sd[:, :], mv[:, :, 1], EPS, None, ALU.add))
            steps.end()

            steps = Steps(dve, s_r, 21, 0)
            dve.wait_ge(s_aff, NBATCH)
            steps.did(nc.vector.tensor_copy(aff[:, :], bank[:, 0, 0:NTE]))
            steps.settled()
            nc.vector.tensor_reduce(out=best[:, :], in_=te(aff), axis=AX.X, op=ALU.max).then_inc(s_best, 1)
            dve.wait_ge(s_best, 1)
            per_tile = [P, NTILE, NE]
            revb = rev[:, :].unsqueeze(1).broadcast_to(per_tile)
            steps.did(nc.vector.tensor_tensor(out=te(eq), in0=te(aff), in1=best[:, :].unsqueeze(2).broadcast_to(per_tile), op=ALU.is_equal))
            steps.settled()
            steps.did(nc.vector.tensor_tensor(out=te(eq), in0=te(eq), in1=revb, op=ALU.mult))
            steps.settled()
            steps.did(nc.vector.tensor_reduce(out=pick[:, :], in_=te(eq), axis=AX.X, op=ALU.max))
            steps.settled()
            steps.did(nc.vector.tensor_tensor(out=te(own), in0=revb, in1=pick[:, :].unsqueeze(2).broadcast_to(per_tile), op=ALU.is_equal))
            steps.settled()
            nc.vector.tensor_copy(ownb[:, :], own[:, :]).then_inc(s_own, 1)
            dve.wait_ge(s_cnt, 1)
            steps.did(nc.vector.tensor_copy(et(count), bank[:, 2, 0:NTE].rearrange("p (t e) -> p e t", e=NE)))
            steps.settled()
            steps.did(nc.vector.tensor_tensor_scan(out=cum[:, :], data0=not_first[:, :], data1=count[:, :], initial=0.0,
                                                   op0=ALU.mult, op1=ALU.add))
            steps.settled()
            per_expert = [P, NE, NTILE]
            total = et(cum)[:, :, NTILE - 1:NTILE].broadcast_to(per_expert)
            steps.did(nc.vector.tensor_tensor(out=et(over), in0=total, in1=firsts[:, :].unsqueeze(1).broadcast_to(per_expert), op=ALU.is_gt))
            steps.settled()
            steps.did(nc.vector.tensor_reduce(out=tiles[:, :], in_=et(over), axis=AX.X, op=ALU.add))
            steps.settled()
            steps.did(nc.vector.tensor_tensor_scan(out=ends[:, :], data0=not_first[:, 1:1 + NE], data1=tiles[:, :], initial=0.0,
                                                   op0=ALU.mult, op1=ALU.add))
            steps.settled()
            steps.did(nc.vector.tensor_tensor(out=base[:, :], in0=ends[:, :], in1=tiles[:, :], op=ALU.subtract))
            steps.settled()
            steps.did(nc.vector.tensor_scalar(base[:, :], base[:, :], float(TS), None, ALU.mult))
            steps.did(nc.vector.tensor_tensor(out=cum[:, :], in0=cum[:, :], in1=count[:, :], op=ALU.subtract))
            steps.settled()
            steps.did(nc.vector.tensor_tensor(out=te(pos), in0=bank[:, 1, 0:NTE].rearrange("p (t e) -> p t e", e=NE), in1=swapped(cum), op=ALU.add))
            steps.settled()
            steps.did(nc.vector.tensor_tensor(out=te(pos), in0=te(pos), in1=base[:, :].unsqueeze(1).broadcast_to(per_tile), op=ALU.add))
            steps.settled()
            steps.did(nc.vector.tensor_tensor(out=pos[:, :], in0=pos[:, :], in1=own[:, :], op=ALU.mult))
            steps.settled()
            steps.did(nc.vector.tensor_reduce(out=slot_f[:, :], in_=te(pos), axis=AX.X, op=ALU.add))
            steps.settled()
            nc.vector.tensor_copy(slot[:, :], slot_f[:, :]).then_inc(s_slot, 1)
            in_tile = [1, NSLOT, NE]
            pastv = past[:, :].rearrange("p (t e) -> p t e", e=NE)
            steps.did(nc.vector.tensor_tensor(out=pastv, in0=ends[0:1, :].unsqueeze(1).broadcast_to(in_tile),
                                              in1=numbers[0:1, :].unsqueeze(2).broadcast_to(in_tile), op=ALU.is_le))
            steps.settled()
            steps.did(nc.vector.tensor_reduce(out=eid_f[:, :], in_=pastv, axis=AX.X, op=ALU.add))
            steps.settled()
            steps.did(nc.vector.tensor_scalar(eid_f[:, :], eid_f[:, :], float(NE - 1), None, ALU.min))
            steps.settled()
            nc.vector.tensor_copy(eid[:, :], eid_f[:, :]).then_inc(s_eid, 1)
            dve.wait_ge(s_sd, 1)
            steps.did(nc.vector.reciprocal(rstd[:, :], sd[:, :]))
            steps.settled()
            for t in range(NTILE):
                nc.vector.tensor_scalar(xn[:, t, :], x[:, t, :], mv[:, t, 0:1], rstd[:, t:t + 1], ALU.subtract, ALU.mult).then_inc(s_xn, 1)
            steps.end()

            def gain_shift(j, turn, i):
                dve.wait_ge(s_sm[i], 16 * turn + 16)
                dve.wait_ge(s_t, j + 1)
                for c in range(DC):
                    ins = nc.vector.tensor_scalar(xsT[i][:, c, :], bank[:, 4 + i, c * TS:(c + 1) * TS], small[i][:, FC + c:FC + c + 1],
                                                  small[i][:, FC + DC + c:FC + DC + c + 1], ALU.mult, ALU.add)
                ins.then_inc(s_xg, 1)

            def tile(j, turn, i, following, second):
                for f in range(FC // 2, FC):
                    if f % 2 == 0:
                        dve.wait_ge(s_h, 4 * j + f // 2 + 1)
                    nc.vector.tensor_scalar(hid[i][:, f, :], hidden_bank(f), small[i][:, f:f + 1], 0.0, ALU.add, ALU.max).then_inc(s_rv, 1)
                if following:
                    gain_shift(j + 1, turn + i, 1 - i)
                dve.wait_ge(s_w2[i], 32 * turn + 32)
                dve.wait_ge(s_yd[i], 16 * turn + 16)
                dve.wait_ge(s_o, j + 1)
                for n in range(SUB):
                    ins = nc.vector.tensor_tensor(out=ys[i][:, n, :], in0=bank[:, 6 + i, n * D:(n + 1) * D], in1=b2[i][:, :], op=ALU.add)
                ins.then_inc(s_ys, 1)

            gain_shift(0, 0, 0)
            slot_tiles(dve, tile)

            dve.wait_ge(s_alpha, 1)
            dve.wait_ge(s_x2, 1)
            steps = Steps(dve, s_f, NGR * (3 * GRP + 1), 0)
            for gr in range(NGR):
                mine = range(GRP * gr, GRP * (gr + 1))
                dve.wait_ge(s_g[gr], 16 * GRP)
                for t in mine:
                    steps.did(nc.vector.scalar_tensor_tensor(out=xn[:, t, :], in0=xn[:, t, :], scalar=alpha[:, t:t + 1], in1=x[:, t, :],
                                                             op0=ALU.mult, op1=ALU.add))
                steps.settled()
                for t in mine:
                    steps.did(nc.vector.bn_stats(out=stats[:, t, :], in_=xn[:, t, :]))
                steps.settled()
                for t in mine:
                    steps.did(nc.vector.bn_aggr(out=mv[:, t, :], in_=stats[:, t, :]))
                steps.settled()
                part = slice(GRP * gr, GRP * (gr + 1))
                steps.did(nc.vector.tensor_scalar(sd[:, part], mv[:, part, 1], EPS, None, ALU.add))
                dve.wait_ge(s_fsd, gr + 1)
                nc.vector.reciprocal(rstd[:, part], sd[:, part]).then_inc(s_frs, 1)
                dve.wait_ge(s_frs, gr + 1)
                for t in mine:
                    nc.vector.tensor_scalar(xn[:, t, :], xn[:, t, :], mv[:, t, 0:1], rstd[:, t:t + 1], ALU.subtract, ALU.mult).then_inc(s_fy, 1)
            steps.end()

        @block.tensor
        def _(pe):
            pe.wait_ge(s_c, 16 * NC)
            for b in range(NBATCH):
                pe.wait_ge(s_x[b], 16)
                for k in range(4):
                    if b:
                        pe.wait_ge(s_xt, 4 * b - 3 + k)
                    for n in range(4):
                        t = TT * b + 4 * (k % 2) + n
                        ins = nc.tensor.transpose(bank[:, 4 + k, n * P:(n + 1) * P], x[:, t, (k // 2) * P:(k // 2 + 1) * P], ident[:, :])
                    ins.then_inc(s_xtr, 1)
                pe.wait_ge(s_xt, 4 * b + 4)
                for t in range(TT):
                    col = (TT * b + t) * NE
                    for kc in range(DC):
                        ins = nc.tensor.matmul(bank[:, 0, col:col + NE], xT[:, kc, t * P:(t + 1) * P], cT[:, kc, :],
                                               start=(kc == 0), stop=(kc == DC - 1))
                ins.then_inc(s_aff, 1)
            pe.wait_ge(s_cb, 2)
            pe.wait_ge(s_own, 1)
            nc.tensor.matmul(bank[:, 1, 0:NTE], upper[:, :], ownb[:, :], start=True, stop=True)
            nc.tensor.matmul(bank[:, 2, 0:NTE], ones[:, :], ownb[:, :], start=True, stop=True).then_inc(s_cnt, 1)

            def transpose_slots(j, turn, i):
                pe.wait_ge(s_xs[i], 16 * turn + 16)
                for c in range(DC):
                    for n in range(SUB):
                        ins = nc.tensor.transpose(bank[:, 4 + i, c * TS + n * P:c * TS + (n + 1) * P], xs[i][:, n, c * P:(c + 1) * P], ident[:, :])
                ins.then_inc(s_t, 1)

            def tile(j, turn, i, following, second):
                pe.wait_ge(s_w1[i], 16 * turn + 16)
                pe.wait_ge(s_xg, j + 1)
                for f in range(FC):
                    for kc in range(DC):
                        ins = nc.tensor.matmul(hidden_bank(f), w1[i][:, kc, f * P:(f + 1) * P], xsT[i][:, kc, :],
                                               start=(kc == 0), stop=(kc == DC - 1))
                    if f % 2 == 1:
                        ins.then_inc(s_h, 1)
                if following:
                    transpose_slots(j + 1, turn + i, 1 - i)
                pe.wait_ge(s_w2[i], 32 * turn + 32)
                for n in range(SUB):
                    for f in range(FC):
                        if n == 0:
                            pe.wait_ge(s_ra if f < 4 else s_rv, (FC // 2) * j + f % 4 + 1)
                        ins = nc.tensor.matmul(bank[:, 6 + i, n * D:(n + 1) * D], hid[i][:, f, n * P:(n + 1) * P], w2[i][:, f, :],
                                               start=(f == 0), stop=(f == FC - 1))
                ins.then_inc(s_o, 1)

            pe.wait_ge(s_slot, 1)
            transpose_slots(0, 0, 0)
            slot_tiles(pe, tile)


def build_program(nc, I, out):
    def scratch(name, shape):
        return nc.dram_tensor(name, shape, F32).ap()

    qk_d = scratch("qk_parts", [NBATCH, 4, D, T])
    ln_d = scratch("line_parts", [NBATCH, 4, NH * NL, T])
    score_d = scratch("router_scores", [NBATCH, T])
    x1 = scratch("x1", [NBATCH, T, D])
    x2 = scratch("x2", [NBATCH, T, D])
    x3 = scratch("x3", [NBATCH, T, D])
    attention(nc, 0, I, I["x"], x1, qk_d, ln_d)
    mixture_of_depths(nc, I, x1, x2, score_d)
    attention(nc, 1, I, x2, x3, qk_d, ln_d)
    sorted_d = scratch("sorted_tokens", [NSLOT * TS, D]); result_d = scratch("slot_results", [NSLOT * TS, D])
    experts(nc, I, x3, out, sorted_d, result_d)


def lay_out(inputs):
    a = {k: np.asarray(v) for k, v in inputs.items()}

    def cont(x):
        return np.ascontiguousarray(x)

    def by_strips(w):
        out = np.zeros((NH, 32, D), np.float32)
        out[:, 0:DH, :] = w.reshape(NH, DH, D)
        return out.reshape(NH * 32, D)

    def by_features(v):
        return v.reshape(NE, -1, P).transpose(0, 2, 1)

    small = cont(np.concatenate([by_features(a["L1_ffn_b1"]), by_features(a["L1_ffn_ln_g"]), by_features(a["L1_ffn_ln_b"])], axis=2))
    swap = np.arange(D) ^ 1
    r = np.arange(P)
    inv = 1.0 / 10000.0 ** (np.arange(0, DH, 2, dtype=np.float32) / DH)
    ang = np.outer(np.arange(T, dtype=np.float32), inv)
    cos = np.cos(ang).astype(np.float32).T[(r % DH) // 2]
    sin = np.sin(ang).astype(np.float32).T[(r % DH) // 2]
    sin = np.where((r % 2 == 0)[:, None], -sin, sin)
    k, q = np.meshgrid(np.arange(P), np.arange(P), indexing="ij")
    big = np.float32(-3e38)
    return {
        "x": cont(a["L0_attn_x"]),
        "L0_wq": cont(a["L0_attn_wq"]), "L0_wqs": cont(a["L0_attn_wq"][:, swap]), "L0_wd": cont(a["L0_attn_w_down"]),
        "L0_wk": cont(a["L0_attn_wk_up"]), "L0_wks": cont(a["L0_attn_wk_up"][:, swap]), "L0_wv": cont(a["L0_attn_wv_up"]),
        "L0_wo": by_strips(a["L0_attn_wo"]),
        "L1_wqkv": cont(a["L1_attn_Wqkv"]), "L1_bqk": cont(a["L1_attn_bqkv"][0:2 * D].reshape(4, P).T), "L1_bv": cont(a["L1_attn_bqkv"][2 * D:]),
        "L1_w12": cont(np.concatenate([a["L1_attn_W1p"], a["L1_attn_W2p"]], axis=1)),
        "L1_pscale": cont(a["L1_attn_plucker_scale"]), "L1_wo": by_strips(a["L1_attn_Wout"]), "L1_bout": cont(a["L1_attn_bout"]),
        "m_wr": cont(a["L0_ffn_w_router"]), "m_w1": cont(a["L0_ffn_W1"]), "m_b1T": cont(a["L0_ffn_b1"].reshape(FC, P).T),
        "m_w2": cont(a["L0_ffn_W2"]), "m_b2": cont(a["L0_ffn_b2"]),
        "e_cT": cont(a["L1_ffn_centroids"].T), "e_small": small,
        "e_w1T": cont(a["L1_ffn_w1"].transpose(0, 2, 1)), 
        "e_w2T": cont(a["L1_ffn_w2"].transpose(0, 2, 1)), "e_b2": cont(a["L1_ffn_b2"]),
        "rope": np.stack([cos, sin]).astype(np.float32),
        "before": np.concatenate([np.ones((P, T - P), np.float32), (q < k).astype(np.float32)], axis=1),
        "upper": (k < q).astype(np.float32),
        "rev": np.tile(NE - np.arange(NE, dtype=np.float32), (P, 1)),
        "not_first": np.tile((np.arange(NTILE * NE) % NTILE != 0).astype(np.float32), (P, 1)),
        "firsts": np.tile(TS * np.arange(NTILE, dtype=np.float32), (P, 1)),
        "numbers": np.tile(np.arange(NSLOT, dtype=np.float32), (P, 1)),
        "ident": np.eye(P, dtype=np.float32),
        "sel": (np.arange(P)[:, None] == 32 * np.arange(HG)[None, :] + DH).astype(np.float32),
        "maskT0": np.where((k >= 64) & (q < 64), big, np.float32(0)).astype(np.float32),
        "maskT1": np.where(k > q, big, np.float32(0)).astype(np.float32),
        "jsign": np.tile(np.array([1, -1, 1, 1, -1, 1], np.float32), (P, 1)),
    }


def kernel(**inputs):
    import concourse.bacc as bacc
    from concourse.bass_utils import run_bass_kernel_spmd

    nc = bacc.Bacc("TRN2", target_bir_lowering=False, num_devices=1)
    arrays = lay_out(inputs)
    aps = {name: nc.dram_tensor(name, list(a.shape), mybir.dt.from_np(a.dtype), kind="ExternalInput").ap() for name, a in arrays.items()}
    out = nc.dram_tensor("out", [NBATCH, T, D], F32, kind="ExternalOutput").ap()
    build_program(nc, aps, out)
    r = run_bass_kernel_spmd(nc, [arrays], core_ids=[0])
    return r.results[0]["out"]
```

```python
import concourse.bass as bass
from concourse import mybir
from contextlib import ExitStack
import numpy as np

F32 = mybir.dt.float32
F32R = mybir.dt.float32r
BF16 = mybir.dt.bfloat16
I32 = mybir.dt.int32
ALU = mybir.AluOpType
ACT = mybir.ActivationFunctionType
AX = mybir.AxisListType

P = 128
NBATCH, T, D = 4, 1024, 256
NH = 16
DH = D // NH
DC = D // P
TT = T // P
BLK = 512
NBLK = T // BLK
HG = 4
NG = NH // HG
FF = 1024
FC = FF // P
NE = 8
NTOK = NBATCH * T
NTILE = NTOK // P
SUB = 2
TS = SUB * P
NSLOT = (NTOK + NE * (TS - 1)) // TS
TOPK = T // 2
EPS = 1e-5

LROW = 64
NL = 6
SHROW = 94
KFULL = 96


PARTS = ((0, 0), (0, 1), (1, 0))


class Stage:

    def __init__(self, nc, tag):
        self.nc, self.tag, self.ctx, self.sems = nc, tag, ExitStack(), []

    def __enter__(self):
        self.ctx.__enter__()
        return self

    def __exit__(self, *a):
        done = self.ctx.__exit__(*a)
        self.nc.clear_and_free_semaphores(self.sems)
        self.nc.all_engine_barrier()
        return done

    def sb(self, name, shape, dt=F32):
        return self.ctx.enter_context(self.nc.sbuf_tensor(f"{self.tag}_{name}", shape, dt))

    def ps(self, name, shape, dt=F32):
        return self.ctx.enter_context(self.nc.psum_tensor(f"{self.tag}_{name}", shape, dt))

    def sem(self, name):
        self.sems.append(self.nc.alloc_semaphore(f"{self.tag}_{name}"))
        return self.sems[-1]

    def block(self):
        return self.ctx.enter_context(self.nc.Block())


def hold(eng, sem, value, passed):
    eng.wait_ge(sem, value)
    eng.sem_inc(passed, 1)


class Steps:

    def __init__(self, eng, sem, per, b):
        self.eng, self.sem, self.per, self.b, self.n = eng, sem, per, b, 0

    def did(self, ins):
        self.n += 1
        ins.then_inc(self.sem, 1)

    def settled(self, passed=None):
        if passed is not None:
            hold(self.eng, self.sem, self.b * self.per + self.n, passed)
        else:
            self.eng.wait_ge(self.sem, self.b * self.per + self.n)

    def end(self):
        assert self.n == self.per, f"{self.n} steps, not {self.per}"


def proj_jobs(layer):
    jobs = []
    if layer == 0:
        for n in range(NBLK):
            jobs.append(("lat", n, 0, "act"))
        for c in range(DC):
            for kind in ("q", "k"):
                for n in range(NBLK):
                    jobs += [(kind, n, c, "dve"), (kind + "_swapped", n, c, "dve")]
        for t in range(TT):
            jobs.append(("v", t, 0, "act"))
    else:
        for h in range(2):
            jobs.append(("points", h, 0, "act"))
        for c in range(DC):
            for kind in ("q", "k"):
                for n in range(NBLK):
                    jobs.append((kind, n, c, "piece"))
        for t in range(TT):
            jobs.append(("v", t, 0, "dve"))
        for w in range(2):
            for h in range(2):
                jobs.append(("lines", w, h, "dve"))
    return jobs


def projections(nc, layer, W, x_in, qk_d, ln_d, v_d):
    with Stage(nc, f"pj{layer}") as S:
        jobs = proj_jobs(layer)
        NPJ = len(jobs)
        NPJ_ACT = sum(j[3] == "act" for j in jobs)
        NPJ_DVE = sum(j[3] == "dve" for j in jobs)
        NNAT = 2 * NBLK * DC
        NST = NNAT // NBLK

        if layer == 0:
            wq = S.sb("wq", [P, DC, D]); wqs = S.sb("wqs", [P, DC, D])
            wd = S.sb("wd", [P, DC, P]); wk = S.sb("wk", [P, D]); wks = S.sb("wks", [P, D]); wv = S.sb("wv", [P, D])
            rope = S.sb("rope", [P, 2, T])
            rt = S.sb("rt", [P, 3, 2, BLK])
            lat = S.sb("lat", [P, T])
        else:
            wqkv = S.sb("wqkv", [P, DC, 3 * D]); w12 = S.sb("w12", [P, DC, P])
            bqk = S.sb("bqk", [P, 4]); bv = S.sb("bv", [P, D])
            jscale = S.sb("jscale", [P, NH, NL]); scale16 = S.sb("scale16", [P, NH]); jsign = S.sb("jsign", [P, NL])
            nat_l = S.sb("nat_l", [96, 4, T], F32R)
            rt = S.sb("rt", [P, 1, 2, BLK])
            points = S.sb("points", [P, 2, TT * 64]); p1 = points[:, 0, :]; p2 = points[:, 1, :]
            coords = S.sb("coords", [P, 2, TT * NH * NL]); la = coords[:, 0, :]; lb = coords[:, 1, :]
            ln2 = S.sb("ln2", [P, P]); lrn = S.sb("lrn", [P, P])
        ident = S.sb("ident", [P, P])
        xin = S.sb("xin", [P, TT, D])
        xT = S.sb("xT", [P, DC, T])
        nat = S.sb("nat", [P, 4, DC, T], F32R)
        values = S.sb("values", [P, NG, TT, HG, 32])
        bank = S.ps("bank", [P, 8, BLK])

        s_w = S.sem("weights_loaded"); s_init = S.sem("constants_set"); s_js = S.sem("line_scales_set")
        s_xin = S.sem("next_tokens_loaded"); s_tr = S.sem("tokens_transposed"); s_te = S.sem("features_ready")
        s_pj = S.sem("projection_ready"); s_pa = S.sem("bank_emptied_by_act"); s_pd = S.sem("bank_emptied_by_dve")
        s_full = S.sem("piece_ready"); s_hi = S.sem("piece_high_ready"); s_nat = S.sem("piece_split"); s_lh = S.sem("line_high_ready")
        s_lv = S.sem("line_steps"); s_lq = S.sem("lines_ready"); s_sq = S.sem("norms_rooted")
        s_qkd = [S.sem(f"pieces_stored{i}") for i in range(NST)]; s_lnd = [S.sem(f"lines_stored{w}") for w in range(2)]
        s_vd = S.sem("values_stored"); s_passed_pool = S.sem("pool_waits_passed")
        block = S.block()

        def full_piece(i):
            return rt[:, 2 if layer == 0 else 0, i % 2, :]

        NW = 8 if layer == 0 else 7
        NLINE = 17

        @block.sync
        def _(sp):
            if layer == 0:
                pairs = [(wq, W["L0_wq"].rearrange("(c p) n -> p c n", p=P)), (wqs, W["L0_wqs"].rearrange("(c p) n -> p c n", p=P)),
                         (wd, W["L0_wd"].rearrange("(c p) n -> p c n", p=P)), (wk, W["L0_wk"]), (wks, W["L0_wks"]),
                         (wv, W["L0_wv"]), (rope, W["rope"].rearrange("k p t -> p k t"))]
            else:
                pairs = [(w12, W["L1_w12"].rearrange("(c p) n -> p c n", p=P)), (wqkv, W["L1_wqkv"].rearrange("(c p) n -> p c n", p=P)),
                         (bqk, W["L1_bqk"]), (bv, W["L1_bv"].partition_broadcast(P)),
                         (scale16, W["L1_pscale"].partition_broadcast(P)), (jsign, W["jsign"])]
            assert len(pairs) == NW - 1
            sp.dma_start(ident[:, :], W["ident"]).then_inc(s_w, 16)
            for dst, src in pairs:
                dst = dst[:, :, :] if len(dst.shape) == 3 else dst[:, :]
                sp.dma_start(dst, src).then_inc(s_w, 16)
            for sem in s_qkd + s_lnd + [s_vd]:
                sp.sem_inc(sem, 16)
            with sp.Fori(0, NBATCH) as b:
                for i in range(NST):
                    c, m = i // 2, 2 * (i % 2)
                    sp.wait_ge(s_nat, b * NNAT + (i + 1) * NBLK)
                    dst = qk_d[b, m:m + 2, c * P:(c + 1) * P, :].rearrange("m p t -> p m t")
                    sp.dma_start(dst, nat[:, m:m + 2, c, :].bitcast(F32)).then_inc(s_qkd[i], 16)
                if layer == 0:
                    sp.wait_ge(s_pa, b * NPJ_ACT + NPJ_ACT)
                else:
                    sp.wait_ge(s_pd, b * NPJ_DVE + TT)
                sp.dma_start(v_d[b].rearrange("g p n -> p g n"), values[:, :, :, :, :].rearrange("p g t h c -> p g (t h c)")).then_inc(s_vd, 16)
                if layer == 1:
                    for w in range(2):
                        sp.wait_ge(s_pd, b * NPJ_DVE + TT + 2 * w + 2)
                        dst = ln_d[b, 2 * w:2 * w + 2].rearrange("m p t -> p m t")
                        sp.dma_start(dst, nat_l[:, 2 * w:2 * w + 2, :].bitcast(F32)).then_inc(s_lnd[w], 16)
            for sem in s_qkd + [s_vd] + (s_lnd if layer == 1 else []):
                sp.wait_ge(sem, 16 * NBATCH + 16)

        @block.gpsimd
        def _(pool):
            def load_tokens(b):
                pool.dma_start(xin[:, :, :], x_in[b].rearrange("(n p) d -> p n d", p=P)).then_inc(s_xin, 16)

            def batch(b, following):
                hold(pool, s_tr, b * 4 + 4, s_passed_pool)
                load_tokens(following)
                i = 0
                for c in range(DC):
                    for m in (0, 2):
                        for n in range(NBLK):
                            pool.wait_ge(s_hi, b * NNAT + i + 1)
                            nc.gpsimd.tensor_tensor(out=nat[:, m + 1, c, n * BLK:(n + 1) * BLK], in0=full_piece(i),
                                                    in1=nat[:, m, c, n * BLK:(n + 1) * BLK].bitcast(F32), op=ALU.subtract).then_inc(s_nat, 1)
                            i += 1

            load_tokens(0)
            nc.gpsimd.memset(values[:, :, :, :, 16:32], 0.0).then_inc(s_init, 1)
            pool.wait_ge(s_init, 1)
            nc.gpsimd.memset(values[:, :, :, :, 16:17], 1.0).then_inc(s_init, 1)
            with pool.Fori(0, NBATCH - 1) as b:
                batch(b, b + 1)
            batch(NBATCH - 1, 0)
            pool.wait_ge(s_xin, 16 * (NBATCH + 1))

        @block.scalar
        def _(act):
            def copy_features(b):
                for k in range(4):
                    act.wait_ge(s_tr, b * 4 + k + 1)
                    nc.scalar.copy(xT[:, k // 2, (k % 2) * BLK:(k % 2 + 1) * BLK], bank[:, 4 + k, :]).then_inc(s_te, 1)

            copy_features(0)
            act.wait_ge(s_w, 16 * NW)
            act.wait_ge(s_init, 2)
            with act.Fori(0, NBATCH) as b:
                na = piece = 0

                def split_high(i):
                    c, m, n = i // 4, 2 * (i // 2 % 2), i % 2
                    if n == 0:
                        act.wait_ge(s_qkd[i // NBLK], b * 16 + 16)
                    act.wait_ge(s_full, b * NNAT + i + 1)
                    nc.scalar.copy(nat[:, m, c, n * BLK:(n + 1) * BLK], full_piece(i)).then_inc(s_hi, 1)

                for r, (kind, i0, i1, eng) in enumerate(jobs):
                    if layer == 0 and kind.endswith("swapped"):
                        split_high(piece)
                        piece += 1
                    if eng == "dve":
                        continue
                    act.wait_ge(s_pj, b * NPJ + r + 1)
                    src = bank[:, r % 4, :]
                    if kind == "lat":
                        nc.scalar.copy(lat[:, i0 * BLK:(i0 + 1) * BLK], src).then_inc(s_pa, 1)
                    elif kind == "v":
                        if i0 == 0:
                            act.wait_ge(s_vd, b * 16 + 16)
                        nc.scalar.copy(values[:, :, i0, :, 0:DH], src[:, 0:D].rearrange("p (g h d) -> p g h d", h=HG, d=DH)).then_inc(s_pa, 1)
                    elif kind == "points":
                        s4 = src.rearrange("p (n w h) -> p n w h", n=4, w=2)
                        for w, dst in enumerate((p1, p2)):
                            ins = nc.scalar.copy(dst[:, i0 * 256:(i0 + 1) * 256].rearrange("p (n h) -> p n h", n=4), s4[:, :, w, :])
                        ins.then_inc(s_pa, 1)
                    else:
                        if piece >= 2:
                            act.wait_ge(s_nat, b * NNAT + piece - 1)
                        col = i1 + (2 if kind == "k" else 0)
                        nc.scalar.activation(full_piece(piece), src, ACT.Identity, bias=bqk[:, col:col + 1]).then_inc(s_full, 1)
                        split_high(piece)
                        piece += 1
                    na += eng == "act"
                assert na == NPJ_ACT
                if layer == 1:
                    act.wait_ge(s_lv, b * NLINE + 9)
                    nc.scalar.activation(lrn[:, :], ln2[:, :], ACT.Sqrt).then_inc(s_sq, 1)
                copy_features(b + 1)
                act.wait_ge(s_nat, b * NNAT + NNAT)

        @block.vector
        def _(dve):
            dve.wait_ge(s_w, 16 * NW)
            dve.wait_ge(s_init, 2)
            if layer == 1:
                for c in range(NL):
                    ins = nc.vector.tensor_scalar(jscale[:, :, c], scale16[:, :], jsign[:, c:c + 1], float(DH) ** 0.5, ALU.mult, ALU.mult)
                ins.then_inc(s_js, 1)
                dve.wait_ge(s_js, 1)
            with dve.Fori(0, NBATCH) as b:
                piece = 0
                nd = 0

                def lines():
                    steps = Steps(dve, s_lv, NLINE, b)
                    dve.wait_ge(s_pa, b * NPJ_ACT + 2)
                    q1 = p1.rearrange("p (n c) -> p n c", c=4)
                    q2 = p2.rearrange("p (n c) -> p n c", c=4)
                    a = la.rearrange("p (n c) -> p n c", c=NL)
                    bb = lb.rearrange("p (n c) -> p n c", c=NL)
                    at_ = 0
                    for i, k in ((0, 3), (1, 2), (2, 1)):
                        for dst, x, y in ((a, q1, q2), (bb, q2, q1)):
                            one = x[:, :, i:i + 1] if k == 1 else x[:, :, i:i + 1].broadcast_to([P, P, k])
                            steps.did(nc.vector.tensor_tensor(out=dst[:, :, at_:at_ + k], in0=one, in1=y[:, :, i + 1:4], op=ALU.mult))
                        at_ += k
                    steps.settled()
                    steps.did(nc.vector.tensor_tensor(out=la, in0=la, in1=lb, op=ALU.subtract))
                    steps.settled()
                    steps.did(nc.vector.tensor_tensor(out=lb, in0=la, in1=la, op=ALU.mult))
                    steps.settled()
                    steps.did(nc.vector.tensor_reduce(out=ln2[:, :], in_=bb, axis=AX.X, op=ALU.add))
                    dve.wait_ge(s_sq, b + 1)
                    steps.did(nc.vector.tensor_scalar(lrn[:, :], lrn[:, :], 1e-12, None, ALU.max))
                    steps.settled()
                    steps.did(nc.vector.reciprocal(ln2[:, :], lrn[:, :]))
                    steps.settled()
                    steps.did(nc.vector.tensor_tensor(out=a, in0=a, in1=ln2[:, :].unsqueeze(2).broadcast_to([P, P, NL]), op=ALU.mult))
                    steps.settled()
                    a4 = la.rearrange("p (n h c) -> p n h c", h=NH, c=NL)
                    b4 = lb.rearrange("p (n h c) -> p n h c", h=NH, c=NL)
                    js = jscale[:, :, :]
                    for c in range(NL - 1):
                        steps.did(nc.vector.tensor_tensor(out=b4[:, :, :, c], in0=a4[:, :, :, NL - 1 - c],
                                                          in1=js[:, :, c].unsqueeze(1).broadcast_to([P, TT, NH]), op=ALU.mult))
                    c = NL - 1
                    nc.vector.tensor_tensor(out=b4[:, :, :, c], in0=a4[:, :, :, NL - 1 - c],
                                            in1=js[:, :, c].unsqueeze(1).broadcast_to([P, TT, NH]), op=ALU.mult).then_inc(s_lq, 1)
                    steps.end()

                for r, (kind, i0, i1, eng) in enumerate(jobs):
                    if eng != "dve":
                        continue
                    if layer == 1 and nd == 0:
                        lines()
                    dve.wait_ge(s_pj, b * NPJ + r + 1)
                    src = bank[:, r % 4, :]
                    if kind in ("q", "k", "q_swapped", "k_swapped"):
                        w = int(kind.endswith("swapped"))
                        nc.vector.tensor_tensor(out=rt[:, w, piece % 2, :], in0=src, in1=rope[:, w, i0 * BLK:(i0 + 1) * BLK],
                                                op=ALU.mult).then_inc(s_pd, 1)
                        if w:
                            if piece >= 2:
                                dve.wait_ge(s_nat, b * NNAT + piece - 1)
                            dve.wait_ge(s_pd, b * NPJ_DVE + nd + 1)
                            nc.vector.tensor_tensor(out=full_piece(piece), in0=rt[:, 0, piece % 2, :], in1=rt[:, 1, piece % 2, :],
                                                    op=ALU.add).then_inc(s_full, 1)
                            piece += 1
                    elif kind == "v":
                        if i0 == 0:
                            dve.wait_ge(s_vd, b * 16 + 16)
                        nc.vector.tensor_tensor(out=values[:, :, i0, :, 0:DH], in0=src[:, 0:D].rearrange("p (g h d) -> p g h d", h=HG, d=DH),
                                                in1=bv[:, :].rearrange("p (g h d) -> p g h d", h=HG, d=DH), op=ALU.add).then_inc(s_pd, 1)
                    else:
                        if i1 == 0:
                            dve.wait_ge(s_lnd[i0], b * 16 + 16)
                        high = nat_l[:, 2 * i0, i1 * BLK:(i1 + 1) * BLK]
                        nc.vector.tensor_copy(high, src[0:96, :]).then_inc(s_lh, 1)
                        dve.wait_ge(s_lh, b * 4 + 2 * i0 + i1 + 1)
                        nc.vector.tensor_tensor(out=nat_l[:, 2 * i0 + 1, i1 * BLK:(i1 + 1) * BLK], in0=src[0:96, :], in1=high.bitcast(F32),
                                                op=ALU.subtract).then_inc(s_pd, 1)
                    nd += 1
                assert nd == NPJ_DVE
                dve.wait_ge(s_nat, b * NNAT + NNAT)

        @block.tensor
        def _(pe):
            pe.wait_ge(s_w, 16 * NW)

            def transpose_tokens(b):
                pe.wait_ge(s_xin, b * 16 + 16)
                for k in range(4):
                    for n in range(4):
                        t = 4 * (k % 2) + n
                        ins = nc.tensor.transpose(bank[:, 4 + k, n * P:(n + 1) * P], xin[:, t, (k // 2) * P:(k // 2 + 1) * P], ident[:, :])
                    ins.then_inc(s_tr, 1)

            transpose_tokens(0)
            with pe.Fori(0, NBATCH) as b:
                pe.wait_ge(s_te, b * 4 + 4)
                emptied = {"act": 0, "dve": 0, "piece": 0}
                users = []

                def all_k(out, pairs):
                    for n, (lhsT, rhs) in enumerate(pairs):
                        ins = nc.tensor.matmul(out, lhsT, rhs, start=(n == 0), stop=(n == len(pairs) - 1))
                    return ins

                lat_done = {}
                for r, (kind, i0, i1, eng) in enumerate(jobs):
                    emptied[eng] += 1
                    users.append((eng, emptied[eng]))
                    if r >= 4:
                        e4, n4 = users[r - 4]
                        if e4 == "act":
                            pe.wait_ge(s_pa, b * NPJ_ACT + n4)
                        elif e4 == "piece":
                            pe.wait_ge(s_full, b * NNAT + n4)
                        else:
                            pe.wait_ge(s_pd, b * NPJ_DVE + n4)
                    if layer == 1 and kind == "lines" and i0 == i1 == 0:
                        transpose_tokens(b + 1)
                    dst = bank[:, r % 4, :]
                    blk = slice(i0 * BLK, (i0 + 1) * BLK)
                    if kind == "lat":
                        lat_done[i0] = emptied["act"]
                        ins = all_k(dst, [(wd[:, kc, :], xT[:, kc, blk]) for kc in range(DC)])
                    elif kind == "points":
                        for n in range(4):
                            tok = slice((4 * i0 + n) * P, (4 * i0 + n + 1) * P)
                            ins = all_k(dst[:, n * P:(n + 1) * P], [(xT[:, kc, tok], w12[:, kc, :]) for kc in range(DC)])
                    elif kind in ("q", "q_swapped", "k", "k_swapped") and (layer == 1 or kind[0] == "q"):
                        if layer == 0:
                            w, o0 = (wq if kind == "q" else wqs), i1 * P
                        else:
                            w, o0 = wqkv, i1 * P + (D if kind == "k" else 0)
                        ins = all_k(dst, [(w[:, kc, o0:o0 + P], xT[:, kc, blk]) for kc in range(DC)])
                    elif kind in ("k", "k_swapped"):
                        pe.wait_ge(s_pa, b * NPJ_ACT + lat_done[i0])
                        w = wk if kind == "k" else wks
                        ins = all_k(dst, [(w[:, i1 * P:(i1 + 1) * P], lat[:, blk])])
                    elif kind == "v":
                        tok = slice(i0 * P, (i0 + 1) * P)
                        if layer == 0:
                            ins = all_k(dst[:, 0:D], [(lat[:, tok], wv[:, :])])
                        else:
                            ins = all_k(dst[:, 0:D], [(xT[:, kc, tok], wqkv[:, kc, 2 * D:3 * D]) for kc in range(DC)])
                    else:
                        pe.wait_ge(s_lq, b + 1)
                        src = la if i0 == 0 else lb
                        for n in range(4):
                            t = 4 * i1 + n
                            ins = nc.tensor.transpose(dst[0:96, n * P:(n + 1) * P], src[:, t * 96:(t + 1) * 96], ident[:, :])
                    ins.then_inc(s_pj, 1)

                if layer == 0:
                    transpose_tokens(b + 1)
                pe.wait_ge(s_pa, b * NPJ_ACT + NPJ_ACT)
                pe.wait_ge(s_pd, b * NPJ_DVE + NPJ_DVE)
                if layer == 1:
                    pe.wait_ge(s_full, b * NNAT + NNAT)


LEAD = 12


def step_offset(i):
    return P * (i if i < 4 else max(0, i - 8))


def places(jobs):
    n = len(jobs)
    return [jobs[k * n // 6:(k + 1) * n // 6] for k in range(6)]


def ring_jobs():
    def maxima(g, following=0):
        return [("max", g, following, j, qt, c) for j in range(HG) for qt in range(TT) for c in range(1 + (qt >= 4))]
    second = maxima(1)
    opening = maxima(0) + second[:2] + [("shift", 0, 0)] + second[2:LEAD]
    line = second[LEAD:]
    for g, following in ((2, 0), (3, 0), (0, 1)):
        more = maxima(g, following)
        prev = ((g - 1) % NG, 0)
        line += more[:2] + [("shift",) + prev] + more[2:]
    more = maxima(1, 1)
    line += more[:2] + [("shift", 0, 1)] + more[2:LEAD]
    steps = 12 * NG

    at = [line[s * len(line) // steps:(s + 1) * len(line) // steps] for s in range(steps)]
    filler = []
    for s in range(steps - 1, steps - 4, -1):
        while at[s] and len(filler) < 6:
            filler.insert(0, at[s].pop())
    for g in range(NG):
        at[12 * g + 6].insert(1, ("sums", 2 * g, 0))
        at[12 * g + 8].insert(2, ("spread", 2 * g, 0))
        if g:
            at[12 * g + 2].insert(1, ("sums", 2 * g - 1, 0))
            at[12 * g + 4].insert(1, ("spread", 2 * g - 1, 0))
    closing = filler[:3] + [("sums", 2 * NG - 1, 0)] + filler[3:] + [("spread", 2 * NG - 1, 0)]
    return opening, at, closing


def attention(nc, layer, W, x_in, x_out, qk_d, ln_d, v_d):
    with Stage(nc, f"at{layer}") as S:
        opening, at, closing = ring_jobs()
        NOPEN = len(opening)
        NR = len([job for jobs in at for job in jobs] + closing)
        NSTEP = 12 * NG
        NPAIR = 2 * NSTEP
        NU = 2 * NG
        NLN = 2 * TT + 1
        SCALE = float(DH) ** -0.5
        NSTK = 8 if layer == 0 else 16
        NW = 2 if layer == 0 else 3

        wo = S.sb("wo", [P, NG, D])
        sel = S.sb("sel", [P, HG]); ident = S.sb("ident", [P, P])
        identb = S.sb("identb", [P, P], BF16); maskT = S.sb("maskT", [P, P], BF16)
        xr = S.sb("xr", [P, TT, D])
        qst = [S.sb(f"qst{g}", [KFULL, HG, T], F32R) for g in range(NG)]
        kst = [S.sb(f"kst{g}", [KFULL, HG, T], F32R) for g in range(NG)]
        vaug = S.sb("vaug", [P, NG, TT, HG, 32])
        probs = S.sb("probs", [P, 4, 2, BLK])
        maskf = probs[:, 0, 0, 0:P]
        o_sb = S.sb("o_sb", [P, 2, BLK])
        rec = S.sb("rec", [P, 4 * HG]); rec_wide = S.sb("rec_wide", [P, BLK])
        oT = S.sb("oT", [P, NG, T])
        if layer == 1:
            bo = S.sb("bo", [P, D])
        mx = S.sb("mx", [P, 2, HG, TT]); mx2 = S.sb("mx2", [P, 2, HG, 4])
        sh = S.sb("sh", [32, 2, P], F32R)
        stats = S.sb("stats", [P, TT, 6]); mv = S.sb("mv", [P, TT, 2]); sd = S.sb("sd", [P, TT]); rstd = S.sb("rstd", [P, TT])
        bank = S.ps("bank", [P, 8, BLK])
        scores = [bank[:, 0:2, :], bank[:, 2:4, :]]
        outputs = bank[:, 4, :]
        NRING = 3

        def ring_bank(r):
            return bank[:, 8 - NRING + r % NRING, :]

        s_w = S.sem("weights_loaded"); s_init = [S.sem(f"constant_rows_set{g}") for g in range(NG)]; s_mask = S.sem("masks_loaded"); s_cast = S.sem("masks_cast")
        s_xr = S.sem("tokens_loaded"); s_bo = S.sem("bias_added")
        s_stk = [S.sem(f"stack_loaded{g}") for g in range(NG)]; s_vl = [S.sem(f"values_loaded{g}") for g in range(NG)]
        s_sh = S.sem("shift_ready"); s_shl = S.sem("shift_loaded")
        s_ring = S.sem("ring_filled"); s_rd = S.sem("ring_emptied"); s_cb = S.sem("maxima_ready"); s_rec = S.sem("reciprocal_steps")
        s_st = S.sem("scores_ready"); s_ex = S.sem("probs_ready"); s_pv = S.sem("values_added"); s_ov = S.sem("output_copied")
        s_wo = S.sem("out_projected"); s_ad = S.sem("residual_added"); s_z = S.sem("ln_steps"); s_sd = S.sem("deviation_ready")
        s_rs = S.sem("rstd_ready"); s_y = S.sem("result_ready"); s_out = S.sem("result_stored")
        s_passed = S.sem("waits_passed"); s_passed_pool = S.sem("pool_waits_passed"); s_passed_dve = S.sem("dve_waits_passed")
        block = S.block()

        def in_batch(jobs, last):
            return [job for job in jobs if not (last and job[2])]

        def ring_order(last):
            return in_batch([job for jobs in at for job in jobs] + closing, last)

        def ring_count(b, r):
            return b * NR + (NOPEN + r + 1)

        def over_batches(eng, batch):
            with eng.Fori(0, NBATCH - 1) as b:
                batch(b, False)
            batch(NBATCH - 1, True)

        @block.sync
        def _(sp):
            def load_stacks(b, g):
                for r, (mq, mk) in enumerate(((0, 2), (0, 3), (1, 2), (1, 3))):
                    for dst, m in ((qst[g], mq), (kst[g], mk)):
                        src = qk_d[b, m, 64 * g:64 * g + 64, :].rearrange("(j p) t -> p j t", j=HG)
                        sp.dma_start(dst[16 * r:16 * r + 16, :, :].bitcast(F32), src).then_inc(s_stk[g], 16)
                        if layer == 1:
                            src = ln_d[b, m, 24 * g:24 * g + 24, :].rearrange("(j p) t -> p j t", j=HG)
                            r0 = LROW + NL * r
                            sp.dma_start(dst[r0:r0 + NL, :, :].bitcast(F32), src).then_inc(s_stk[g], 16)

            def load_values(b, g):
                sp.dma_start(vaug[:, g, :, :, :].rearrange("p t h c -> p (t h c)"), v_d[b, g]).then_inc(s_vl[g], 16)

            def load_shift(g):
                for m in range(2):
                    dst = qst[g][SHROW + m:SHROW + m + 1, :, :].bitcast(F32).rearrange("o j (n t) -> o (j n) t", t=P)
                    sp.dma_start(dst, sh[:, m, :].bitcast(F32)).then_inc(s_shl, 16)

            def load_tokens(b):
                sp.dma_start(xr[:, :, :], x_in[b].rearrange("(n p) d -> p n d", p=P)).then_inc(s_xr, 16)

            sp.dma_start(ident[:, :], W["ident"]).then_inc(s_mask, 16)
            sp.dma_start(maskf, W[f"maskT{layer}"]).then_inc(s_mask, 16)
            for g in range(NG):
                sp.wait_ge(s_init[g], 2)
                load_stacks(0, g)
                if g == 0:
                    sp.dma_start(sel[:, :], W["sel"]).then_inc(s_w, 16)
                    sp.dma_start(wo[:, :, :], W[f"L{layer}_wo"].rearrange("(c p) n -> p c n", p=P)).then_inc(s_w, 16)
                    if layer == 1:
                        sp.dma_start(bo[:, :], W["L1_bout"].partition_broadcast(P)).then_inc(s_w, 16)
                load_values(0, g)
            load_tokens(0)
            sp.wait_ge(s_rd, opening.index(("shift", 0, 0)) + 1)
            load_shift(0)

            def batch(b, last):
                order = ring_order(last)
                for g in range(NG):
                    if g + 1 < NG or not last:
                        job = ("shift", (g + 1) % NG, (g + 1) // NG)
                        sp.wait_ge(s_rd, ring_count(b, order.index(job)))
                        load_shift(job[1])
                    if not last:
                        sp.wait_ge(s_st, b * NPAIR + 24 * (g + 1))
                        load_stacks(b + 1, g)
                        sp.wait_ge(s_pv, b * NSTEP + 12 * (g + 1))
                        load_values(b + 1, g)
                sp.wait_ge(s_y, b * TT + TT)
                sp.dma_start(x_out[b].rearrange("(n p) d -> p n d", p=P), xr[:, :, :]).then_inc(s_out, 16)
                hold(sp, s_out, b * 16 + 16, s_passed)
                if not last:
                    load_tokens(b + 1)

            over_batches(sp, batch)

        @block.gpsimd
        def _(pool):
            for g in range(NG):
                nc.gpsimd.memset(qst[g][LROW:KFULL, :, :].bitcast(F32), 0.0).then_inc(s_init[g], 1)
                if g:
                    nc.gpsimd.memset(kst[g][LROW:KFULL, :, :].bitcast(F32), -1.0).then_inc(s_init[g], 1)
            if layer == 1:
                for g in range(NG):
                    hold(pool, s_init[g], 2, s_passed_pool)
                pool.wait_ge(s_w, 16 * NW)
                with pool.Fori(0, NBATCH) as b:
                    pool.wait_ge(s_xr, b * 16 + 16)
                    for t in range(TT):
                        nc.gpsimd.tensor_tensor(out=xr[:, t, :], in0=xr[:, t, :], in1=bo[:, :], op=ALU.add).then_inc(s_bo, 1)

        @block.scalar
        def _(act):
            def batch(b, last):
                order = ring_order(last)

                def copy_output(u):
                    act.wait_ge(s_pv, b * NSTEP + (u // 2) * 12 + (12 if u % 2 else 4))
                    if u >= 2:
                        act.wait_ge(s_rd, ring_count(b, order.index(("spread", u - 2, 0))))
                    nc.scalar.copy(o_sb[:, u % 2, :], outputs).then_inc(s_ov, 1)

                for s in range(NSTEP):
                    i = s % 12
                    off = step_offset(i)
                    for p in range(2):
                        e = 2 * s + p
                        act.wait_ge(s_st, b * NPAIR + e + 1)
                        if s >= 2:
                            act.wait_ge(s_pv, b * NSTEP + s - 1)
                        nc.scalar.activation(probs[:, e % 4, :, off:], scores[e % 2][:, :, off:], ACT.Exp, scale=SCALE).then_inc(s_ex, 1)
                    if i == 4:
                        copy_output(2 * (s // 12))
                    if i == 0 and s > 0:
                        copy_output(2 * (s // 12) - 1)
                copy_output(NU - 1)
                act.wait_ge(s_z, b * NLN + NLN)
                nc.scalar.activation(sd[:, :], sd[:, :], ACT.Sqrt).then_inc(s_sd, 1)

            act.wait_ge(s_cast, 2)
            over_batches(act, batch)

        @block.vector
        def _(dve):
            nc.vector.memset(kst[0][LROW:KFULL, :, :].bitcast(F32), -1.0).then_inc(s_init[0], 1)
            dve.wait_ge(s_mask, 32)
            nc.vector.tensor_copy(identb[:, :], ident[:, :]).then_inc(s_cast, 1)
            nc.vector.tensor_copy(maskT[:, :], maskf).then_inc(s_cast, 1)

            def ring_job(job, b, through, src):
                if job[0] == "max":
                    _, g, following, j, qt, c = job
                    dve.wait_ge(s_ring, through)
                    w = BLK if (qt >= 4 and c == 0) else P * (qt % 4 + 1)
                    dst = mx2[:, g % 2, j, qt - 4:qt - 3] if c else mx[:, g % 2, j, qt:qt + 1]
                    nc.vector.tensor_reduce(out=dst, in_=src[:, 0:w], axis=AX.X, op=ALU.max).then_inc(s_rd, 1)
                    if (j, qt, c) == (HG - 1, TT - 1, 1):
                        dve.wait_ge(s_rd, through)
                        nc.vector.tensor_tensor(out=mx[:, g % 2, :, 4:8], in0=mx[:, g % 2, :, 4:8], in1=mx2[:, g % 2, :, :],
                                                op=ALU.max).then_inc(s_cb, 1)
                elif job[0] == "shift":
                    n = (b + job[2]) * NG + job[1]
                    dve.wait_ge(s_ring, through)
                    if not isinstance(n, int) or n > 0:
                        dve.wait_ge(s_shl, n * 32)
                    nc.vector.tensor_copy(sh[:, 0, :], src[0:32, 0:P]).then_inc(s_sh, 1)
                    dve.wait_ge(s_sh, n + 1)
                    nc.vector.tensor_tensor(out=sh[:, 1, :], in0=src[0:32, 0:P], in1=sh[:, 0, :].bitcast(F32), op=ALU.subtract).then_inc(s_rd, 1)
                elif job[0] == "sums":
                    u = job[1]
                    dve.wait_ge(s_ring, through)
                    nc.vector.reciprocal(rec[:, :], src[:, 0:4 * HG]).then_inc(s_rec, 1)
                    dve.wait_ge(s_rec, (b * NU + u) * 2 + 1)
                    nc.vector.tensor_copy(rec_wide[:, :].rearrange("p (n k) -> p n k", k=32),
                                          rec[:, :].unsqueeze(2).broadcast_to([P, 4 * HG, 32])).then_inc(s_rec, 1)
                    dve.wait_ge(s_rec, (b * NU + u) * 2 + 2)
                    dve.sem_inc(s_rd, 1)
                else:
                    u = job[1]
                    dve.wait_ge(s_ring, through)
                    nc.vector.tensor_tensor(out=oT[:, u // 2, (u % 2) * BLK:(u % 2 + 1) * BLK], in0=o_sb[:, u % 2, :],
                                            in1=src, op=ALU.mult).then_inc(s_rd, 1)

            for r, job in enumerate(opening):
                ring_job(job, 0, r + 1, bank[:, r % 8, :])

            def batch(b, last):
                for r, job in enumerate(ring_order(last)):
                    ring_job(job, b, ring_count(b, r), ring_bank(r))
                if layer == 0:
                    dve.wait_ge(s_xr, b * 16 + 16)
                else:
                    dve.wait_ge(s_bo, b * TT + TT)
                steps = Steps(dve, s_z, NLN, b)
                for t in range(TT + 1):
                    if t < TT:
                        dve.wait_ge(s_wo, b * TT + t + 1)
                        nc.vector.tensor_tensor(out=xr[:, t, :], in0=bank[:, t % 4, 0:D], in1=xr[:, t, :], op=ALU.add).then_inc(s_ad, 1)
                    if t:
                        dve.wait_ge(s_ad, b * TT + t)
                        steps.did(nc.vector.bn_stats(out=stats[:, t - 1, :], in_=xr[:, t - 1, :]))
                steps.settled(s_passed_dve)
                for t in range(TT):
                    steps.did(nc.vector.bn_aggr(out=mv[:, t, :], in_=stats[:, t, :]))
                steps.settled()
                steps.did(nc.vector.tensor_scalar(sd[:, :], mv[:, :, 1], EPS, None, ALU.add))
                steps.end()
                dve.wait_ge(s_sd, b + 1)
                nc.vector.reciprocal(rstd[:, :], sd[:, :]).then_inc(s_rs, 1)
                dve.wait_ge(s_rs, b + 1)
                for t in range(TT):
                    nc.vector.tensor_scalar(xr[:, t, :], xr[:, t, :], mv[:, t, 0:1], rstd[:, t:t + 1], ALU.subtract, ALU.mult).then_inc(s_y, 1)

            over_batches(dve, batch)

        @block.tensor
        def _(pe):
            def ring_job(job, b, through, dst):
                if job[0] == "max":
                    _, g, following, j, qt, c = job
                    if j == 0 and qt == 0:
                        pe.wait_ge(s_stk[g], (b + following) * (NSTK * 16) + NSTK * 16)
                    w = BLK if (qt >= 4 and c == 0) else P * (qt % 4 + 1)
                    diag = qt < 4 or c == 1
                    ins = nc.tensor.matmul(dst[:, 0:w], qst[g][0:SHROW, j, qt * P:(qt + 1) * P],
                                           kst[g][0:SHROW, j, c * BLK:c * BLK + w], start=True, stop=not diag)
                    if diag:
                        ins = nc.tensor.matmul(dst[:, w - P:w], maskT[:, :], identb[:, :], start=False, stop=True)
                elif job[0] == "shift":
                    pe.wait_ge(s_cb, (b + job[2]) * NG + job[1] + 1)
                    ins = nc.tensor.transpose(dst[0:32, 0:P], mx[:, job[1] % 2, :, :].rearrange("p j n -> p (j n)"), ident[:, :])
                elif job[0] == "sums":
                    pe.wait_ge(s_ov, b * NU + job[1] + 1)
                    for n in range(4):
                        ins = nc.tensor.matmul(dst[:, n * HG:(n + 1) * HG], o_sb[:, job[1] % 2, n * P:(n + 1) * P], sel[:, :],
                                               start=True, stop=True)
                else:
                    pe.wait_ge(s_rec, (b * NU + job[1]) * 2 + 2)
                    for n in range(4):
                        ins = nc.tensor.transpose(dst[:, n * P:(n + 1) * P], rec_wide[:, n * P:(n + 1) * P], ident[:, :])
                ins.then_inc(s_ring, 1)

            pe.wait_ge(s_cast, 2)
            for r, job in enumerate(opening):
                if r >= 8:
                    pe.wait_ge(s_rd, r - 7)
                ring_job(job, 0, r + 1, bank[:, r % 8, :])
            pe.wait_ge(s_w, 16 * NW)
            pe.wait_ge(s_rd, NOPEN)

            def batch(b, last):
                ring = [0]

                def ring_jobs_now(jobs):
                    for job in jobs:
                        r = ring[0]
                        ring[0] += 1
                        pe.wait_ge(s_rd, ring_count(b, r - NRING if r >= NRING else -1))
                        ring_job(job, b, ring_count(b, r), ring_bank(r))

                def step_of(s):
                    i = s % 12
                    qb, kt = (0, i) if i < 4 else (1, i - 4)
                    return s // 12, qb, kt, P * max(0, kt - 4 * qb)

                def score(s, j):
                    g, qb, kt, off = step_of(s)
                    e = 2 * s + j // 2
                    if j % 2 == 0 and e >= 2:
                        pe.wait_ge(s_ex, b * NPAIR + e - 1)
                    dst = scores[e % 2][:, j % 2, :]
                    diag = kt >= 4 * qb
                    ins = nc.tensor.matmul(dst[:, off:], kst[g][0:KFULL, j, kt * P:(kt + 1) * P],
                                           qst[g][0:KFULL, j, qb * BLK + off:(qb + 1) * BLK], start=True, stop=not diag)
                    if diag:
                        ins = nc.tensor.matmul(dst[:, off:off + P], identb[:, :], maskT[:, :], start=False, stop=True)
                    if j % 2 == 1:
                        ins.then_inc(s_st, 1)

                def values(s, half):
                    g, qb, kt, off = step_of(s)
                    u = 2 * g + qb
                    if half == 0:
                        if kt == 0 and qb == 0:
                            pe.wait_ge(s_vl[g], b * 16 + 16)
                        if kt == 0 and u >= 1:
                            pe.wait_ge(s_ov, b * NU + u)
                        pe.wait_ge(s_ex, b * NPAIR + 2 * s + 2)
                    for j in (2 * half, 2 * half + 1):
                        e = 2 * s + j // 2
                        ins = nc.tensor.matmul(bank[32 * j:32 * j + 32, 4, off:], vaug[:, g, kt, j, :],
                                               probs[:, e % 4, j % 2, off:], start=(kt == 0), stop=(kt == 4 * qb + 3))
                    if half == 1:
                        ins.then_inc(s_pv, 1)

                for s in range(NSTEP):
                    if s % 12 == 0:
                        pe.wait_ge(s_shl, (b * NG + s // 12) * 32 + 32)
                    now = places(in_batch(at[s], last))
                    for k in range(6):
                        if k < 4:
                            score(s, k)
                        elif s:
                            values(s - 1, k - 4)
                        ring_jobs_now(now[k])
                for half in range(2):
                    values(NSTEP - 1, half)
                ring_jobs_now(in_batch(closing, last))
                assert ring[0] == len(ring_order(last))

                pe.wait_ge(s_ex, b * NPAIR + NPAIR)
                pe.wait_ge(s_rd, ring_count(b, ring[0] - 1))
                for t in range(TT):
                    if t >= 4:
                        pe.wait_ge(s_ad, b * TT + t - 3)
                    for g in range(NG):
                        ins = nc.tensor.matmul(bank[:, t % 4, 0:D], oT[:, g, t * P:(t + 1) * P], wo[:, g, :], start=(g == 0), stop=(g == NG - 1))
                    ins.then_inc(s_wo, 1)
                pe.wait_ge(s_ad, b * TT + TT)

            over_batches(pe, batch)


def mixture_of_depths(nc, W, x_in, x_out, score_d):
    with Stage(nc, "mod") as S:
        w1 = S.sb("w1", [P, DC, FF]); w2 = S.sb("w2", [P, FC, D])
        b1 = S.sb("b1", [P, FC]); b2 = S.sb("b2", [P, D]); wr = S.sb("wr", [P, D])
        ident = S.sb("ident", [P, P]); before = S.sb("before", [P, T])
        w1p = S.sb("w1p", [P, 2, DC, FF], F32R); w2p = S.sb("w2p", [P, 2, FC, D], F32R)
        xTp = S.sb("xTp", [P, 2, DC, T], F32R); hidp = S.sb("hidp", [P, 2, NBLK, FC, BLK], F32R)
        gelu = S.sb("gelu", [P, 4, BLK])
        xr = S.sb("xr", [P, TT, D]); x2 = S.sb("x2", [P, TT, D])
        prod = S.sb("prod", [P, TT, D])
        z = S.sb("z", [P, TT, D])
        sc = S.sb("sc", [P, TT]); scT = S.sb("scT", [TT, P]); row = S.sb("row", [P, T]); hit = S.sb("hit", [P, T])
        above = S.sb("above", [P, TT]); ties = S.sb("ties", [P, TT]); sig = S.sb("sig", [P, TT]); gate = S.sb("gate", [P, TT])
        stats = S.sb("stats", [P, TT, 6]); mv = S.sb("mv", [P, TT, 2]); sd = S.sb("sd", [P, TT]); rstd = S.sb("rstd", [P, TT])
        bank = S.ps("bank", [P, 8, BLK])
        NW = 7
        NH1 = NBLK * FC
        NSC = TT
        SCORES_AT = FC - 3
        UPDATE_BANKS = (4, 5, 7)
        NRK = 2 * TT + 3
        NZ = 4 * TT + 1
        s_w = S.sem("weights_loaded"); s_xr = S.sem("tokens_loaded")
        s_x2 = S.sem("doubled"); s_sc = S.sem("scores_ready"); s_sct = S.sem("scores_transposed"); s_scc = S.sem("score_row_copied")
        s_scd = S.sem("score_row_stored"); s_row = S.sem("score_row_loaded"); s_rk = S.sem("rank_steps"); s_sig = S.sem("sigmoid_ready")
        s_wh = S.sem("weights_high_ready"); s_wl = S.sem("weights_low_ready")
        s_h = S.sem("hidden_ready"); s_ge = S.sem("gelu_ready"); s_gh = S.sem("hidden_high_ready"); s_gl = S.sem("hidden_split")
        s_tl = S.sem("features_split")
        s_o = S.sem("update_ready"); s_z = S.sem("ln_steps")
        s_sd = S.sem("deviation_ready"); s_rs = S.sem("rstd_ready"); s_y = S.sem("result_ready"); s_passed = S.sem("waits_passed")
        s_tr = S.sem("tokens_transposed"); s_te = S.sem("features_ready"); s_out = S.sem("result_stored")
        block = S.block()

        def update_bank(t):
            return bank[:, UPDATE_BANKS[t % len(UPDATE_BANKS)], 0:D]

        @block.sync
        def _(sp):
            def load_tokens(b):
                sp.dma_start(xr[:, :, :], x_in[b].rearrange("(n p) d -> p n d", p=P)).then_inc(s_xr, 16)

            sp.dma_start(ident[:, :], W["ident"]).then_inc(s_w, 16)
            load_tokens(0)
            sp.dma_start(w1[:, :, :], W["m_w1"].rearrange("(c p) n -> p c n", p=P)).then_inc(s_w, 16)
            sp.dma_start(w2[:, :, :], W["m_w2"].rearrange("(c p) n -> p c n", p=P)).then_inc(s_w, 16)
            sp.dma_start(b1[:, :], W["m_b1T"]).then_inc(s_w, 16)
            sp.dma_start(b2[:, :], W["m_b2"].partition_broadcast(P)).then_inc(s_w, 16)
            sp.dma_start(wr[:, :], W["m_wr"].partition_broadcast(P)).then_inc(s_w, 16)
            sp.dma_start(before[:, :], W["before"]).then_inc(s_w, 16)
            sp.sem_inc(s_out, 16)

            def batch(b, following):
                sp.wait_ge(s_scc, b + 1)
                sp.dma_start(score_d[b].rearrange("(n p) -> n p", p=P), scT[:, :]).then_inc(s_scd, 16)
                sp.wait_ge(s_scd, b * 16 + 16)
                sp.dma_start(row[:, :], score_d[b].partition_broadcast(P)).then_inc(s_row, 16)
                sp.wait_ge(s_x2, b + 1)
                sp.wait_ge(s_tr, b * 4 + 4)
                load_tokens(following)
                sp.wait_ge(s_y, b * TT + TT)
                sp.dma_start(x_out[b].rearrange("(n p) d -> p n d", p=P), z[:, :, :]).then_inc(s_out, 16)

            with sp.Fori(0, NBATCH - 1) as b:
                batch(b, b + 1)
            batch(NBATCH - 1, 0)
            sp.wait_ge(s_xr, (NBATCH + 1) * 16)
            sp.wait_ge(s_out, NBATCH * 16 + 16)

        @block.gpsimd
        def _(pool):
            with pool.Fori(0, NBATCH) as b:
                for q in range(NH1):
                    if q == NH1 // 2:
                        pool.wait_ge(s_xr, b * 16 + 16)
                        nc.gpsimd.tensor_tensor(out=x2[:, :, :], in0=xr[:, :, :], in1=xr[:, :, :], op=ALU.add).then_inc(s_x2, 1)
                    pool.wait_ge(s_gh, b * NH1 + q + 1)
                    nc.gpsimd.tensor_tensor(out=hidp[:, 1, q // FC, q % FC, :], in0=gelu[:, q % 4, :],
                                            in1=hidp[:, 0, q // FC, q % FC, :].bitcast(F32), op=ALU.subtract).then_inc(s_gl, 1)
                pool.wait_ge(s_z, b * NZ + NZ)

        @block.scalar
        def _(act):
            def copy_features(b):
                for k in range(4):
                    act.wait_ge(s_tr, b * 4 + k + 1)
                    nc.scalar.copy(xTp[:, 0, k // 2, (k % 2) * BLK:(k % 2 + 1) * BLK], bank[:, k, :]).then_inc(s_te, 1)

            copy_features(0)
            act.wait_ge(s_w, 16 * NW)
            nc.scalar.copy(w1p[:, 0, :, :], w1[:, :, :]).then_inc(s_wh, 1)
            nc.scalar.copy(w2p[:, 0, :, :], w2[:, :, :]).then_inc(s_wh, 1)
            with act.Fori(0, NBATCH) as b:
                act.wait_ge(s_sc, b * NSC + NSC)
                nc.scalar.activation(sig[:, :], sc[:, :], ACT.Sigmoid).then_inc(s_sig, 1)
                for q in range(NH1 + 1):
                    if q < NH1:
                        if q >= 4:
                            act.wait_ge(s_gl, b * NH1 + q - 3)
                        act.wait_ge(s_h, b * NH1 + q + 1)
                        nc.scalar.activation(gelu[:, q % 4, :], bank[:, q % 4, :], ACT.Gelu_apprx_tanh,
                                             bias=b1[:, q % FC:q % FC + 1]).then_inc(s_ge, 1)
                    if q:
                        act.wait_ge(s_ge, b * NH1 + q)
                        nc.scalar.copy(hidp[:, 0, (q - 1) // FC, (q - 1) % FC, :], gelu[:, (q - 1) % 4, :]).then_inc(s_gh, 1)
                copy_features(b + 1)
                act.wait_ge(s_z, b * NZ + NZ)
                nc.scalar.activation(sd[:, :], sd[:, :], ACT.Sqrt).then_inc(s_sd, 1)

        @block.vector
        def _(dve):
            def split_features(b):
                for k in range(4):
                    c, blk = k // 2, slice((k % 2) * BLK, (k % 2 + 1) * BLK)
                    dve.wait_ge(s_te, b * 4 + k + 1)
                    nc.vector.tensor_tensor(out=xTp[:, 1, c, blk], in0=bank[:, k, :], in1=xTp[:, 0, c, blk].bitcast(F32),
                                            op=ALU.subtract).then_inc(s_tl, 1)

            split_features(0)
            dve.wait_ge(s_w, 16 * NW)
            for n, (full, parts) in enumerate(((w1, w1p), (w2, w2p))):
                dve.wait_ge(s_wh, n + 1)
                nc.vector.tensor_tensor(out=parts[:, 1, :, :], in0=full[:, :, :], in1=parts[:, 0, :, :].bitcast(F32), op=ALU.subtract).then_inc(s_wl, 1)
            with dve.Fori(0, NBATCH) as b:
                dve.wait_ge(s_xr, b * 16 + 16)
                for t in range(TT):
                    nc.vector.tensor_tensor_reduce(out=prod[:, t, :], in0=xr[:, t, :], in1=wr[:, :], scale=1.0, scalar=0.0,
                                                   op0=ALU.mult, op1=ALU.add, accum_out=sc[:, t:t + 1]).then_inc(s_sc, 1)
                dve.wait_ge(s_sct, b + 1)
                nc.vector.tensor_copy(scT[:, :], bank[0:TT, 6, 0:P]).then_inc(s_scc, 1)
                dve.wait_ge(s_row, b * 16 + 16)
                steps = Steps(dve, s_rk, NRK, b)
                for t in range(TT):
                    steps.settled()
                    steps.did(nc.vector.tensor_scalar(hit[:, :], row[:, :], sc[:, t:t + 1], 0.0, ALU.is_gt, ALU.add,
                                                      accum_out=above[:, t:t + 1]))
                    steps.settled()
                    n = P * (t + 1)
                    steps.did(nc.vector.scalar_tensor_tensor(out=hit[:, 0:n], in0=row[:, 0:n], scalar=sc[:, t:t + 1],
                                                             in1=before[:, T - n:T], op0=ALU.is_equal, op1=ALU.mult,
                                                             accum_out=ties[:, t:t + 1]))
                steps.settled()
                steps.did(nc.vector.tensor_tensor(out=above[:, :], in0=above[:, :], in1=ties[:, :], op=ALU.add))
                steps.settled()
                steps.did(nc.vector.tensor_scalar(above[:, :], above[:, :], float(TOPK), None, ALU.is_lt))
                steps.settled()
                dve.wait_ge(s_sig, b + 1)
                steps.did(nc.vector.tensor_tensor(out=gate[:, :], in0=above[:, :], in1=sig[:, :], op=ALU.mult))
                steps.settled()
                steps.end()
                dve.wait_ge(s_x2, b + 1)
                dve.wait_ge(s_out, b * 16 + 16)
                steps = Steps(dve, s_z, NZ, b)
                for t in range(TT):
                    if t == TT - 2:
                        split_features(b + 1)
                    dve.wait_ge(s_o, b * TT + t + 1)
                    steps.did(nc.vector.tensor_tensor(out=z[:, t, :], in0=update_bank(t), in1=b2[:, :], op=ALU.add))
                    steps.settled()
                    steps.did(nc.vector.scalar_tensor_tensor(out=z[:, t, :], in0=z[:, t, :], scalar=gate[:, t:t + 1], in1=x2[:, t, :],
                                                             op0=ALU.mult, op1=ALU.add))
                steps.settled()
                for t in range(TT):
                    steps.did(nc.vector.bn_stats(out=stats[:, t, :], in_=z[:, t, :]))
                steps.settled(s_passed)
                for t in range(TT):
                    steps.did(nc.vector.bn_aggr(out=mv[:, t, :], in_=stats[:, t, :]))
                steps.settled()
                steps.did(nc.vector.tensor_scalar(sd[:, :], mv[:, :, 1], EPS, None, ALU.add))
                steps.end()
                dve.wait_ge(s_sd, b + 1)
                nc.vector.reciprocal(rstd[:, :], sd[:, :]).then_inc(s_rs, 1)
                dve.wait_ge(s_rs, b + 1)
                for t in range(TT):
                    nc.vector.tensor_scalar(z[:, t, :], z[:, t, :], mv[:, t, 0:1], rstd[:, t:t + 1], ALU.subtract, ALU.mult).then_inc(s_y, 1)

        @block.tensor
        def _(pe):
            def transpose_tokens(b):
                pe.wait_ge(s_xr, b * 16 + 16)
                for k in range(4):
                    for n in range(4):
                        t = 4 * (k % 2) + n
                        ins = nc.tensor.transpose(bank[:, k, n * P:(n + 1) * P], xr[:, t, (k // 2) * P:(k // 2 + 1) * P], ident[:, :])
                    ins.then_inc(s_tr, 1)

            pe.wait_ge(s_w, 16 * NW)
            transpose_tokens(0)
            pe.wait_ge(s_wl, 2)
            with pe.Fori(0, NBATCH) as b:
                pe.wait_ge(s_tl, b * 4 + 4)
                for n in range(NBLK):
                    for f in range(FC):
                        q = n * FC + f
                        if q >= 4:
                            pe.wait_ge(s_ge, b * NH1 + q - 3)
                        for kc in range(DC):
                            for pw, px in PARTS:
                                ins = nc.tensor.matmul(bank[:, q % 4, :], w1p[:, pw, kc, f * P:(f + 1) * P], xTp[:, px, kc, n * BLK:(n + 1) * BLK],
                                                       start=(kc == 0 and (pw, px) == PARTS[0]), stop=(kc == DC - 1 and (pw, px) == PARTS[-1]))
                        ins.then_inc(s_h, 1)
                        if n == 0 and f == SCORES_AT:
                            pe.wait_ge(s_sc, b * NSC + NSC)
                            nc.tensor.transpose(bank[0:TT, 6, 0:P], sc[:, :], ident[:, :]).then_inc(s_sct, 1)
                for t in range(TT):
                    if t == TT - 2:
                        pe.wait_ge(s_ge, b * NH1 + NH1)
                        transpose_tokens(b + 1)
                    pe.wait_ge(s_gl, b * NH1 + FC * (t // 4 + 1))
                    if t >= len(UPDATE_BANKS):
                        pe.wait_ge(s_z, b * NZ + 2 * (t - len(UPDATE_BANKS)) + 1)
                    for f in range(FC):
                        for px, pw in PARTS:
                            ins = nc.tensor.matmul(update_bank(t), hidp[:, px, t // 4, f, (t % 4) * P:(t % 4 + 1) * P], w2p[:, pw, f, :],
                                                   start=(f == 0 and (px, pw) == PARTS[0]), stop=(f == FC - 1 and (px, pw) == PARTS[-1]))
                    ins.then_inc(s_o, 1)


def experts(nc, W, x_in, out, sorted_d, result_d):
    with Stage(nc, "moe") as S:
        NTE = NTILE * NE
        cT = S.sb("cT", [P, DC, NE])
        ident = S.sb("ident", [P, P])
        upper_f = S.sb("upper_f", [P, P]); upper = S.sb("upper", [P, P], BF16); ones = S.sb("ones", [P, P], BF16)
        rev = S.sb("rev", [P, NE])
        not_first = S.sb("not_first", [P, NTE])
        firsts = S.sb("firsts", [P, NTILE])
        numbers = S.sb("numbers", [P, NSLOT])
        x = S.sb("x", [P, NTILE, D])
        xn = S.sb("xn", [P, NTILE, D])
        xT = [S.sb(f"xT{i}", [P, DC, T]) for i in range(2)]
        zero = S.sb("zero", [P, D])
        aff = S.sb("aff", [P, NTE]); eq = S.sb("eq", [P, NTE]); own = S.sb("own", [P, NTE]); ownb = S.sb("ownb", [P, NTE], BF16)
        best = S.sb("best", [P, NTILE]); pick = S.sb("pick", [P, NTILE]); alpha = S.sb("alpha", [P, NTILE])
        count = S.sb("count", [P, NTE]); cum = S.sb("cum", [P, NTE]); over = S.sb("over", [P, NTE]); pos = S.sb("pos", [P, NTE])
        tiles = S.sb("tiles", [P, NE]); ends = S.sb("ends", [P, NE]); base = S.sb("base", [P, NE])
        slot_f = S.sb("slot_f", [P, NTILE]); slot = S.sb("slot", [P, NTILE], I32)
        past = S.sb("past", [1, NSLOT * NE]); eid_f = S.sb("eid_f", [1, NSLOT]); eid = S.sb("eid", [1, NSLOT], I32)
        stats = S.sb("stats", [P, NTILE, 6]); mv = S.sb("mv", [P, NTILE, 2]); sd = S.sb("sd", [P, NTILE]); rstd = S.sb("rstd", [P, NTILE])
        off = S.sb("off", [P, NTILE])
        w1 = [S.sb(f"w1_{i}", [P, DC, FF]) for i in range(2)]
        w2 = [S.sb(f"w2_{i}", [P, FC, D]) for i in range(2)]
        small = [S.sb(f"small{i}", [P, FC + 2 * DC]) for i in range(2)]
        b2 = [S.sb(f"b2_{i}", [P, D]) for i in range(2)]
        xs = [S.sb(f"xs{i}", [P, SUB, D]) for i in range(2)]
        xsT = [S.sb(f"xsT{i}", [P, DC, TS]) for i in range(2)]
        hid = [S.sb(f"hid{i}", [P, FC, TS]) for i in range(2)]
        ys = [S.sb(f"ys{i}", [P, SUB, D]) for i in range(2)]
        bank = S.ps("bank", [P, 8, BLK])

        NC = 7
        TURNS = (NSLOT - 2) // 2
        GRP = 8
        NGR = NTILE // GRP
        s_c = S.sem("constants_loaded"); s_cb = S.sem("constants_cast"); s_x = [S.sem(f"tokens_loaded{b}") for b in range(NBATCH)]
        s_xtr = S.sem("tokens_transposed"); s_xt = S.sem("features_ready"); s_zero = S.sem("zeros_set"); s_zd = S.sem("slots_zeroed")
        s_aff = S.sem("affinities_ready"); s_r = S.sem("route_steps"); s_best = S.sem("best_ready"); s_alpha = S.sem("alpha_ready")
        s_own = S.sem("own_ready"); s_cnt = S.sem("counts_ready"); s_slot = S.sem("slots_ready"); s_eid = S.sem("tile_experts_ready")
        s_n = S.sem("norm_steps"); s_sd = S.sem("deviation_ready"); s_xn = S.sem("normalised"); s_sc = S.sem("scattered"); s_x2 = S.sem("doubled")
        s_w1 = [S.sem(f"first_weights_loaded{i}") for i in range(2)]; s_w2 = [S.sem(f"second_weights_loaded{i}") for i in range(2)]
        s_sm = [S.sem(f"small_weights_loaded{i}") for i in range(2)]; s_xs = [S.sem(f"slots_loaded{i}") for i in range(2)]
        s_t = S.sem("slots_transposed"); s_xg = S.sem("slot_features_ready")
        s_h = S.sem("hidden_ready"); s_ra = S.sem("relu_by_act"); s_rv = S.sem("relu_by_dve")
        s_o = S.sem("slot_result_ready"); s_ys = S.sem("slot_result_biased"); s_yd = [S.sem(f"slot_result_stored{i}") for i in range(2)]
        s_g = [S.sem(f"gathered{i}") for i in range(NGR)]; s_f = S.sem("final_steps"); s_fsd = S.sem("final_deviation_ready")
        s_fy = S.sem("final_ready"); s_fya = S.sem("final_ready_by_act"); s_passed = S.sem("waits_passed"); s_passed_pool = S.sem("pool_waits_passed"); s_frs = S.sem("final_rstd_ready"); s_out = S.sem("result_stored")
        block = S.block()

        def te(t):
            return t[:, :].rearrange("p (t e) -> p t e", e=NE)

        def et(t):
            return t[:, :].rearrange("p (e t) -> p e t", e=NE)

        def swapped(t):
            return t[:, :].rearrange("p (e t) -> p t e", e=NE)

        def slot_tiles(eng, body):
            with eng.Fori(0, TURNS) as turn:
                for i in range(2):
                    body(2 * turn + i, turn, i, True, True)
            for j in range(2 * TURNS, NSLOT):
                body(j, j // 2, j % 2, j + 1 < NSLOT, j + 2 < NSLOT)

        def hidden_bank(f):
            return bank[:, f // 2, (f % 2) * TS:(f % 2 + 1) * TS]

        @block.sync
        def _(sp):
            sp.dma_start(ident[:, :], W["ident"]).then_inc(s_c, 16)
            sp.dma_start(cT[:, :, :], W["e_cT"].rearrange("(c p) e -> p c e", p=P)).then_inc(s_c, 16)
            for b in range(NBATCH):
                sp.dma_start(x[:, TT * b:TT * b + TT, :], x_in[b].rearrange("(n p) d -> p n d", p=P)).then_inc(s_x[b], 16)
            for dst, src in ((upper_f[:, :], W["upper"]), (rev[:, :], W["rev"]), (not_first[:, :], W["not_first"]),
                             (firsts[:, :], W["firsts"]), (numbers[:, :], W["numbers"])):
                sp.dma_start(dst, src).then_inc(s_c, 16)
            sp.wait_ge(s_zero, 1)
            slots = sorted_d.rearrange("(n p) d -> p n d", p=P)
            sp.dma_start(slots, zero[:, :].unsqueeze(1).broadcast_to([P, NSLOT * SUB, D])).then_inc(s_zd, 16)

            def expert_of(j):
                return sp.value_load(eid[0:1, bass.ds(j, 1)], min_val=0, max_val=NE - 1)

            def load_first(e, i):
                sp.dma_start(small[i][:, :], W["e_small"][e]).then_inc(s_sm[i], 16)
                sp.dma_start(w1[i][:, :, :], W["e_w1T"][e].rearrange("(c p) n -> p c n", p=P)).then_inc(s_w1[i], 16)

            def load_second(e, i):
                sp.dma_start(w2[i][:, :, :], W["e_w2T"][e].rearrange("(c p) n -> p c n", p=P)).then_inc(s_w2[i], 16)
                sp.dma_start(b2[i][:, :], W["e_b2"][e].partition_broadcast(P)).then_inc(s_w2[i], 16)

            for i in range(2):
                sp.sem_inc(s_yd[i], 16)
            sp.wait_ge(s_eid, 1)
            for j in range(2):
                e = expert_of(j)
                load_first(e, j)
                load_second(e, j)

            def tile(j, turn, i, following, second):
                if second:
                    e = expert_of(j + 2)
                    sp.wait_ge(s_ra, 4 * j + 4)
                    hold(sp, s_rv, 4 * j + 4, s_passed)
                    load_first(e, i)
                hold(sp, s_ys, j + 1, s_passed)
                sp.dma_start(result_d[bass.ds(j * TS, TS), :].rearrange("(n p) d -> p n d", p=P), ys[i][:, :, :]).then_inc(s_yd[i], 16)
                if second:
                    load_second(e, i)

            slot_tiles(sp, tile)
            for gr in range(NGR):
                sp.wait_ge(s_fy, GRP // 2 * (gr + 1))
                sp.wait_ge(s_fya, GRP // 2 * (gr + 1))
                tok = out.rearrange("b (n p) d -> (b n) p d", p=P)[GRP * gr:GRP * (gr + 1)].rearrange("n p d -> p n d")
                sp.dma_start(tok, xn[:, GRP * gr:GRP * (gr + 1), :]).then_inc(s_out, 16)
            sp.wait_ge(s_out, 16 * NGR)

        @block.gpsimd
        def _(pool):
            nc.gpsimd.memset(zero[:, :], 0.0).then_inc(s_zero, 1)
            pool.wait_ge(s_slot, 1)
            pool.wait_ge(s_zd, 16)
            pool.wait_ge(s_xn, NTILE)
            for t in range(NTILE):
                nc.gpsimd.indirect_dma_start(out=sorted_d[:, :], out_offset=bass.IndirectOffsetOnAxis(ap=slot[:, t:t + 1], axis=0),
                                             in_=xn[:, t, :], in_offset=None).then_inc(s_sc, 16)
            pool.wait_ge(s_sc, 16 * NTILE)

            def load_slots(j, i):
                pool.dma_start(xs[i][:, :, :], sorted_d[bass.ds(j * TS, TS), :].rearrange("(n p) d -> p n d", p=P)).then_inc(s_xs[i], 16)

            for i in range(2):
                load_slots(i, i)
            nc.gpsimd.tensor_tensor(out=x[:, :, :], in0=x[:, :, :], in1=x[:, :, :], op=ALU.add).then_inc(s_x2, 1)

            def tile(j, turn, i, following, second):
                if second:
                    hold(pool, s_t, j + 1, s_passed_pool)
                    load_slots(j + 2, i)

            slot_tiles(pool, tile)
            for i in range(2):
                pool.wait_ge(s_yd[i], 16 * ((NSLOT + 1 - i) // 2) + 16)
            for t in range(NTILE):
                nc.gpsimd.indirect_dma_start(out=xn[:, t, :], out_offset=None, in_=result_d[:, :],
                                             in_offset=bass.IndirectOffsetOnAxis(ap=slot[:, t:t + 1], axis=0)).then_inc(s_g[t // GRP], 16)

        @block.scalar
        def _(act):
            for b in range(NBATCH):
                if b >= 2:
                    act.wait_ge(s_aff, b - 1)
                for k in range(4):
                    act.wait_ge(s_xtr, 4 * b + k + 1)
                    nc.scalar.copy(xT[b % 2][:, k // 2, (k % 2) * BLK:(k % 2 + 1) * BLK], bank[:, 4 + k, :]).then_inc(s_xt, 1)
            act.wait_ge(s_n, 2 * NTILE + 1)
            nc.scalar.activation(sd[:, :], sd[:, :], ACT.Sqrt).then_inc(s_sd, 1)
            act.wait_ge(s_best, 1)
            nc.scalar.activation(alpha[:, :], best[:, :], ACT.Sigmoid).then_inc(s_alpha, 1)

            def tile(j, turn, i, following, second):
                act.wait_ge(s_sm[i], 16 * turn + 16)
                for f in range(FC // 2):
                    if f % 2 == 0:
                        act.wait_ge(s_h, 4 * j + f // 2 + 1)
                    nc.scalar.activation(hid[i][:, f, :], hidden_bank(f), ACT.Relu, bias=small[i][:, f:f + 1]).then_inc(s_ra, 1)

            slot_tiles(act, tile)
            for gr in range(NGR):
                act.wait_ge(s_f, (gr + 1) * (3 * GRP + 1))
                part = sd[:, GRP * gr:GRP * (gr + 1)]
                nc.scalar.activation(part, part, ACT.Sqrt).then_inc(s_fsd, 1)
                act.wait_ge(s_frs, 2 * gr + 2)
                for t in range(GRP * gr + GRP // 2, GRP * (gr + 1)):
                    nc.scalar.activation(xn[:, t, :], xn[:, t, :], ACT.Identity, bias=off[:, t:t + 1], scale=rstd[:, t:t + 1]).then_inc(s_fya, 1)

        @block.vector
        def _(dve):
            dve.wait_ge(s_c, 16 * NC)
            nc.vector.tensor_copy(upper[:, :], upper_f[:, :]).then_inc(s_cb, 1)
            nc.vector.memset(ones[:, :], 1.0).then_inc(s_cb, 1)
            steps = Steps(dve, s_n, 2 * NTILE + 1, 0)
            for t in range(NTILE):
                dve.wait_ge(s_x[t // TT], 16)
                steps.did(nc.vector.bn_stats(out=stats[:, t, :], in_=x[:, t, :]))
            steps.settled()
            for t in range(NTILE):
                steps.did(nc.vector.bn_aggr(out=mv[:, t, :], in_=stats[:, t, :]))
            steps.settled()
            steps.did(nc.vector.tensor_scalar(sd[:, :], mv[:, :, 1], EPS, None, ALU.add))
            steps.end()

            steps = Steps(dve, s_r, 21, 0)
            dve.wait_ge(s_sd, 1)
            steps.did(nc.vector.reciprocal(rstd[:, :], sd[:, :]))
            steps.settled()
            for t in range(NTILE):
                nc.vector.tensor_scalar(xn[:, t, :], x[:, t, :], mv[:, t, 0:1], rstd[:, t:t + 1], ALU.subtract, ALU.mult).then_inc(s_xn, 1)
            dve.wait_ge(s_aff, NBATCH)
            steps.did(nc.vector.tensor_copy(aff[:, :], bank[:, 0, 0:NTE]))
            steps.settled()
            nc.vector.tensor_reduce(out=best[:, :], in_=te(aff), axis=AX.X, op=ALU.max).then_inc(s_best, 1)
            dve.wait_ge(s_best, 1)
            per_tile = [P, NTILE, NE]
            revb = rev[:, :].unsqueeze(1).broadcast_to(per_tile)
            steps.did(nc.vector.tensor_tensor(out=te(eq), in0=te(aff), in1=best[:, :].unsqueeze(2).broadcast_to(per_tile), op=ALU.is_equal))
            steps.settled()
            steps.did(nc.vector.tensor_tensor(out=te(eq), in0=te(eq), in1=revb, op=ALU.mult))
            steps.settled()
            steps.did(nc.vector.tensor_reduce(out=pick[:, :], in_=te(eq), axis=AX.X, op=ALU.max))
            steps.settled()
            steps.did(nc.vector.tensor_tensor(out=te(own), in0=revb, in1=pick[:, :].unsqueeze(2).broadcast_to(per_tile), op=ALU.is_equal))
            steps.settled()
            nc.vector.tensor_copy(ownb[:, :], own[:, :]).then_inc(s_own, 1)
            dve.wait_ge(s_cnt, 1)
            steps.did(nc.vector.tensor_copy(et(count), bank[:, 2, 0:NTE].rearrange("p (t e) -> p e t", e=NE)))
            steps.settled()
            steps.did(nc.vector.tensor_tensor_scan(out=cum[:, :], data0=not_first[:, :], data1=count[:, :], initial=0.0,
                                                   op0=ALU.mult, op1=ALU.add))
            steps.settled()
            per_expert = [P, NE, NTILE]
            total = et(cum)[:, :, NTILE - 1:NTILE].broadcast_to(per_expert)
            steps.did(nc.vector.tensor_tensor(out=et(over), in0=total, in1=firsts[:, :].unsqueeze(1).broadcast_to(per_expert), op=ALU.is_gt))
            steps.settled()
            steps.did(nc.vector.tensor_reduce(out=tiles[:, :], in_=et(over), axis=AX.X, op=ALU.add))
            steps.settled()
            steps.did(nc.vector.tensor_tensor_scan(out=ends[:, :], data0=not_first[:, 1:1 + NE], data1=tiles[:, :], initial=0.0,
                                                   op0=ALU.mult, op1=ALU.add))
            steps.settled()
            steps.did(nc.vector.tensor_tensor(out=base[:, :], in0=ends[:, :], in1=tiles[:, :], op=ALU.subtract))
            steps.settled()
            steps.did(nc.vector.tensor_scalar(base[:, :], base[:, :], float(TS), None, ALU.mult))
            steps.did(nc.vector.tensor_tensor(out=cum[:, :], in0=cum[:, :], in1=count[:, :], op=ALU.subtract))
            steps.settled()
            steps.did(nc.vector.tensor_tensor(out=te(pos), in0=bank[:, 1, 0:NTE].rearrange("p (t e) -> p t e", e=NE), in1=swapped(cum), op=ALU.add))
            steps.settled()
            steps.did(nc.vector.tensor_tensor(out=te(pos), in0=te(pos), in1=base[:, :].unsqueeze(1).broadcast_to(per_tile), op=ALU.add))
            steps.settled()
            steps.did(nc.vector.tensor_tensor(out=pos[:, :], in0=pos[:, :], in1=own[:, :], op=ALU.mult))
            steps.settled()
            steps.did(nc.vector.tensor_reduce(out=slot_f[:, :], in_=te(pos), axis=AX.X, op=ALU.add))
            steps.settled()
            nc.vector.tensor_copy(slot[:, :], slot_f[:, :]).then_inc(s_slot, 1)
            in_tile = [1, NSLOT, NE]
            pastv = past[:, :].rearrange("p (t e) -> p t e", e=NE)
            steps.did(nc.vector.tensor_tensor(out=pastv, in0=ends[0:1, :].unsqueeze(1).broadcast_to(in_tile),
                                              in1=numbers[0:1, :].unsqueeze(2).broadcast_to(in_tile), op=ALU.is_le))
            steps.settled()
            steps.did(nc.vector.tensor_reduce(out=eid_f[:, :], in_=pastv, axis=AX.X, op=ALU.add))
            steps.settled()
            steps.did(nc.vector.tensor_scalar(eid_f[:, :], eid_f[:, :], float(NE - 1), None, ALU.min))
            steps.settled()
            nc.vector.tensor_copy(eid[:, :], eid_f[:, :]).then_inc(s_eid, 1)
            steps.end()

            def gain_shift(j, turn, i):
                dve.wait_ge(s_sm[i], 16 * turn + 16)
                dve.wait_ge(s_t, j + 1)
                for c in range(DC):
                    ins = nc.vector.tensor_scalar(xsT[i][:, c, :], bank[:, 4 + i, c * TS:(c + 1) * TS], small[i][:, FC + c:FC + c + 1],
                                                  small[i][:, FC + DC + c:FC + DC + c + 1], ALU.mult, ALU.add)
                ins.then_inc(s_xg, 1)

            def tile(j, turn, i, following, second):
                for f in range(FC // 2, FC):
                    if f % 2 == 0:
                        dve.wait_ge(s_h, 4 * j + f // 2 + 1)
                    nc.vector.tensor_scalar(hid[i][:, f, :], hidden_bank(f), small[i][:, f:f + 1], 0.0, ALU.add, ALU.max).then_inc(s_rv, 1)
                if following:
                    gain_shift(j + 1, turn + i, 1 - i)
                dve.wait_ge(s_w2[i], 32 * turn + 32)
                dve.wait_ge(s_yd[i], 16 * turn + 16)
                dve.wait_ge(s_o, j + 1)
                for n in range(SUB):
                    ins = nc.vector.tensor_tensor(out=ys[i][:, n, :], in0=bank[:, 6 + i, n * D:(n + 1) * D], in1=b2[i][:, :], op=ALU.add)
                ins.then_inc(s_ys, 1)

            gain_shift(0, 0, 0)
            slot_tiles(dve, tile)

            dve.wait_ge(s_alpha, 1)
            dve.wait_ge(s_x2, 1)
            steps = Steps(dve, s_f, NGR * (3 * GRP + 1), 0)
            for gr in range(NGR):
                mine = range(GRP * gr, GRP * (gr + 1))
                dve.wait_ge(s_g[gr], 16 * GRP)
                for t in mine:
                    steps.did(nc.vector.scalar_tensor_tensor(out=xn[:, t, :], in0=xn[:, t, :], scalar=alpha[:, t:t + 1], in1=x[:, t, :],
                                                             op0=ALU.mult, op1=ALU.add))
                steps.settled()
                for t in mine:
                    steps.did(nc.vector.bn_stats(out=stats[:, t, :], in_=xn[:, t, :]))
                steps.settled()
                for t in mine:
                    steps.did(nc.vector.bn_aggr(out=mv[:, t, :], in_=stats[:, t, :]))
                steps.settled()
                part = slice(GRP * gr, GRP * (gr + 1))
                steps.did(nc.vector.tensor_scalar(sd[:, part], mv[:, part, 1], EPS, None, ALU.add))
                dve.wait_ge(s_fsd, gr + 1)
                nc.vector.reciprocal(rstd[:, part], sd[:, part]).then_inc(s_frs, 1)
                dve.wait_ge(s_frs, 2 * gr + 1)
                nc.vector.scalar_tensor_tensor(out=off[:, part], in0=mv[:, part, 0], scalar=-1.0, in1=rstd[:, part],
                                               op0=ALU.mult, op1=ALU.mult).then_inc(s_frs, 1)
                for t in mine[0:GRP // 2]:
                    nc.vector.tensor_scalar(xn[:, t, :], xn[:, t, :], mv[:, t, 0:1], rstd[:, t:t + 1], ALU.subtract, ALU.mult).then_inc(s_fy, 1)
            steps.end()

        @block.tensor
        def _(pe):
            pe.wait_ge(s_c, 16 * NC)
            def transpose_tokens(b):
                pe.wait_ge(s_x[b], 16)
                for k in range(4):
                    if b:
                        pe.wait_ge(s_xt, 4 * b - 3 + k)
                    for n in range(4):
                        t = TT * b + 4 * (k % 2) + n
                        ins = nc.tensor.transpose(bank[:, 4 + k, n * P:(n + 1) * P], x[:, t, (k // 2) * P:(k // 2 + 1) * P], ident[:, :])
                    ins.then_inc(s_xtr, 1)

            transpose_tokens(0)
            for b in range(NBATCH):
                if b + 1 < NBATCH:
                    transpose_tokens(b + 1)
                pe.wait_ge(s_xt, 4 * b + 4)
                for t in range(TT):
                    col = (TT * b + t) * NE
                    for kc in range(DC):
                        ins = nc.tensor.matmul(bank[:, 0, col:col + NE], xT[b % 2][:, kc, t * P:(t + 1) * P], cT[:, kc, :],
                                               start=(kc == 0), stop=(kc == DC - 1))
                ins.then_inc(s_aff, 1)
            pe.wait_ge(s_cb, 2)
            pe.wait_ge(s_own, 1)
            nc.tensor.matmul(bank[:, 1, 0:NTE], upper[:, :], ownb[:, :], start=True, stop=True)
            nc.tensor.matmul(bank[:, 2, 0:NTE], ones[:, :], ownb[:, :], start=True, stop=True).then_inc(s_cnt, 1)

            def transpose_slots(j, turn, i):
                pe.wait_ge(s_xs[i], 16 * turn + 16)
                for c in range(DC):
                    for n in range(SUB):
                        ins = nc.tensor.transpose(bank[:, 4 + i, c * TS + n * P:c * TS + (n + 1) * P], xs[i][:, n, c * P:(c + 1) * P], ident[:, :])
                ins.then_inc(s_t, 1)

            def tile(j, turn, i, following, second):
                pe.wait_ge(s_w1[i], 16 * turn + 16)
                pe.wait_ge(s_xg, j + 1)
                for f in range(FC):
                    for kc in range(DC):
                        ins = nc.tensor.matmul(hidden_bank(f), w1[i][:, kc, f * P:(f + 1) * P], xsT[i][:, kc, :],
                                               start=(kc == 0), stop=(kc == DC - 1))
                    if f % 2 == 1:
                        ins.then_inc(s_h, 1)
                if following:
                    transpose_slots(j + 1, turn + i, 1 - i)
                pe.wait_ge(s_w2[i], 32 * turn + 32)
                for n in range(SUB):
                    for f in range(FC):
                        if n == 0:
                            pe.wait_ge(s_ra if f < 4 else s_rv, (FC // 2) * j + f % 4 + 1)
                        ins = nc.tensor.matmul(bank[:, 6 + i, n * D:(n + 1) * D], hid[i][:, f, n * P:(n + 1) * P], w2[i][:, f, :],
                                               start=(f == 0), stop=(f == FC - 1))
                ins.then_inc(s_o, 1)

            pe.wait_ge(s_slot, 1)
            transpose_slots(0, 0, 0)
            slot_tiles(pe, tile)


def build_program(nc, I, out):
    def scratch(name, shape):
        return nc.dram_tensor(name, shape, F32).ap()

    qk_d = scratch("qk_parts", [NBATCH, 4, D, T])
    ln_d = scratch("line_parts", [NBATCH, 4, NH * NL, T])
    v_d = scratch("v_parts", [NBATCH, NG, P, TT * HG * 32])
    score_d = scratch("router_scores", [NBATCH, T])
    x1 = scratch("x1", [NBATCH, T, D])
    x2 = scratch("x2", [NBATCH, T, D])
    x3 = scratch("x3", [NBATCH, T, D])
    projections(nc, 0, I, I["x"], qk_d, ln_d, v_d)
    attention(nc, 0, I, I["x"], x1, qk_d, ln_d, v_d)
    mixture_of_depths(nc, I, x1, x2, score_d)
    projections(nc, 1, I, x2, qk_d, ln_d, v_d)
    attention(nc, 1, I, x2, x3, qk_d, ln_d, v_d)
    sorted_d = scratch("sorted_tokens", [NSLOT * TS, D]); result_d = scratch("slot_results", [NSLOT * TS, D])
    experts(nc, I, x3, out, sorted_d, result_d)


def lay_out(inputs):
    a = {k: np.asarray(v) for k, v in inputs.items()}

    def cont(x):
        return np.ascontiguousarray(x)

    def by_strips(w):
        out = np.zeros((NH, 32, D), np.float32)
        out[:, 0:DH, :] = w.reshape(NH, DH, D)
        return out.reshape(NH * 32, D)

    def by_features(v):
        return v.reshape(NE, -1, P).transpose(0, 2, 1)

    small = cont(np.concatenate([by_features(a["L1_ffn_b1"]), by_features(a["L1_ffn_ln_g"]), by_features(a["L1_ffn_ln_b"])], axis=2))
    swap = np.arange(D) ^ 1
    r = np.arange(P)
    inv = 1.0 / 10000.0 ** (np.arange(0, DH, 2, dtype=np.float32) / DH)
    ang = np.outer(np.arange(T, dtype=np.float32), inv)
    cos = np.cos(ang).astype(np.float32).T[(r % DH) // 2]
    sin = np.sin(ang).astype(np.float32).T[(r % DH) // 2]
    sin = np.where((r % 2 == 0)[:, None], -sin, sin)
    k, q = np.meshgrid(np.arange(P), np.arange(P), indexing="ij")
    big = np.float32(-3e38)
    return {
        "x": cont(a["L0_attn_x"]),
        "L0_wq": cont(a["L0_attn_wq"]), "L0_wqs": cont(a["L0_attn_wq"][:, swap]), "L0_wd": cont(a["L0_attn_w_down"]),
        "L0_wk": cont(a["L0_attn_wk_up"]), "L0_wks": cont(a["L0_attn_wk_up"][:, swap]), "L0_wv": cont(a["L0_attn_wv_up"]),
        "L0_wo": by_strips(a["L0_attn_wo"]),
        "L1_wqkv": cont(a["L1_attn_Wqkv"]), "L1_bqk": cont(a["L1_attn_bqkv"][0:2 * D].reshape(4, P).T), "L1_bv": cont(a["L1_attn_bqkv"][2 * D:]),
        "L1_w12": cont(np.concatenate([a["L1_attn_W1p"], a["L1_attn_W2p"]], axis=1)),
        "L1_pscale": cont(a["L1_attn_plucker_scale"]), "L1_wo": by_strips(a["L1_attn_Wout"]), "L1_bout": cont(a["L1_attn_bout"]),
        "m_wr": cont(a["L0_ffn_w_router"]), "m_w1": cont(a["L0_ffn_W1"]), "m_b1T": cont(a["L0_ffn_b1"].reshape(FC, P).T),
        "m_w2": cont(a["L0_ffn_W2"]), "m_b2": cont(a["L0_ffn_b2"]),
        "e_cT": cont(a["L1_ffn_centroids"].T), "e_small": small,
        "e_w1T": cont(a["L1_ffn_w1"].transpose(0, 2, 1)), 
        "e_w2T": cont(a["L1_ffn_w2"].transpose(0, 2, 1)), "e_b2": cont(a["L1_ffn_b2"]),
        "rope": np.stack([cos, sin]).astype(np.float32),
        "before": np.concatenate([np.ones((P, T - P), np.float32), (q < k).astype(np.float32)], axis=1),
        "upper": (k < q).astype(np.float32),
        "rev": np.tile(NE - np.arange(NE, dtype=np.float32), (P, 1)),
        "not_first": np.tile((np.arange(NTILE * NE) % NTILE != 0).astype(np.float32), (P, 1)),
        "firsts": np.tile(TS * np.arange(NTILE, dtype=np.float32), (P, 1)),
        "numbers": np.tile(np.arange(NSLOT, dtype=np.float32), (P, 1)),
        "ident": np.eye(P, dtype=np.float32),
        "sel": (np.arange(P)[:, None] == 32 * np.arange(HG)[None, :] + DH).astype(np.float32),
        "maskT0": np.where((k >= 64) & (q < 64), big, np.float32(0)).astype(np.float32),
        "maskT1": np.where(k > q, big, np.float32(0)).astype(np.float32),
        "jsign": np.tile(np.array([1, -1, 1, 1, -1, 1], np.float32), (P, 1)),
    }


def kernel(**inputs):
    import concourse.bacc as bacc
    from concourse.bass_utils import run_bass_kernel_spmd

    nc = bacc.Bacc("TRN2", target_bir_lowering=False, num_devices=1)
    arrays = lay_out(inputs)
    aps = {name: nc.dram_tensor(name, list(a.shape), mybir.dt.from_np(a.dtype), kind="ExternalInput").ap() for name, a in arrays.items()}
    out = nc.dram_tensor("out", [NBATCH, T, D], F32, kind="ExternalOutput").ap()
    build_program(nc, aps, out)
    r = run_bass_kernel_spmd(nc, [arrays], core_ids=[0])
    return r.results[0]["out"]
```
